# Optimizing a Trainium2 kernel written in Bass

```python
import numpy as np
import jax
import jax.numpy as jnp

def _softmax(x, axis=-1):
    return jax.nn.softmax(x, axis=axis)

def _gelu(x):
    return jax.nn.gelu(x, approximate=True)

def _silu(x):
    return jax.nn.silu(x)

def _sigmoid(x):
    return jax.nn.sigmoid(x)

def _layernorm(x, axis=-1, eps=1e-05):
    m = jnp.mean(x, axis=axis, keepdims=True)
    v = jnp.var(x, axis=axis, keepdims=True)
    return (x - m) / jnp.sqrt(v + eps)

def _scatter_add(tgt, idx, src, axis=0):
    return tgt.at[idx].add(src)

def _segment_sum(src, seg, n):
    return jax.ops.segment_sum(src, seg, n)
kernel_name = 'mk_prb_d2_jaxref_r8_2366e5'

def setup_inputs(seed: int=0):
    np.random.seed(seed)
    _w = jnp.asarray

    def _L0_attn_setup():
        import jax, jax.numpy as jnp
        import numpy as np
        LN_EPS = 1e-05

        def _ssm_scan(x_ssm, A, Bm, C, reverse):
            Bb, L, di = x_ssm.shape
            ds = Bm.shape[1]

            def step(h, x_t):
                h = jnp.clip(h * A[None] + x_t[:, :, None] * Bm[None], -10.0, 10.0)
                y = jnp.einsum('bid,id->bi', h, C)
                return (h, y)
            h0 = jnp.zeros((Bb, di, ds), x_ssm.dtype)
            _, ys = jax.lax.scan(step, h0, jnp.swapaxes(x_ssm, 0, 1), reverse=reverse)
            return jnp.swapaxes(ys, 0, 1)
        key = jax.random.key(seed)
        ks = jax.random.split(key, 6)
        B, L, D = (4, 256, 128)
        d_state, expand = (16, 2)
        d_inner = D * expand
        x = jax.random.normal(ks[0], (B, L, D), jnp.float32)
        in_proj_w = jax.random.normal(ks[1], (d_inner * 2, D), jnp.float32) * np.float32(1.0 / np.sqrt(D))
        A_log = jax.random.normal(ks[2], (d_inner, d_state), jnp.float32)
        B_mat = jax.random.normal(ks[3], (d_inner, d_state), jnp.float32) * np.float32(1.0 / np.sqrt(d_state))
        C_mat = jnp.full((d_inner, d_state), 0.01, jnp.float32)
        out_proj_w = jax.random.normal(ks[4], (D, d_inner), jnp.float32) * np.float32(1.0 / np.sqrt(d_inner))
        ln_w = jnp.ones((D,), jnp.float32)
        ln_b = jnp.zeros((D,), jnp.float32)
        return {'x': x, 'in_proj_w': in_proj_w, 'A_log': A_log, 'B_mat': B_mat, 'C_mat': C_mat, 'out_proj_w': out_proj_w, 'ln_w': ln_w, 'ln_b': ln_b}
    _L0_attn_in = _L0_attn_setup()

    def _L0_ffn_setup():
        import jax, jax.numpy as jnp
        import numpy as np
        H = 128
        I = 256
        E = 8
        B, S = (2, 128)

        def _swiglu(x, wg, wu, wd):
            return jax.nn.silu(x @ wg) * (x @ wu) @ wd
        key = jax.random.key(seed)
        ks = jax.random.split(key, 8)
        sc_h = 1.0 / np.sqrt(H)
        sc_i = 1.0 / np.sqrt(I)
        return {'hidden_states': jax.random.normal(ks[0], (B, S, H), jnp.float32), 'gate_w': jax.random.normal(ks[1], (H, E), jnp.float32) * sc_h, 'sh_gate': jax.random.normal(ks[2], (H, I), jnp.float32) * sc_h, 'sh_up': jax.random.normal(ks[3], (H, I), jnp.float32) * sc_h, 'sh_down': jax.random.normal(ks[4], (I, H), jnp.float32) * sc_i, 'rt_gate': jax.random.normal(ks[5], (E, H, I), jnp.float32) * sc_h, 'rt_up': jax.random.normal(ks[6], (E, H, I), jnp.float32) * sc_h, 'rt_down': jax.random.normal(ks[7], (E, I, H), jnp.float32) * sc_i}
    _L0_ffn_in = _L0_ffn_setup()

    def _L1_attn_setup():
        import jax, jax.numpy as jnp
        import numpy as np
        EMB = 128
        HEADS = 16
        HEAD_DIM = EMB // HEADS
        MAX_LEN = 125
        key = jax.random.key(seed)
        ks = jax.random.split(key, 11)
        s = 0.02
        x = jax.random.normal(ks[0], (4, 128, EMB), dtype=jnp.float32)
        Wq = jax.random.normal(ks[1], (EMB, EMB), dtype=jnp.float32) * s
        bq = jnp.zeros((EMB,), dtype=jnp.float32)
        Wk = jax.random.normal(ks[2], (EMB, EMB), dtype=jnp.float32) * s
        bk = jnp.zeros((EMB,), dtype=jnp.float32)
        Wv = jax.random.normal(ks[3], (EMB, EMB), dtype=jnp.float32) * s
        bv = jnp.zeros((EMB,), dtype=jnp.float32)
        Wp = jax.random.normal(ks[4], (EMB, EMB), dtype=jnp.float32) * s
        bp = jnp.zeros((EMB,), dtype=jnp.float32)
        bias_table = jax.random.normal(ks[5], (2 * MAX_LEN - 1, HEADS), dtype=jnp.float32) * 0.02
        temperature = jnp.ones((1,), dtype=jnp.float32)
        return {'x': x, 'Wq': Wq, 'bq': bq, 'Wk': Wk, 'bk': bk, 'Wv': Wv, 'bv': bv, 'Wp': Wp, 'bp': bp, 'bias_table': bias_table, 'temperature': temperature}
    _L1_attn_in = _L1_attn_setup()

    def _L1_ffn_setup():
        import jax, jax.numpy as jnp
        import numpy as np
        H = 128
        I = 88
        E = 64
        TOP_K = 8
        NG = 8
        TOPK_GROUP = 4
        N_SHARED = 2
        ROUTED_SCALE = 2.5
        S_I = I * N_SHARED

        def _route(x, gate_w, gate_bias):
            T = x.shape[0]
            logits = x @ gate_w.T
            scores = jax.nn.sigmoid(logits)
            scores_for_choice = scores + gate_bias[None, :]
            grp = scores_for_choice.reshape(T, NG, E // NG)
            group_scores = jnp.sum(jax.lax.top_k(grp, 2)[0], axis=-1)
            _, gidx = jax.lax.top_k(group_scores, TOPK_GROUP)
            gmask = jnp.zeros((T, NG), dtype=scores.dtype).at[jnp.arange(T)[:, None], gidx].set(1.0)
            emask = jnp.repeat(gmask, E // NG, axis=1)
            masked = jnp.where(emask > 0, scores_for_choice, 0.0)
            _, topk_idx = jax.lax.top_k(masked, TOP_K)
            topk_w = jnp.take_along_axis(scores, topk_idx, axis=1)
            topk_w = topk_w / (jnp.sum(topk_w, axis=-1, keepdims=True) + 1e-20)
            topk_w = topk_w * ROUTED_SCALE
            rw = jnp.zeros((T, E), dtype=scores.dtype).at[jnp.arange(T)[:, None], topk_idx].add(topk_w)
            return rw

        def _mlp(x, gw, uw, dw):
            return jax.nn.silu(x @ gw.T) * (x @ uw.T) @ dw.T
        key = jax.random.key(seed)
        ks = jax.random.split(key, 10)
        sc = 0.02
        return {'hidden_states': jax.random.normal(ks[0], (1, 128, H), dtype=jnp.float32), 'gate_w': sc * jax.random.normal(ks[1], (E, H), dtype=jnp.float32), 'gate_bias': sc * jax.random.normal(ks[2], (E,), dtype=jnp.float32), 'Wg': sc * jax.random.normal(ks[3], (E, I, H), dtype=jnp.float32), 'Wu': sc * jax.random.normal(ks[4], (E, I, H), dtype=jnp.float32), 'Wd': sc * jax.random.normal(ks[5], (E, H, I), dtype=jnp.float32), 'Sg': sc * jax.random.normal(ks[6], (S_I, H), dtype=jnp.float32), 'Su': sc * jax.random.normal(ks[7], (S_I, H), dtype=jnp.float32), 'Sd': sc * jax.random.normal(ks[8], (H, S_I), dtype=jnp.float32)}
    _L1_ffn_in = _L1_ffn_setup()
    _d = {'L0_attn_x': _L0_attn_in['x'], 'L0_attn_in_proj_w': _L0_attn_in['in_proj_w'], 'L0_attn_A_log': _L0_attn_in['A_log'], 'L0_attn_B_mat': _L0_attn_in['B_mat'], 'L0_attn_C_mat': _L0_attn_in['C_mat'], 'L0_attn_out_proj_w': _L0_attn_in['out_proj_w'], 'L0_attn_ln_w': _L0_attn_in['ln_w'], 'L0_attn_ln_b': _L0_attn_in['ln_b'], 'L0_ffn_gate_w': _L0_ffn_in['gate_w'], 'L0_ffn_sh_gate': _L0_ffn_in['sh_gate'], 'L0_ffn_sh_up': _L0_ffn_in['sh_up'], 'L0_ffn_sh_down': _L0_ffn_in['sh_down'], 'L0_ffn_rt_gate': _L0_ffn_in['rt_gate'], 'L0_ffn_rt_up': _L0_ffn_in['rt_up'], 'L0_ffn_rt_down': _L0_ffn_in['rt_down'], 'L1_attn_Wq': _L1_attn_in['Wq'], 'L1_attn_bq': _L1_attn_in['bq'], 'L1_attn_Wk': _L1_attn_in['Wk'], 'L1_attn_bk': _L1_attn_in['bk'], 'L1_attn_Wv': _L1_attn_in['Wv'], 'L1_attn_bv': _L1_attn_in['bv'], 'L1_attn_Wp': _L1_attn_in['Wp'], 'L1_attn_bp': _L1_attn_in['bp'], 'L1_attn_bias_table': _L1_attn_in['bias_table'], 'L1_attn_temperature': _L1_attn_in['temperature'], 'L1_ffn_gate_w': _L1_ffn_in['gate_w'], 'L1_ffn_gate_bias': _L1_ffn_in['gate_bias'], 'L1_ffn_Wg': _L1_ffn_in['Wg'], 'L1_ffn_Wu': _L1_ffn_in['Wu'], 'L1_ffn_Wd': _L1_ffn_in['Wd'], 'L1_ffn_Sg': _L1_ffn_in['Sg'], 'L1_ffn_Su': _L1_ffn_in['Su'], 'L1_ffn_Sd': _L1_ffn_in['Sd']}
    _x0 = _d['L0_attn_x']
    _d['L0_attn_x'] = jax.random.normal(jax.random.fold_in(jax.random.key(seed), 1), (2, 1024, 128), dtype=_x0.dtype)
    del _x0
    return _d

def reference(L0_attn_x, L0_attn_in_proj_w, L0_attn_A_log, L0_attn_B_mat, L0_attn_C_mat, L0_attn_out_proj_w, L0_attn_ln_w, L0_attn_ln_b, L0_ffn_gate_w, L0_ffn_sh_gate, L0_ffn_sh_up, L0_ffn_sh_down, L0_ffn_rt_gate, L0_ffn_rt_up, L0_ffn_rt_down, L1_attn_Wq, L1_attn_bq, L1_attn_Wk, L1_attn_bk, L1_attn_Wv, L1_attn_bv, L1_attn_Wp, L1_attn_bp, L1_attn_bias_table, L1_attn_temperature, L1_ffn_gate_w, L1_ffn_gate_bias, L1_ffn_Wg, L1_ffn_Wu, L1_ffn_Wd, L1_ffn_Sg, L1_ffn_Su, L1_ffn_Sd):

    def _L0_attn_ref(x, in_proj_w, A_log, B_mat, C_mat, out_proj_w, ln_w, ln_b):
        import jax, jax.numpy as jnp
        import numpy as np
        LN_EPS = 1e-05

        def _ssm_scan(x_ssm, A, Bm, C, reverse):
            Bb, L, di = x_ssm.shape
            ds = Bm.shape[1]

            def step(h, x_t):
                h = jnp.clip(h * A[None] + x_t[:, :, None] * Bm[None], -10.0, 10.0)
                y = jnp.einsum('bid,id->bi', h, C)
                return (h, y)
            h0 = jnp.zeros((Bb, di, ds), x_ssm.dtype)
            _, ys = jax.lax.scan(step, h0, jnp.swapaxes(x_ssm, 0, 1), reverse=reverse)
            return jnp.swapaxes(ys, 0, 1)
        mu = jnp.mean(x, axis=-1, keepdims=True)
        var = jnp.mean((x - mu) ** 2, axis=-1, keepdims=True)
        xn = (x - mu) * jax.lax.rsqrt(var + LN_EPS) * ln_w + ln_b
        x_proj = jnp.einsum('bld,ed->ble', xn, in_proj_w)
        x_ssm, gate = jnp.split(x_proj, 2, axis=-1)
        A = -jnp.clip(jnp.exp(A_log), -10.0, -0.01)
        out_f = _ssm_scan(x_ssm, A, B_mat, C_mat, reverse=False)
        out_b = _ssm_scan(x_ssm, A, B_mat, C_mat, reverse=True)
        out = (out_f + out_b) * 0.5 * jax.nn.silu(gate)
        return jnp.einsum('bli,di->bld', out, out_proj_w)

    def _L0_ffn_ref(hidden_states, gate_w, sh_gate, sh_up, sh_down, rt_gate, rt_up, rt_down):
        import jax, jax.numpy as jnp
        import numpy as np
        H = 128
        I = 256
        E = 8
        B, S = (2, 128)

        def _swiglu(x, wg, wu, wd):
            return jax.nn.silu(x @ wg) * (x @ wu) @ wd
        b, s, h = hidden_states.shape
        x = hidden_states.reshape(-1, h)
        logits = x @ gate_w
        top_val = jnp.max(logits, axis=-1, keepdims=True)
        top_id = jnp.argmax(logits, axis=-1)
        score = jax.nn.sigmoid(top_val)
        xs = x * score
        g = jnp.einsum('th,ehi->eti', xs, rt_gate)
        u = jnp.einsum('th,ehi->eti', xs, rt_up)
        act = jax.nn.silu(g) * u
        y = jnp.einsum('eti,eih->eth', act, rt_down)
        onehot = jax.nn.one_hot(top_id, E, dtype=x.dtype)
        routed = jnp.einsum('eth,te->th', y, onehot)
        shared = _swiglu(x, sh_gate, sh_up, sh_down)
        return (shared + routed).reshape(b, s, h)

    def _L1_attn_ref(x, Wq, bq, Wk, bk, Wv, bv, Wp, bp, bias_table, temperature):
        import jax, jax.numpy as jnp
        import numpy as np
        EMB = 128
        HEADS = 16
        HEAD_DIM = EMB // HEADS
        MAX_LEN = 125
        B, N, C = x.shape
        H, D = (HEADS, C // HEADS)

        def split_heads(t):
            return t.reshape(B, N, H, D).transpose(0, 2, 1, 3)
        q = split_heads(x @ Wq + bq)
        k = split_heads(x @ Wk + bk)
        v = split_heads(x @ Wv + bv)
        energy = jnp.einsum('bhqd,bhkd->bhqk', q, k)
        pos = jnp.arange(N)
        rel = pos[:, None] - pos[None, :] + (N - 1)
        rel = jnp.clip(rel, 0, bias_table.shape[0] - 1)
        bias = bias_table[rel].transpose(2, 0, 1)
        energy = energy + bias[None]
        scaling = jnp.sqrt(jnp.float32(C))
        temp = jnp.clip(temperature[0], 0.1, 10.0)
        att = jax.nn.softmax(energy / (scaling * temp), axis=-1)
        out = jnp.einsum('bhqk,bhkd->bhqd', att, v)
        out = out.transpose(0, 2, 1, 3).reshape(B, N, C)
        return out @ Wp + bp

    def _L1_ffn_ref(hidden_states, gate_w, gate_bias, Wg, Wu, Wd, Sg, Su, Sd):
        import jax, jax.numpy as jnp
        import numpy as np
        H = 128
        I = 88
        E = 64
        TOP_K = 8
        NG = 8
        TOPK_GROUP = 4
        N_SHARED = 2
        ROUTED_SCALE = 2.5
        S_I = I * N_SHARED

        def _route(x, gate_w, gate_bias):
            T = x.shape[0]
            logits = x @ gate_w.T
            scores = jax.nn.sigmoid(logits)
            scores_for_choice = scores + gate_bias[None, :]
            grp = scores_for_choice.reshape(T, NG, E // NG)
            group_scores = jnp.sum(jax.lax.top_k(grp, 2)[0], axis=-1)
            _, gidx = jax.lax.top_k(group_scores, TOPK_GROUP)
            gmask = jnp.zeros((T, NG), dtype=scores.dtype).at[jnp.arange(T)[:, None], gidx].set(1.0)
            emask = jnp.repeat(gmask, E // NG, axis=1)
            masked = jnp.where(emask > 0, scores_for_choice, 0.0)
            _, topk_idx = jax.lax.top_k(masked, TOP_K)
            topk_w = jnp.take_along_axis(scores, topk_idx, axis=1)
            topk_w = topk_w / (jnp.sum(topk_w, axis=-1, keepdims=True) + 1e-20)
            topk_w = topk_w * ROUTED_SCALE
            rw = jnp.zeros((T, E), dtype=scores.dtype).at[jnp.arange(T)[:, None], topk_idx].add(topk_w)
            return rw

        def _mlp(x, gw, uw, dw):
            return jax.nn.silu(x @ gw.T) * (x @ uw.T) @ dw.T
        B, S, _ = hidden_states.shape
        x = hidden_states.reshape(B * S, H)
        rw = _route(x, gate_w, gate_bias)
        expert_out = jax.vmap(lambda gw_, uw_, dw_: _mlp(x, gw_, uw_, dw_))(Wg, Wu, Wd)
        routed = jnp.einsum('eth,te->th', expert_out, rw)
        shared = _mlp(x, Sg, Su, Sd)
        out = (routed + shared).reshape(B, S, H)
        return out
    x = L0_attn_x
    xn = _layernorm(x, axis=-1)
    x = x + _L0_attn_ref(xn, L0_attn_in_proj_w, L0_attn_A_log, L0_attn_B_mat, L0_attn_C_mat, L0_attn_out_proj_w, L0_attn_ln_w, L0_attn_ln_b) + _L0_ffn_ref(xn, L0_ffn_gate_w, L0_ffn_sh_gate, L0_ffn_sh_up, L0_ffn_sh_down, L0_ffn_rt_gate, L0_ffn_rt_up, L0_ffn_rt_down)
    xn = _layernorm(x, axis=-1)
    x = x + _L1_attn_ref(xn, L1_attn_Wq, L1_attn_bq, L1_attn_Wk, L1_attn_bk, L1_attn_Wv, L1_attn_bv, L1_attn_Wp, L1_attn_bp, L1_attn_bias_table, L1_attn_temperature) + _L1_ffn_ref(xn, L1_ffn_gate_w, L1_ffn_gate_bias, L1_ffn_Wg, L1_ffn_Wu, L1_ffn_Wd, L1_ffn_Sg, L1_ffn_Su, L1_ffn_Sd)
    return x

_drawn_inputs = setup_inputs


def setup_inputs(seed=0):
    import zlib

    import numpy as np

    out = dict(_drawn_inputs(seed))
    spreads = {'L0_attn_C_mat': (0.009999999776482582, 0.6),
     'L0_attn_ln_w': (1.0, 0.6),
     'L0_attn_ln_b': (0.0, 0.8),
     'L1_attn_bq': (0.0, 2.0),
     'L1_attn_bk': (0.0, 2.0),
     'L1_attn_bv': (0.0, 2.0),
     'L1_attn_bp': (0.0, 0.8)}
    factors = {'L0_attn_in_proj_w': 8.0,
     'L0_attn_B_mat': 8.0,
     'L0_attn_out_proj_w': 8.0,
     'L1_attn_Wq': 64.0,
     'L1_attn_Wk': 64.0,
     'L1_attn_Wv': 39.389,
     'L1_attn_Wp': 11.961,
     'L1_attn_bias_table': 64.0,
     'L1_ffn_gate_w': 8.0,
     'L1_ffn_gate_bias': 8.0,
     'L1_ffn_Wg': 8.0,
     'L1_ffn_Wu': 8.0,
     'L1_ffn_Wd': 8.0,
     'L1_ffn_Sg': 8.0,
     'L1_ffn_Su': 8.0,
     'L1_ffn_Sd': 8.0,
     'L0_ffn_gate_w': 4.572,
     'L0_ffn_sh_gate': 3.235,
     'L0_ffn_sh_up': 3.063,
     'L0_ffn_sh_down': 3.052,
     'L0_ffn_rt_gate': 4.583,
     'L0_ffn_rt_up': 4.337,
     'L0_ffn_rt_down': 4.347}
    for name, (base, spread) in spreads.items():
        noise = np.random.default_rng([zlib.crc32(name.encode()), seed]).standard_normal(out[name].shape)
        drawn = base * np.exp(spread * noise) if base else spread * noise
        out[name] = jnp.asarray(drawn.astype(out[name].dtype))
    for name, factor in factors.items():
        out[name] = (out[name] * factor).astype(out[name].dtype)
    return out
```

```python
import concourse.bass as bass
from concourse import mybir
from contextlib import ExitStack
import numpy as np

F32 = mybir.dt.float32
BF16 = mybir.dt.bfloat16
U32 = mybir.dt.uint32
ALU = mybir.AluOpType
ACT = mybir.ActivationFunctionType
X = mybir.AxisListType.X

P = 128
BATCH, LEN, DIM = 2, 1024, 128
TOK = BATCH * LEN
TILES = TOK // P
EPS = 1e-5

HALVES, STATES = 2, 16
SEG = 128
SEGS = TOK // SEG
WARM = 24
WIN = 8
WINDOWS = (SEG + WARM) // WIN
WARM_WINDOWS = WARM // WIN
CH = HALVES * STATES
COL = CH * SEGS
PADSEG = SEG + 2 * WARM
H_MAX = 10.0

E0, I0 = 8, 256
CHUNK = 512
CHUNKS = TOK // CHUNK
CT = CHUNK // P

HEADS, HD = 16, 8
QT = LEN // P
UNITS = HEADS * BATCH
PARTS_Q = (0, 0, 1, 1, 0, 2)
PARTS_K = (0, 1, 0, 1, 2, 0)
KROWS = 65
MAXROW = 8 * len(PARTS_Q)
BIASED = 248
CORNER = 2 * P

E1, I1, TOPK, GROUPS, TOPG = 64, 88, 8, 8, 4
MT = TOK * TOPK // P + E1
SLOTS = MT + 8
KEY = 32768.0


def build(nc, A):
    ctx = ExitStack()
    with ctx:
        def sb(name, shape, dt=F32):
            return ctx.enter_context(nc.sbuf_tensor(name, shape, dt))

        def sem(name):
            return ctx.enter_context(nc.semaphore(name))

        ident = sb("ident", [P, P])
        iota8 = sb("iota8", [P, 8])
        lnwb = sb("lnwb", [P, 2])
        w_gate0 = sb("w_gate0", [P, E0])
        resid = sb("resid", [P, TILES, DIM])
        xnT = sb("xnT", [P, TOK])
        xsT = sb("xsT", [P, TOK])
        arena = sb("arena", [P, 34304])
        cursor = [0]

        def carve(n):
            cursor[0] += n
            assert cursor[0] <= 34304
            return arena[:, cursor[0] - n:cursor[0]]

        scan_flat = [carve(WIN * COL) for _ in range(4)]
        scan_f = [s.rearrange("p (m c) -> p m c", m=WIN) for s in scan_flat[:2]]
        scan_b = [s.rearrange("p (m c) -> p m c", m=WIN) for s in scan_flat[2:]]
        diagC = carve(CH * P).rearrange("p (c n) -> p c n", c=CH)
        xssm = carve(HALVES * SEGS * PADSEG).rearrange("p (h s m) -> p h s m", h=HALVES, s=SEGS)
        sgate = carve(HALVES * TOK).rearrange("p (h t) -> p h t", h=HALVES)
        y_flat = carve(HALVES * TOK)
        y = y_flat.rearrange("p (h t) -> p h t", h=HALVES)
        xn = y_flat[:, 0:TOK].rearrange("p (t d) -> p t d", t=TILES)
        xaT = y_flat[:, TOK:2 * TOK]
        xa = scan_flat[0][:, 0:TOK].rearrange("p (t d) -> p t d", t=TILES)
        sq = scan_flat[1][:, 0:TOK].rearrange("p (t d) -> p t d", t=TILES)
        xs = scan_flat[0][:, TOK:2 * TOK].rearrange("p (t d) -> p t d", t=TILES)
        w_in = scan_flat[2][:, 0:2 * HALVES * P]
        zeros = sb("zeros", [P, COL])
        ABC = sb("ABC", [P, 3, CH])
        decay = sb("decay", [P, 1])
        w_gu = sb("w_gu", [P, 2 * I0])
        w_dn = sb("w_dn", [P, 2, DIM])
        w_out = sb("w_out", [P, 2, DIM])
        silu_g = sb("silu_g", [P, 2, CHUNK])
        up = sb("up", [P, 2, CHUNK])
        act = sb("act", [P, 2, CHUNK])
        stat = sb("stat", [P, 4, TILES])
        logit = sb("logit", [P, TILES, E0])
        top = sb("top", [P, TILES, 8])
        topi = sb("topi", [P, TILES, 8], U32)
        topf = sb("topf", [P, TILES, 1])
        score = sb("score", [P, TILES])
        onehot = sb("onehot", [P, TILES, E0])

        U32W = LEN // 2
        Qs = arena[:, 0:(UNITS + 1) * U32W].bitcast(BF16)
        Ks = arena[:, (UNITS + 1) * U32W:(2 * UNITS + 2) * U32W].bitcast(BF16)
        cursor[0] = 0
        w_q, w_k, w_v, bv_t, strict, ones, bp_t = (carve(P) for _ in range(7))
        w_gate1, gbias = carve(E1), carve(E1)
        w_sh = carve(4 * I1)
        w_shd = carve(2 * DIM).rearrange("p (k d) -> p k d", k=2)
        TE = TILES * E1

        def table():
            return carve(TE).rearrange("p (t e) -> p t e", t=TILES)

        sc1, sfc, masked, repl, M, rw, carry, slot, key = (table() for _ in range(9))
        net = [carve(TE // 2) for _ in range(3)]
        cmp8 = carve(8 * E1).rearrange("p (k e) -> p k e", k=8)
        cmp8b = carve(8 * E1).rearrange("p (k e) -> p k e", k=8)
        ones64 = carve(E1)
        nt, endt, base1 = carve(E1), carve(E1), carve(E1)
        qf, kf = carve(TOK), carve(TOK)
        parts = [carve(TOK // 2).bitcast(BF16) for _ in range(6)]
        sq1 = carve(TOK).rearrange("p (t d) -> p t d", t=TILES)
        xn1 = xsT[:, :].rearrange("p (t d) -> p t d", t=TILES)
        xn1T = xnT
        att = xnT[:, :].rearrange("p (t d) -> p t d", t=TILES)
        attT = xsT
        w_p = sb("w_p", [P, P])
        small = sb("small", [P, 32])
        bq, bk, temp, jcol, blast = small[:, 0:1], small[:, 1:2], small[:, 2:3], small[:, 3:5], small[:, 5:21]
        inv, bqi, zero = small[:, 21:22], small[:, 22:23], small[:, 23:24]
        gs, gtop, gidx, gidxf = logit, top, topi, onehot
        gmask = carve(TILES * 8).rearrange("p (t g) -> p t g", t=TILES)
        etop = sb("etop", [P, TILES, 8])
        den1 = sb("den1", [P, TILES])
        slots = sb("slots", [P, TILES, TOPK], U32)
        w8 = sb("w8", [P, TILES, TOPK])
        ntu = sb("ntu", [P, E1], U32)
        exp_of = sb("exp_of", [P, 2])
        etab = sb("etab", [1, 2 * P], U32)
        V = sb("V", [P, TILES, HEADS, HD + 1])
        nm = sb("nm", [P, UNITS, QT])
        nmT = [sb(f"nmT{k}", [P, 2, P], BF16) for k in range(3)]
        nmr = xnT[:, 0:2 * P].rearrange("p (c n) -> p c n", c=2)
        rec = sb("rec", [P, 1, QT])
        sums = zeros[:, 4 * I1:4 * I1 + QT * (HD + 1)].rearrange("p (q d) -> p q d", q=QT)
        corner_f = sb("corner_f", [P, 2, 2 * CORNER + 1])
        corner_p = sb("corner_p", [P, 2, 3, 2 * CORNER], BF16)
        identb = sb("identb", [P, P], BF16)
        Pt = [silu_g, up]
        m_x, m_y = (act[:, k, :].rearrange("p (b d) -> p b d", b=4) for k in range(2))
        m_gu = sb("m_gu", [P, 4, 2 * I1])
        m_dn = w_gu[:, :].rearrange("p (b d) -> p b d", b=4)
        m_xT, m_aT = w_dn, w_out
        m_th, m_a = (zeros[:, k * 2 * I1:(k + 1) * 2 * I1].rearrange("p (b n) -> p b n", b=2) for k in range(2))
        m_b = arena[:, (2 * UNITS + 2) * U32W:(2 * UNITS + 2) * U32W + 2 * I1].rearrange("p (b n) -> p b n", b=2)
        ybuf = arena[:, 0:2 * TOPK * DIM].rearrange("p (b k d) -> p b k d", b=2, k=TOPK)
        d_parts = nc.dram_tensor("d_parts", (6, P, TOK), BF16).ap()
        d_nm = nc.dram_tensor("d_nm", (3, 2, P, P), BF16).ap()
        d_xs = nc.dram_tensor("d_xs", (SLOTS * P, DIM), F32).ap()
        d_ys = nc.dram_tensor("d_ys", (MT * P, DIM), F32).ap()

        psum = ctx.enter_context(nc.psum_tensor("psum", [P, 8 * 512], F32))
        bank = [psum[:, i * 512:(i + 1) * 512] for i in range(8)]

        s_x = sem("s_x"); s_const = sem("s_const"); s_w = sem("s_w")
        ln_step = sem("ln_step")
        var_ready = sem("var_ready"); std_ready = sem("std_ready")
        xn_ready = sem("xn_ready"); xnT_psum = sem("xnT_psum"); xnT_ready = sem("xnT_ready")
        xa_ready = sem("xa_ready"); xaT_psum = sem("xaT_psum"); xaT_ready = sem("xaT_ready")
        xs_ready = sem("xs_ready"); xsT_psum = sem("xsT_psum"); xsT_ready = sem("xsT_ready")
        logit_psum = sem("logit_psum"); logit_ready = sem("logit_ready")
        score_ready = sem("score_ready"); onehot_ready = sem("onehot_ready")
        proj_psum = sem("proj_psum"); proj_evac = sem("proj_evac")
        a_exp = sem("a_exp"); scan_consts = sem("scan_consts")
        pads = sem("pads"); halo = sem("halo"); zeros_ready = sem("zeros_ready")
        uf_ready = sem("uf_ready"); ub_ready = sem("ub_ready")
        f_step = sem("f_step"); b_step = sem("b_step")
        window_read = sem("window_read")
        y_added = sem("y_added")
        gu_psum = sem("gu_psum"); gu_evac = sem("gu_evac"); act_ready = sem("act_ready")
        dn_psum = sem("dn_psum"); dn_added = sem("dn_added")
        wgu_in = sem("wgu_in"); wdn_in = sem("wdn_in")
        o_ready = sem("o_ready"); out_psum = sem("out_psum"); x1_ready = sem("x1_ready")
        s_out = sem("s_out")
        logit_max = sem("logit_max")
        corner_idb = sem("corner_idb"); v_ones = sem("v_ones")
        l1_w = sem("l1_w"); l1_p = sem("l1_p"); xs_zero = sem("xs_zero")
        xn1_ready = sem("xn1_ready"); xn1T_psum = sem("xn1T_psum"); xn1T_ready = sem("xn1T_ready")
        lg1_psum = sem("lg1_psum"); sc1_ready = sem("sc1_ready"); inv_ready = sem("inv_ready")
        qk_psum = sem("qk_psum"); qk_ready = sem("qk_ready"); v_psum = sem("v_psum"); v_ready = sem("v_ready")
        part_ready = sem("part_ready"); rest_step = sem("rest_step"); parts_out = sem("parts_out"); stacked = sem("stacked")
        mask_ready = sem("mask_ready"); rank_psum = sem("rank_psum"); slots_ready = sem("slots_ready")
        exp_ready = sem("exp_ready"); etab_psum = sem("etab_psum"); etab_ready = sem("etab_ready"); w8_ready = sem("w8_ready")
        scattered = sem("scattered"); bp_added = sem("bp_added")
        sgu_psum = sem("sgu_psum"); sgu_evac = sem("sgu_evac"); sact_ready = sem("sact_ready")
        sdn_psum = sem("sdn_psum"); sdn_added = sem("sdn_added")
        corner_in = [sem(f"corner_in{k}") for k in range(2)]; corner_step = sem("corner_step"); corner_used = sem("corner_used")
        sq_psum = sem("sq_psum"); max_ready = sem("max_ready"); nmT_psum = sem("nmT_psum"); nmT_ready = sem("nmT_ready")
        nm_out = sem("nm_out"); nm_in = sem("nm_in")
        st_psum = sem("st_psum"); p_ready = sem("p_ready"); p_free = sem("p_free"); pair_free = sem("pair_free"); att_free = sem("att_free"); mx_used = sem("mx_used"); att_psum = sem("att_psum"); att_ready = sem("att_ready")
        rec_ready = sem("rec_ready")
        mx_in, mgu_in, mdn_in = ([sem(f"{n}_in{k}") for k in range(4)] for n in ("mx", "mgu", "mdn")); mxT_psum = sem("mxT_psum"); mxT_ready = sem("mxT_ready"); mgu_psum = sem("mgu_psum"); mth_ready = sem("mth_ready")
        ma_step = sem("ma_step"); ma_ready = sem("ma_ready"); maT_psum = sem("maT_psum"); maT_ready = sem("maT_ready")
        my_psum = sem("my_psum"); my_ready = sem("my_ready"); my_out = [sem(f"my_out{k}") for k in range(4)]
        y_in = [sem(f"y_in{k}") for k in range(2)]; y_used = sem("y_used"); attT_psum = sem("attT_psum"); attT_ready = sem("attT_ready")
        fin_psum = sem("fin_psum"); fin_ready = sem("fin_ready"); routed_added = sem("routed_added")

        block = ctx.enter_context(nc.Block())
        U = STATES * 2
        TB = 4

        @block.sync
        def _(sp):
            for k in range(4):
                sp.dma_start(resid[:, 4 * k:4 * k + 4, :], A["x"][4 * k * P:4 * (k + 1) * P].rearrange("(t p) d -> p t d", p=P)).then_inc(s_x, 16)
            for dst, name in ((ident, "ident"), (iota8, "iota8"), (lnwb, "lnwb"), (w_gate0, "w_gate0")):
                sp.dma_start(dst[:, :], A[name]).then_inc(s_const, 16)
            sp.dma_start(ABC[:, :, :], A["abc"]).then_inc(s_const, 16)
            sp.dma_start(small[:, 0:21], A["small"]).then_inc(s_const, 16)
            sp.dma_start(w_in, A["w_in"]).then_inc(s_w, 16)
            sp.dma_start(w_out[:, :, :], A["w_out"]).then_inc(s_w, 16)
            sp.dma_start(w_gu[:, :], A["w_gu0"][0]).then_inc(wgu_in, 16)
            sp.dma_start(w_dn[:, :, :], A["w_dn0"][0]).then_inc(wdn_in, 16)
            sp.wait_ge(zeros_ready, 1)
            with sp.Fori(0, SLOTS // 4) as z:
                sp.dma_start(d_xs[bass.ds(z * 4 * P, 4 * P)].rearrange("(p r) d -> p (r d)", p=P), zeros[:, :]).then_inc(xs_zero, 16)
            with sp.Fori(0, E0) as e:
                sp.wait_ge(gu_psum, 2 * CHUNKS * (e + 1))
                sp.dma_start(w_gu[:, :], A["w_gu0"][bass.ds(e + 1, 1)].rearrange("a p n -> p (a n)")).then_inc(wgu_in, 16)
                sp.wait_ge(dn_psum, CHUNKS * (e + 1))
                sp.dma_start(w_dn[:, :, :], A["w_dn0"][bass.ds(e + 1, 1)].rearrange("a p k n -> p (a k) n")).then_inc(wdn_in, 16)
            sp.wait_ge(window_read, 2 * E0 + 1)
            sp.wait_ge(uf_ready, 2 * (WINDOWS + 1))
            sp.wait_ge(ub_ready, 2 * (WINDOWS + 1))
            for dst, name in ((w_q, "w_q"), (w_k, "w_k"), (w_v, "w_v"), (bv_t, "bv_t"), (strict, "strict"), (ones, "ones"),
                              (w_gate1, "w_gate1"), (gbias, "gbias"), (w_sh, "w_sh")):
                sp.dma_start(dst, A[name]).then_inc(l1_w, 16)
            sp.dma_start(w_shd[0:I1, :, :], A["w_shd"]).then_inc(l1_w, 16)
            sp.dma_start(w_p[:, :], A["w_p"]).then_inc(l1_p, 16)
            sp.dma_start(bp_t, A["bp_t"]).then_inc(l1_p, 16)
            for k, (done, count) in {0: (part_ready, 1), 3: (part_ready, 2), 1: (part_ready, 3), 4: (part_ready, 4),
                                     2: (rest_step, 3), 5: (rest_step, 4)}.items():
                sp.wait_ge(done, count)
                sp.dma_start(d_parts[k], parts[k]).then_inc(parts_out, 16)
            sp.wait_ge(parts_out, 96)
            sp.wait_ge(w8_ready, 1)
            sp.wait_ge(sdn_psum, CHUNKS)
            sp.wait_ge(v_psum, 4)
            for side, (stack, groups) in enumerate(((Qs, PARTS_Q), (Ks, PARTS_K))):
                for g, part in enumerate(groups):
                    sp.dma_start(stack[8 * g:8 * g + 8, 0:UNITS * LEN].rearrange("d (h n) -> d h n", h=HEADS),
                                 d_parts[3 * side + part].rearrange("(h d) n -> d h n", d=HD)).then_inc(stacked, 16)
            sp.dma_start(Qs[MAXROW:64, 0:UNITS * LEN], A["fill_q"][0:16]).then_inc(stacked, 16)
            sp.dma_start(Qs[64:65, 0:UNITS * LEN], A["fill_q"][15:16]).then_inc(stacked, 16)
            for stack in (Qs, Ks):
                sp.dma_start(stack[0:KROWS, UNITS * LEN:], A["fill_unit"]).then_inc(stacked, 16)
            sp.dma_start(Ks[MAXROW:64, 0:UNITS * LEN], A["fill_k"][0:16]).then_inc(stacked, 16)
            sp.dma_start(Ks[64:65, 0:UNITS * LEN], A["fill_k"][15:16]).then_inc(stacked, 16)

            def load_corner(n, buf):
                sp.dma_start(corner_f[:, buf, :], A["corners"][bass.ds(n, 1)].rearrange("a p n -> p (a n)")).then_inc(corner_in[buf], 16)

            for k in range(2):
                load_corner(k, k)
            with sp.Fori(0, HEADS // 2) as hp:
                for k in range(2):
                    sp.wait_ge(corner_step, 6 * (2 * hp + k + 1))
                    load_corner(2 * hp + k + 2, k)
            for k in range(3):
                sp.wait_ge(nmT_ready, k + 1)
                sp.dma_start(d_nm[k].rearrange("c p n -> p c n"), nmT[k][:, :, :]).then_inc(nm_out, 16)
            sp.wait_ge(nm_out, 48)
            sp.dma_start(Qs[MAXROW:MAXROW + 3, 0:UNITS * LEN], d_nm.rearrange("k c p n -> k (c p n)")).then_inc(nm_in, 16)
            sp.wait_ge(scattered, 16 * TILES * TOPK)
            sp.wait_ge(etab_ready, 1)

            def expert(j):
                return bass.ds(sp.value_load(etab[0:1, bass.ds(j, 1)], min_val=0, max_val=E1 - 1), 1)

            def load_x(j, buf):
                sp.dma_start(m_x[:, buf, :], d_xs[bass.ds(j * P, P)]).then_inc(mx_in[buf], 16)

            def load_gu(e, buf):
                sp.dma_start(m_gu[:, buf, :], A["w_gu1"][e].rearrange("a p n -> p (a n)")).then_inc(mgu_in[buf], 16)

            def load_dn(e, buf):
                sp.dma_start(m_dn[0:I1, buf, :], A["w_dn1"][e].rearrange("a p n -> p (a n)")).then_inc(mdn_in[buf], 16)

            for j in range(7):
                if j < 4:
                    load_dn(expert(j), j)
                else:
                    sp.wait_ge(mxT_psum, j - 3)
                load_x(j, j % 4)
                if j == 4 or j == 5:
                    sp.wait_ge(mgu_psum, j - 3)
                if j < 6:
                    load_gu(expert(j), j % 4)
            with sp.Fori(0, HEADS // 2) as hp:
                for k in range(24):
                    j = 24 * hp + k
                    e_gu, e_dn = expert(j + 6), expert(j + 4)
                    sp.wait_ge(mxT_psum, j + 4)
                    load_x(j + 7, (k + 3) % 4)
                    sp.wait_ge(mgu_psum, j + 3)
                    load_gu(e_gu, (k + 2) % 4)
                    sp.wait_ge(my_psum, j + 1)
                    load_dn(e_dn, k % 4)
                    sp.wait_ge(my_ready, j + 2)
                    sp.dma_start(d_ys[bass.ds(j * P, P)], m_y[:, k % 4, :]).then_inc(my_out[k % 4], 16)
                    if k % 12 == 6:
                        sp.wait_ge(corner_step, 6 * (HEADS + 2 * hp + k // 12 + 1))
                        load_corner(HEADS + 2 * hp + k // 12 + 2, k // 12)
            for k in range(4):
                sp.wait_ge(y_used, 4 * k + 4)
                sp.dma_start(A["out"][4 * k * P:4 * (k + 1) * P].rearrange("(t p) d -> p t d", p=P), resid[:, 4 * k:4 * k + 4, :]).then_inc(s_out, 16)
            sp.wait_ge(s_out, 64)
            for k in range(4):
                sp.wait_ge(mx_in[k], 16 * ((MT + 7 - k + 3) // 4))
                sp.wait_ge(mgu_in[k], 16 * ((MT + 6 - k + 3) // 4))
                sp.wait_ge(mdn_in[k], 16 * ((MT + 4 - k + 3) // 4))
            for k in range(2):
                sp.wait_ge(corner_in[k], 16 * (HEADS + 1))

        @block.gpsimd
        def _(pool):
            pool.memset(zeros[:, :], 0.0).then_inc(zeros_ready, 1)
            pool.memset(xssm[:, :, 0:1, 0:WARM], 0.0).then_inc(window_read, 1)
            pool.memset(xssm[:, :, SEGS // 2:SEGS // 2 + 1, 0:WARM], 0.0)
            pool.memset(xssm[:, :, SEGS // 2 - 1:SEGS // 2, WARM + SEG:PADSEG], 0.0)
            pool.memset(xssm[:, :, SEGS - 1:SEGS, WARM + SEG:PADSEG], 0.0).then_inc(pads, 1)
            for h in range(HALVES):
                pool.wait_ge(proj_evac, CHUNKS * (h + 1))
                for b in range(BATCH):
                    s0, s1 = b * SEGS // 2, (b + 1) * SEGS // 2
                    pool.tensor_copy(xssm[:, h, s0 + 1:s1, 0:WARM], xssm[:, h, s0:s1 - 1, SEG:SEG + WARM]).then_inc(halo, 1)
                    pool.tensor_copy(xssm[:, h, s0:s1 - 1, WARM + SEG:PADSEG], xssm[:, h, s0 + 1:s1, WARM:2 * WARM]).then_inc(halo, 1)
            pool.wait_ge(halo, 8)
            pool.wait_ge(pads, 1)
            pool.wait_ge(s_const, 96)

            def window_inputs(w, buf, h):
                base = SEG + 2 * WARM - WIN - WIN * w
                for m in range(WIN):
                    x_in = xssm[:, h, :, bass.ds(base + m, 1)].rearrange("p s a -> p a s").broadcast_to([P, STATES, SEGS])
                    b_in = ABC[:, 1, h * STATES:(h + 1) * STATES].unsqueeze(2).broadcast_to([P, STATES, SEGS])
                    out = buf[:, m, h * STATES * SEGS:(h + 1) * STATES * SEGS].rearrange("p (d s) -> p d s", d=STATES)
                    last = pool.tensor_tensor(out, x_in, b_in, ALU.mult)
                last.then_inc(ub_ready, 1)

            def gate_mul(n):
                pool.wait_ge(gu_evac, n + 1)
                pool.tensor_tensor(act[:, :, :], silu_g[:, :, :], up[:, :, :], ALU.mult).then_inc(act_ready, 1)

            pool.wait_ge(proj_psum, 4 * CHUNKS)
            for h in range(HALVES):
                window_inputs(0, scan_b[0], h)
            for h in range(HALVES):
                window_inputs(1, scan_b[1], h)
            for c in range(CHUNKS):
                if c:
                    pool.wait_ge(dn_psum, c)
                gate_mul(c)
                pool.wait_ge(b_step, 2 * WIN * (1 + c // 2) + 1)
                window_inputs(2 + c // 2, scan_b[c // 2], c % 2)
            with pool.Fori(0, E0) as e:
                for c in range(CHUNKS):
                    i, n = c // 2, CHUNKS * (e + 1) + c
                    if c % 2 == 0:
                        pool.wait_ge(b_step, 2 * WIN * (2 * e + 3 + i) + 1)
                        pool.wait_ge(window_read, 2 * e + i + 1)
                    window_inputs(2 * e + 4 + i, scan_b[i], c % 2)
                    pool.wait_ge(dn_psum, n)
                    gate_mul(n)

            pool.tensor_copy(identb[:, :], ident[:, :]).then_inc(corner_idb, 1)
            pool.memset(V[:, :, :, HD:HD + 1], 1.0).then_inc(v_ones, 1)
            pool.memset(zero, 0.0).then_inc(v_ones, 1)
            for k in range(4):
                pool.memset(small[:, 24 + k:25 + k], 0.0).then_inc(my_out[k], 16)
            pool.wait_ge(v_ones, 2)
            pool.wait_ge(xn1_ready, 1)
            pool.wait_ge(l1_p, 32)
            pool.tensor_tensor(resid[:, :, :], resid[:, :, :], bp_t.unsqueeze(1).broadcast_to([P, TILES, DIM]), ALU.add).then_inc(bp_added, 1)

            def rest(n, out, whole, part):
                pool.wait_ge(part_ready, n)
                pool.tensor_tensor(out, whole, part, ALU.subtract).then_inc(rest_step, 1)

            rest(1, qf, qf, parts[0])
            rest(2, kf, kf, parts[3])
            for c in range(CHUNKS):
                pool.wait_ge(sgu_evac, c + 1)
                if c:
                    pool.wait_ge(sdn_psum, c)
                pool.tensor_tensor(act[0:I1, :, :], silu_g[0:I1, :, :], up[0:I1, :, :], ALU.mult).then_inc(sact_ready, 1)
            rest(3, parts[2], qf, parts[1])
            rest(4, parts[5], kf, parts[4])

            def split_corner(n, buf, loads):
                f, p = corner_f[:, buf, 0:2 * CORNER], corner_p[:, buf]
                last_row = corner_f[:, buf, 2 * CORNER:].broadcast_to([P, 2 * CORNER])
                pool.wait_ge(corner_in[buf], loads)
                pool.tensor_tensor(f, f, last_row, ALU.subtract).then_inc(corner_step, 1)
                pool.wait_ge(corner_step, 6 * n + 1)
                pool.tensor_tensor(f, f, inv.broadcast_to([P, 2 * CORNER]), ALU.mult).then_inc(corner_step, 1)
                pool.wait_ge(corner_step, 6 * n + 2)
                pool.tensor_tensor(p[:, 0, :], f, zero.broadcast_to([P, 2 * CORNER]), ALU.add).then_inc(corner_step, 1)
                pool.wait_ge(corner_step, 6 * n + 3)
                pool.tensor_tensor(f, f, p[:, 0, :], ALU.subtract).then_inc(corner_step, 1)
                pool.wait_ge(corner_step, 6 * n + 4)
                pool.tensor_tensor(p[:, 1, :], f, zero.broadcast_to([P, 2 * CORNER]), ALU.add).then_inc(corner_step, 1)
                pool.wait_ge(corner_step, 6 * n + 5)
                pool.tensor_tensor(p[:, 2, :], f, p[:, 1, :], ALU.subtract).then_inc(corner_step, 1)

            pool.wait_ge(inv_ready, 1)
            pool.wait_ge(xs_zero, 16 * (SLOTS // 4))
            pool.wait_ge(slots_ready, 1)
            for n in range(HEADS):
                if n >= 2:
                    pool.wait_ge(corner_used, n - 1)
                split_corner(n, n % 2, 16 * (n // 2 + 1))
                for k in range(TOPK):
                    pool.indirect_dma_start(d_xs, bass.IndirectOffsetOnAxis(ap=slots[:, n, k:k + 1], axis=0),
                                            xn1[:, n, :], None).then_inc(scattered, 16)
            with pool.Fori(0, HEADS // 2) as hp:
                for k in range(2):
                    n = HEADS + 2 * hp + k
                    pool.wait_ge(corner_used, n - 1)
                    split_corner(n, k, 16 * (HEADS // 2 + hp + 1))
            for b in range(4):
                pool.wait_ge(my_out[b], 16 * (MT // 4 + 1))
            pool.wait_ge(p_free, 2 + 8 * UNITS)
            for t in range(TILES):
                if t >= 2:
                    pool.wait_ge(y_used, t - 1)
                for k in range(TOPK):
                    pool.indirect_dma_start(ybuf[:, t % 2, k, :], None, d_ys,
                                            bass.IndirectOffsetOnAxis(ap=slots[:, t, k:k + 1], axis=0)).then_inc(y_in[t % 2], 16)

        @block.scalar
        def _(sc):
            for k in range(2):
                sc.wait_ge(var_ready, k + 1)
                sc.activation(stat[:, 2, :], stat[:, 1, :], ACT.Sqrt).then_inc(std_ready, 1)
            for g in range(TILES // TB):
                sc.wait_ge(xnT_psum, g + 1)
                sc.activation(xnT[:, g * 512:(g + 1) * 512], bank[g % 2][:, :], ACT.Copy).then_inc(xnT_ready, 1)
            sc.wait_ge(logit_psum, 1)
            sc.activation(logit[:, :, :], bank[7][:, 0:TILES * E0], ACT.Copy).then_inc(logit_ready, 1)
            sc.wait_ge(s_const, 96)
            for g in range(TILES // TB):
                sc.wait_ge(xaT_psum, g + 1)
                sc.activation(xaT[:, g * 512:(g + 1) * 512], bank[2 + g % 2][:, :], ACT.Identity,
                              scale=lnwb[:, 0:1], bias=lnwb[:, 1:2]).then_inc(xaT_ready, 1)
            sc.wait_ge(pads, 1)
            for k in range(HALVES * CHUNKS):
                h, c = k // CHUNKS, k % CHUNKS
                sc.wait_ge(proj_psum, k + 1)
                sc.activation(xssm[:, h, CT * c:CT * c + CT, WARM:WARM + SEG],
                              bank[4 + k % 2][:, :], ACT.Copy).then_inc(proj_evac, 1)
            sc.activation(ABC[:, 0, :], ABC[:, 0, :], ACT.Exp).then_inc(a_exp, 1)
            sc.wait_ge(logit_max, 1)
            sc.activation(score[:, :], top[:, :, 0:1], ACT.Sigmoid).then_inc(score_ready, 1)
            for g in range(TILES // TB):
                sc.wait_ge(xsT_psum, g + 1)
                sc.activation(xsT[:, g * 512:(g + 1) * 512], bank[g % 2][:, :], ACT.Copy).then_inc(xsT_ready, 1)
            for k in range(HALVES * CHUNKS, 2 * HALVES * CHUNKS):
                h, c = k // CHUNKS - HALVES, k % CHUNKS
                sc.wait_ge(proj_psum, k + 1)
                sc.activation(sgate[:, h, c * CHUNK:(c + 1) * CHUNK], bank[4 + k % 2][:, :], ACT.Silu).then_inc(proj_evac, 1)
            sc.wait_ge(halo, 8)
            sc.wait_ge(proj_psum, 4 * CHUNKS)

            def window_inputs(w, buf, h):
                for ch in range(h * STATES, (h + 1) * STATES):
                    x_in = xssm[:, h, :, bass.ds(WIN * w, WIN)].rearrange("p s m -> p m s")
                    last = sc.activation(buf[:, :, ch * SEGS:(ch + 1) * SEGS], x_in, ACT.Copy, scale=ABC[:, 1, ch:ch + 1])
                last.then_inc(uf_ready, 1)

            def evac_gu(n):
                for m in range(2):
                    sc.wait_ge(gu_psum, 2 * n + m + 1)
                    sc.activation(silu_g[:, m, :], bank[m][:, :], ACT.Silu)
                    last = sc.activation(up[:, m, :], bank[2 + m][:, :], ACT.Copy)
                last.then_inc(gu_evac, 1)

            for h in range(HALVES):
                window_inputs(0, scan_f[0], h)
            for h in range(HALVES):
                window_inputs(1, scan_f[1], h)
            for c in range(CHUNKS):
                if c:
                    sc.wait_ge(act_ready, c)
                evac_gu(c)
                sc.wait_ge(f_step, 2 * WIN * (1 + c // 2) + 1)
                window_inputs(2 + c // 2, scan_f[c // 2], c % 2)
            with sc.Fori(0, E0) as e:
                for c in range(CHUNKS):
                    i, n = c // 2, CHUNKS * (e + 1) + c
                    if c % 2 == 0:
                        sc.wait_ge(f_step, 2 * WIN * (2 * e + 3 + i) + 1)
                        sc.wait_ge(window_read, 2 * e + i + 1)
                    window_inputs(2 * e + 4 + i, scan_f[i], c % 2)
                    sc.wait_ge(act_ready, n)
                    evac_gu(n)

            sc.wait_ge(var_ready, 3)
            sc.activation(stat[:, 2, :], stat[:, 1, :], ACT.Sqrt).then_inc(std_ready, 1)
            for g in range(TILES // TB):
                sc.wait_ge(xn1T_psum, g + 1)
                sc.activation(xn1T[:, g * 512:(g + 1) * 512], bank[g % 2], ACT.Copy).then_inc(xn1T_ready, 1)
            sc.wait_ge(inv_ready, 1)
            for k in range(2 * CHUNKS):
                sc.wait_ge(qk_psum, k + 1)
                c = k % CHUNKS
                out = (qf if k < CHUNKS else kf)[:, c * CHUNK:(c + 1) * CHUNK]
                if k < CHUNKS:
                    sc.activation(out, bank[2 + k % 2], ACT.Identity, scale=inv, bias=bqi).then_inc(qk_ready, 1)
                else:
                    sc.activation(out, bank[2 + k % 2], ACT.Identity, bias=bk).then_inc(qk_ready, 1)
            for k in range(2):
                sc.wait_ge(lg1_psum, k + 1)
                sc.activation(sc1[:, 8 * k:8 * k + 8, :], bank[6 + k].rearrange("p (t e) -> p t e", e=E1), ACT.Sigmoid).then_inc(sc1_ready, 1)
            sc.wait_ge(qk_ready, 2 * CHUNKS)
            sc.activation(parts[0], qf, ACT.Copy).then_inc(part_ready, 1)
            sc.activation(parts[3], kf, ACT.Copy).then_inc(part_ready, 1)
            for c in range(CHUNKS):
                if c:
                    sc.wait_ge(sact_ready, c)
                for m in range(2):
                    sc.wait_ge(sgu_psum, 2 * c + m + 1)
                    sc.activation(silu_g[0:I1, m, :], bank[m][0:I1, :], ACT.Silu)
                    last = sc.activation(up[0:I1, m, :], bank[2 + m][0:I1, :], ACT.Copy)
                last.then_inc(sgu_evac, 1)
            sc.wait_ge(rest_step, 1)
            sc.activation(parts[1], qf, ACT.Copy).then_inc(part_ready, 1)
            sc.wait_ge(rest_step, 2)
            sc.activation(parts[4], kf, ACT.Copy).then_inc(part_ready, 1)

            def half_tanh(j, k):
                sc.wait_ge(mgu_psum, j + 1)
                sc.activation(m_th[:, k, :], bank[6][:, 0:I1], ACT.Tanh, scale=0.5).then_inc(mth_ready, 1)

            half_tanh(0, 0)
            half_tanh(1, 1)
            sc.activation(stat[:, 0, :], stat[:, 1, :], ACT.Copy).then_inc(p_free, 2)
            sc.wait_ge(sact_ready, CHUNKS)
            with sc.Fori(0, HEADS // 2) as hp:
                for k in range(4):
                    for g in range(8):
                        G = 32 * hp + 8 * k + g
                        if g < 6:
                            j = 24 * hp + 6 * k + g
                            sc.wait_ge(ma_ready, j + 1)
                            half_tanh(j + 2, g % 2)
                        sc.wait_ge(st_psum, G + 1)
                        sc.wait_ge(p_free, G + 1)
                        sc.activation(Pt[g % 2][:, :, :], psum[:, 1024 * (g % 2):1024 * (g % 2) + 1024].rearrange("p (a n) -> p a n", a=2),
                                      ACT.Exp).then_inc(p_ready, 1)
            for g in range(TILES // TB):
                sc.wait_ge(attT_psum, g + 1)
                sc.activation(attT[:, g * 512:(g + 1) * 512], bank[g % 2], ACT.Copy).then_inc(attT_ready, 1)

        @block.tensor
        def _(pe):
            pe.wait_ge(s_const, 96)
            pe.wait_ge(xn_ready, 1)
            for g in range(TILES // TB):
                if g >= 2:
                    pe.wait_ge(xnT_ready, g - 1)
                for i in range(TB):
                    last = pe.transpose(bank[g % 2][:, i * P:(i + 1) * P], xn[:, g * TB + i, :], ident[:, :])
                last.then_inc(xnT_psum, 1)
            pe.wait_ge(xnT_ready, 4)
            for t in range(TILES):
                last = pe.matmul(bank[7][:, t * E0:(t + 1) * E0], xnT[:, t * P:(t + 1) * P], w_gate0[:, :], start=True, stop=True)
            last.then_inc(logit_psum, 1)
            pe.wait_ge(xa_ready, 1)
            for g in range(TILES // TB):
                if g >= 2:
                    pe.wait_ge(xaT_ready, g - 1)
                for i in range(TB):
                    last = pe.transpose(bank[2 + g % 2][:, i * P:(i + 1) * P], xa[:, g * TB + i, :], ident[:, :])
                last.then_inc(xaT_psum, 1)
            pe.wait_ge(s_w, 32)
            for k in range(2 * HALVES * CHUNKS):
                if k == HALVES * CHUNKS:
                    pe.wait_ge(xs_ready, 1)
                    for g in range(TILES // TB):
                        if g >= 2:
                            pe.wait_ge(xsT_ready, g - 1)
                        for i in range(TB):
                            last = pe.transpose(bank[g % 2][:, i * P:(i + 1) * P], xs[:, g * TB + i, :], ident[:, :])
                        last.then_inc(xsT_psum, 1)
                m, c = k // CHUNKS, k % CHUNKS
                pe.wait_ge(xaT_ready, min(c + 1, 4))
                if k >= 2:
                    pe.wait_ge(proj_evac, k - 1)
                pe.matmul(bank[4 + k % 2][:, :], w_in[:, m * P:(m + 1) * P], xaT[:, c * CHUNK:(c + 1) * CHUNK],
                          start=True, stop=True).then_inc(proj_psum, 1)

            def gate_up(src, c, n):
                pe.wait_ge(gu_evac, n) if not (isinstance(n, int) and n == 0) else None
                for m in range(2):
                    pe.matmul(bank[m][:, :], w_gu[:, m * P:(m + 1) * P], src[:, c * CHUNK:(c + 1) * CHUNK], start=True, stop=True)
                    pe.matmul(bank[2 + m][:, :], w_gu[:, I0 + m * P:I0 + (m + 1) * P], src[:, c * CHUNK:(c + 1) * CHUNK],
                              start=True, stop=True).then_inc(gu_psum, 1)

            def down(n):
                pe.wait_ge(act_ready, n + 1)
                if not (isinstance(n, int) and n == 0):
                    pe.wait_ge(dn_added, n)
                for q in range(CT):
                    for m in range(2):
                        last = pe.matmul(bank[4][:, q * P:(q + 1) * P], act[:, m, q * P:(q + 1) * P], w_dn[:, m, :],
                                         start=(m == 0), stop=(m == 1))
                last.then_inc(dn_psum, 1)

            def contract(w, i, d):
                step, scan = (f_step, scan_f) if d == 0 else (b_step, scan_b)
                pe.wait_ge(step, 2 * WIN * (w + 1))
                for h in range(HALVES):
                    for s in range(STATES):
                        ch = h * STATES + s
                        last = pe.matmul(bank[5 + i][:, (2 * d + h) * P:(2 * d + h + 1) * P], diagC[:, ch, :],
                                         scan[(3 + i) % 2][:, :, ch * SEGS:(ch + 1) * SEGS],
                                         start=(s == 0), stop=(s == STATES - 1))
                return last

            pe.wait_ge(wgu_in, 16)
            pe.wait_ge(wdn_in, 16)
            pe.wait_ge(xsT_ready, 4)
            for c in range(CHUNKS):
                gate_up(xnT, c, c)
                down(c)
            pe.wait_ge(scan_consts, 1)
            with pe.Fori(0, E0) as e:
                pe.wait_ge(wgu_in, 16 * e + 32)
                for c in range(CHUNKS):
                    gate_up(xsT, c, CHUNKS * (e + 1) + c)
                    i, d = c // 2, c % 2
                    if d == 0:
                        pe.wait_ge(y_added, 2 * e + 1)
                    last = contract(2 * e + 3 + i, i, d)
                    if d == 1:
                        last.then_inc(window_read, 1)
                    if c == 0:
                        pe.wait_ge(wdn_in, 16 * e + 32)
                    down(CHUNKS * (e + 1) + c)
            pe.wait_ge(o_ready, 1)
            pe.wait_ge(gu_evac, CHUNKS * (E0 + 1))
            for g in range(TILES // TB):
                for q in range(TB):
                    t = g * TB + q
                    for h in range(HALVES):
                        last = pe.matmul(bank[g][:, q * P:(q + 1) * P], sgate[:, h, t * P:(t + 1) * P], w_out[:, h, :],
                                         start=(h == 0), stop=(h == 1))
                last.then_inc(out_psum, 1)

            def transposes(src, dst, done, free):
                for g in range(TILES // TB):
                    if g >= 2:
                        pe.wait_ge(free, g - 1)
                    for i in range(TB):
                        last = pe.transpose(bank[g % 2][:, i * P:(i + 1) * P], src[:, g * TB + i, :], ident[:, :])
                    last.then_inc(done, 1)

            pe.wait_ge(xn1_ready, 1)
            transposes(xn1, xn1T, xn1T_psum, xn1T_ready)
            pe.wait_ge(xn1T_ready, 4)
            pe.wait_ge(l1_w, 160)
            for t in range(TILES):
                last = pe.matmul(bank[6 + t // 8][:, (t % 8) * E1:(t % 8 + 1) * E1], xn1T[:, t * P:(t + 1) * P], w_gate1, start=True, stop=True)
                if t % 8 == 7:
                    last.then_inc(lg1_psum, 1)
            for k in range(2 * CHUNKS):
                if k >= 2:
                    pe.wait_ge(qk_ready, k - 1)
                c = k % CHUNKS
                pe.matmul(bank[2 + k % 2], w_q if k < CHUNKS else w_k, xn1T[:, c * CHUNK:(c + 1) * CHUNK], start=True, stop=True).then_inc(qk_psum, 1)
            for g in range(TILES // TB):
                if g >= 2:
                    pe.wait_ge(v_ready, g - 1)
                for q in range(TB):
                    t = g * TB + q
                    last = pe.matmul(bank[4 + g % 2][:, q * P:(q + 1) * P], xn1T[:, t * P:(t + 1) * P], w_v, start=True, stop=True)
                last.then_inc(v_psum, 1)
            pe.wait_ge(qk_ready, 2 * CHUNKS)
            pe.wait_ge(v_ready, 4)
            for c in range(CHUNKS):
                if c:
                    pe.wait_ge(sgu_evac, c)
                for m in range(2):
                    pe.matmul(bank[m][0:I1, :], w_sh[:, m * I1:(m + 1) * I1], xn1T[:, c * CHUNK:(c + 1) * CHUNK], start=True, stop=True)
                    pe.matmul(bank[2 + m][0:I1, :], w_sh[:, (2 + m) * I1:(3 + m) * I1], xn1T[:, c * CHUNK:(c + 1) * CHUNK],
                              start=True, stop=True).then_inc(sgu_psum, 1)
                pe.wait_ge(sact_ready, c + 1)
                if c:
                    pe.wait_ge(sdn_added, c)
                for q in range(CT):
                    for m in range(2):
                        last = pe.matmul(bank[4][:, q * P:(q + 1) * P], act[0:I1, m, q * P:(q + 1) * P], w_shd[0:I1, m, :],
                                         start=(m == 0), stop=(m == 1))
                last.then_inc(sdn_psum, 1)
            pe.wait_ge(mask_ready, 1)
            pe.wait_ge(sgu_evac, CHUNKS)
            pe.wait_ge(sc1_ready, 2)
            for k in range(2):
                pe.matmul(bank[6 + k], strict, M[:, 8 * k:8 * k + 8, :], start=True, stop=True)
                last = pe.matmul(bank[2 + k], ones, M[:, 8 * k:8 * k + 8, :], start=True, stop=True)
            last.then_inc(rank_psum, 1)
            pe.wait_ge(exp_ready, 1)
            for c in range(2):
                last = pe.matmul(bank[0][0:1, c * P:(c + 1) * P], exp_of[:, c:c + 1], ident[:, :], start=True, stop=True)
            last.then_inc(etab_psum, 1)

            pe.wait_ge(stacked, 16 * 18)
            pe.wait_ge(corner_idb, 1)
            pe.wait_ge(etab_ready, 1)
            pe.wait_ge(slots_ready, 1)
            with pe.Fori(0, HEADS // 2) as hp:
                for k in range(4):
                    u = 4 * hp + k
                    for q in range(QT):
                        pair = bank[2 * (q % 2):2 * (q % 2) + 2]
                        n = 32 * hp + 8 * k + q
                        pe.wait_ge(pair_free, n + 1)
                        queries = Qs[0:KROWS, bass.ds(u * LEN + q * P, P)]
                        for a in range(2):
                            biased = a == 1 and q < 2
                            last = pe.matmul(pair[a], queries, Ks[0:KROWS, bass.ds(u * LEN + a * 512, 512)], start=True, stop=not biased)
                            if biased:
                                if k % 2 == 0 and q == 0:
                                    pe.wait_ge(corner_step, 6 * (2 * hp + k // 2 + 1))
                                for p in range(3):
                                    last = pe.matmul(pair[1][:, CORNER:], identb[:, :], corner_p[:, k // 2, p, q * CORNER:(q + 1) * CORNER],
                                                     start=False, stop=(p == 2))
                        last.then_inc(sq_psum, 1)
                        if k % 2 == 1 and q == 2:
                            pass
                    if k % 2 == 1:
                        pe.wait_ge(sq_psum, 32 * hp + 8 * k + 8)
                        pe.nop().then_inc(corner_used, 1)
            pe.wait_ge(pair_free, 2 + 8 * UNITS)
            for c in range(2):
                last = pe.transpose(bank[0][:, c * P:(c + 1) * P], nm[:, 16 * c:16 * c + 16, :].rearrange("p u q -> p (u q)"), ident[:, :])
            last.then_inc(nmT_psum, 1)

            def x_transpose(j, k4, loads):
                pe.wait_ge(mx_in[k4], 16 * loads)
                pe.transpose(bank[5][:, 0:P], m_x[:, k4, :], ident[:, :]).then_inc(mxT_psum, 1)

            def tile_gate_up(j, k2, k4, loads):
                pe.wait_ge(mgu_in[k4], 16 * loads)
                pe.wait_ge(mxT_ready, j + 1)
                pe.matmul(bank[6][:, 0:2 * I1], m_xT[:, k2, :], m_gu[:, k4, :], start=True, stop=True).then_inc(mgu_psum, 1)

            def a_transpose(j, k2):
                pe.wait_ge(ma_ready, j + 1)
                pe.transpose(bank[7][0:I1, 0:P], m_b[:, k2, :], ident[:, :]).then_inc(maT_psum, 1)

            def tile_down(j, k2, k4, loads):
                pe.wait_ge(mdn_in[k4], 16 * loads)
                pe.wait_ge(maT_ready, j + 1)
                pe.matmul(bank[7][:, 256:256 + P], m_aT[0:I1, k2, :], m_dn[0:I1, k4, :], start=True, stop=True).then_inc(my_psum, 1)

            def keys_scores(u, g):
                qh, kp = g // 4, g % 4
                for a in range(2):
                    kt = 2 * kp + a
                    out = bank[2 * (g % 2) + a]
                    biased = g == 3
                    last = pe.matmul(out, Ks[0:KROWS, bass.ds(u * LEN + kt * P, P)], Qs[0:KROWS, bass.ds(u * LEN + qh * 512, 512)],
                                     start=True, stop=not biased)
                    if biased:
                        for p in range(3):
                            last = pe.matmul(out[:, 0:CORNER], identb[:, :], corner_p[:, (hpk[0] // 2) % 2, p, a * CORNER:(a + 1) * CORNER],
                                             start=False, stop=(p == 2))
                last.then_inc(st_psum, 1)

            hpk = [0]
            x_transpose(0, 0, 1)
            pe.wait_ge(mxT_ready, 1)
            x_transpose(1, 1, 1)
            tile_gate_up(0, 0, 0, 1)
            pe.wait_ge(mxT_ready, 2)
            x_transpose(2, 2, 1)
            pe.wait_ge(ma_ready, 1)
            tile_gate_up(1, 1, 1, 1)
            a_transpose(0, 0)
            pe.wait_ge(nm_in, 16)
            pe.wait_ge(nmT_ready, 3)
            keys_scores(0, 0)
            keys_scores(0, 1)
            with pe.Fori(0, HEADS // 2) as hp:
                for k in range(4):
                    u = 4 * hp + k
                    hpk[0] = k
                    for g in range(8):
                        G = 32 * hp + 8 * k + g
                        if g < 6:
                            i = 6 * k + g
                            j = 24 * hp + i
                            pe.wait_ge(mxT_ready, j + 3)
                            x_transpose(j + 3, (i + 3) % 4, 6 * hp + (i + 3) // 4 + 1)
                            pe.wait_ge(ma_ready, j + 2)
                            tile_gate_up(j + 2, i % 2, (i + 2) % 4, 6 * hp + (i + 2) // 4 + 1)
                            pe.wait_ge(maT_ready, j + 1)
                            pe.wait_ge(my_ready, j + 1)
                            a_transpose(j + 1, (i + 1) % 2)
                            tile_down(j, i % 2, i % 4, 6 * hp + i // 4 + 1)
                        pe.wait_ge(p_ready, G + 1)
                        if g == 1 and k % 2 == 0:
                            pe.wait_ge(corner_step, 6 * (HEADS + 2 * hp + k // 2 + 1))
                        keys_scores(u if g < 6 else u + 1, (g + 2) % 8)
                        if g == 2 and k % 2 == 1:
                            pass
                        if g == 0:
                            pe.wait_ge(att_free, u + 1)
                        qh, kp = g // 4, g % 4
                        for a in range(2):
                            for q in range(4):
                                last = pe.matmul(bank[4][:, 16 * (4 * qh + q):16 * (4 * qh + q) + HD + 1],
                                                 Pt[g % 2][:, a, q * P:(q + 1) * P],
                                                 V[:, (k % 2) * QT + 2 * kp + a, bass.ds(2 * hp + k // 2, 1), :].rearrange("p a d -> p (a d)"),
                                                 start=(g == 0 and a == 0 and q == 0), stop=(kp == 3 and a == 1), skip_group_check=True)
                        last.then_inc(p_free, 1)
                        if k % 2 == 1 and g == 7:
                            pe.wait_ge(p_free, G + 3)
                            pe.nop().then_inc(corner_used, 1)
            pe.wait_ge(att_ready, UNITS)
            transposes(att, attT, attT_psum, attT_ready)
            for g in range(TILES // TB):
                pe.wait_ge(attT_ready, g + 1)
                for q in range(TB):
                    t = g * TB + q
                    last = pe.matmul(bank[2 + g][:, q * P:(q + 1) * P], attT[:, t * P:(t + 1) * P], w_p[:, :], start=True, stop=True)
                last.then_inc(fin_psum, 1)

        @block.vector
        def _(dve):
            steps = [0]

            def link(ins):
                steps[0] += 1
                ins.then_inc(ln_step, 1)
                dve.wait_ge(ln_step, steps[0])

            norms = [0]
            sq_of = [sq]

            def bcast(v):
                return v.unsqueeze(2).broadcast_to([P, TILES, DIM])

            def norm(src, dst, done):
                link(dve.tensor_reduce(stat[:, 0, :], src, X, ALU.add))
                link(dve.tensor_scalar(stat[:, 0, :], stat[:, 0, :], 1.0 / DIM, None, ALU.mult))
                link(dve.tensor_tensor(dst, src, bcast(stat[:, 0, :]), ALU.subtract))
                link(dve.tensor_tensor(sq_of[0], dst, dst, ALU.mult))
                link(dve.tensor_reduce(stat[:, 1, :], sq_of[0], X, ALU.add))
                dve.tensor_scalar(stat[:, 1, :], stat[:, 1, :], 1.0 / DIM, EPS, ALU.mult, ALU.add).then_inc(var_ready, 1)
                norms[0] += 1
                dve.wait_ge(std_ready, norms[0])
                link(dve.reciprocal(stat[:, 3, :], stat[:, 2, :]))
                dve.tensor_tensor(dst, dst, bcast(stat[:, 3, :]), ALU.mult).then_inc(done, 1)

            dve.wait_ge(s_x, 64)
            norm(resid[:, :, :], xn, xn_ready)
            dve.wait_ge(xn_ready, 1)
            norm(xn, xa, xa_ready)
            dve.wait_ge(logit_ready, 1)
            for t in range(TILES):
                last = dve.max(top[:, t, :], logit[:, t, :])
            last.then_inc(logit_max, 1)
            dve.wait_ge(logit_max, 1)
            for t in range(TILES):
                last = dve.max_index(topi[:, t, :], top[:, t, :], logit[:, t, :])
            link(last)
            link(dve.tensor_copy(topf[:, :, :], topi[:, :, 0:1]))
            dve.wait_ge(s_const, 96)
            dve.tensor_tensor(onehot[:, :, :], iota8[:, :].unsqueeze(1).broadcast_to([P, TILES, 8]),
                              topf[:, :, :].broadcast_to([P, TILES, 8]), ALU.is_equal).then_inc(onehot_ready, 1)
            dve.wait_ge(score_ready, 1)
            dve.tensor_tensor(xs, xn, bcast(score[:, :]), ALU.mult).then_inc(xs_ready, 1)
            dve.wait_ge(a_exp, 1)
            link(dve.tensor_scalar(ABC[:, 0, :], ABC[:, 0, :], -10.0, -0.01, ALU.max, ALU.min))
            link(dve.tensor_reduce(decay[:, :], ABC[:, 0, :], X, ALU.max))
            link(dve.tensor_scalar(decay[:, :], decay[:, :], -1.0, None, ALU.mult))
            for ch in range(CH):
                last = dve.tensor_scalar(diagC[:, ch, :], ident[:, :], ABC[:, 2, ch:ch + 1], None, ALU.mult)
            last.then_inc(scan_consts, 1)
            dve.wait_ge(proj_psum, 4 * CHUNKS)
            dve.memset(y_flat, 0.0).then_inc(y_added, 1)
            dve.wait_ge(zeros_ready, 1)
            dve.wait_ge(y_added, 1)

            def window(w, p, first=False, extra=()):
                extra = dict(extra)
                dve.wait_ge(uf_ready, 2 * w + 2)
                dve.wait_ge(ub_ready, 2 * w + 2)
                for j in range(WIN):
                    prev_f = scan_f[p][:, j - 1, :] if j else scan_f[1 - p][:, WIN - 1, :]
                    prev_b = scan_b[p][:, WIN - j, :] if j else scan_b[1 - p][:, 0, :]
                    if first and j == 0:
                        prev_f = prev_b = zeros[:, :]
                    cur_f, cur_b = scan_f[p][:, j, :], scan_b[p][:, WIN - 1 - j, :]
                    for step, prev, cur in ((f_step, prev_f, cur_f), (b_step, prev_b, cur_b)):
                        if not (first and j == 0):
                            dve.wait_ge(step, 2 * WIN * w + 2 * j)
                        dve.scalar_tensor_tensor(cur, prev, decay[:, 0:1], cur, ALU.mult, ALU.add).then_inc(step, 1)
                    for step, cur in ((f_step, cur_f), (b_step, cur_b)):
                        dve.wait_ge(step, 2 * WIN * w + 2 * j + 1)
                        dve.tensor_scalar(cur, cur, -H_MAX, H_MAX, ALU.max, ALU.min).then_inc(step, 1)
                    if j in extra:
                        extra[j]()

            def add_down(n, c, weight):
                dve.wait_ge(dn_psum, n + 1)
                for q in range(CT):
                    t = c * CT + q
                    out = bank[4][:, q * P:(q + 1) * P]
                    if weight is None:
                        last = dve.tensor_tensor(resid[:, t, :], resid[:, t, :], out, ALU.add)
                    else:
                        last = dve.scalar_tensor_tensor(resid[:, t, :], out, onehot[:, t, weight], resid[:, t, :], ALU.mult, ALU.add)
                last.then_inc(dn_added, 1)

            def add_y(n, i):
                dve.wait_ge(window_read, n + 2)
                lo = WIN * n
                for d, base in ((0, lo), (1, SEG - WIN - lo)):
                    for h in range(HALVES):
                        dst = y[:, h, :].rearrange("p (s t) -> p s t", s=SEGS)[:, :, bass.ds(base, WIN)]
                        src = bank[5 + i][:, (2 * d + h) * P:(2 * d + h + 1) * P].rearrange("p (m s) -> p s m", m=WIN)
                        last = dve.tensor_tensor(dst, dst, src, ALU.add)
                last.then_inc(y_added, 1)

            window(0, 0, first=True)
            window(1, 1, extra={7: lambda: (add_down(0, 0, None), add_down(1, 1, None))})
            window(2, 0, extra={7: lambda: (add_down(2, 2, None), add_down(3, 3, None))})
            with dve.Fori(0, E0) as e:
                def lag(n):
                    return lambda: add_down(CHUNKS * (e + 1) + n, n, bass.ds(e, 1))
                window(2 * e + 3, 1)
                window(2 * e + 4, 0, extra={1: lag(0), 5: lag(1), 7: lambda: add_y(2 * e, 0)})
                lag(2)()
                lag(3)()
                add_y(2 * e + 1, 1)
            dve.wait_ge(y_added, 2 * E0 + 1)
            dve.scalar_tensor_tensor(sgate[:, :, :], y[:, :, :], 0.5, sgate[:, :, :], ALU.mult, ALU.mult).then_inc(o_ready, 1)
            for g in range(TILES // TB):
                dve.wait_ge(out_psum, g + 1)
                dve.tensor_tensor(resid[:, g * TB:(g + 1) * TB, :], resid[:, g * TB:(g + 1) * TB, :], bank[g][:, :].rearrange("p (t d) -> p t d", t=TB), ALU.add).then_inc(x1_ready, 1)

            link(dve.tensor_scalar(inv, temp, 0.1, 10.0, ALU.max, ALU.min))
            link(dve.tensor_scalar(inv, inv, float(np.sqrt(np.float32(DIM))), None, ALU.mult))
            link(dve.reciprocal(inv, inv))
            dve.tensor_tensor(bqi, bq, inv, ALU.mult).then_inc(inv_ready, 1)
            sq_of[0] = sq1
            dve.wait_ge(x1_ready, 4)
            norm(resid[:, :, :], xn1, xn1_ready)
            dve.wait_ge(sc1_ready, 2)
            flat = lambda a: a.rearrange("p t e -> p (t e)")
            link(dve.tensor_tensor(sfc, sc1, gbias.unsqueeze(1).broadcast_to([P, TILES, E1]), ALU.add))
            G8 = TILES * GROUPS
            v8 = flat(sfc).rearrange("p (g k) -> p g k", k=8)

            def three(a, n):
                return a[:, 0:G8 * n].rearrange("p (g k) -> p g k", k=n)

            hi, lo, lo2 = three(net[0], 4), three(net[1], 4), None
            dve.tensor_tensor(hi, v8[:, :, 0:4], v8[:, :, 4:8], ALU.max)
            link(dve.tensor_tensor(lo, v8[:, :, 0:4], v8[:, :, 4:8], ALU.min))
            for n in (2, 1):
                mid, top_lo = three(net[2], n), net[2][:, G8 * n:2 * G8 * n].rearrange("p (g k) -> p g k", k=n)
                dve.tensor_tensor(mid, hi[:, :, 0:n], hi[:, :, n:2 * n], ALU.min)
                link(dve.tensor_tensor(top_lo, lo[:, :, 0:n], lo[:, :, n:2 * n], ALU.max))
                dve.tensor_tensor(hi[:, :, 0:n], hi[:, :, 0:n], hi[:, :, n:2 * n], ALU.max)
                link(dve.tensor_tensor(lo[:, :, 0:n], mid, top_lo, ALU.max))
            link(dve.tensor_tensor(gs[:, :, :].rearrange("p t g -> p (t g)").unsqueeze(2), hi[:, :, 0:1], lo[:, :, 0:1], ALU.add))
            for t in range(TILES):
                last = dve.max(gtop[:, t, :], gs[:, t, :])
            link(last)
            for t in range(TILES):
                last = dve.max_index(gidx[:, t, :], gtop[:, t, :], gs[:, t, :])
            link(last)
            link(dve.tensor_copy(gidxf[:, :, :], gidx[:, :, :]))
            pick = net[0][:, 0:G8 * TOPG].rearrange("p (t g k) -> p t g k", t=TILES, g=GROUPS)
            link(dve.tensor_tensor(pick, iota8[:, :].unsqueeze(1).unsqueeze(3).broadcast_to([P, TILES, GROUPS, TOPG]),
                                   gidxf[:, :, 0:TOPG].unsqueeze(2).broadcast_to([P, TILES, GROUPS, TOPG]), ALU.is_equal))
            link(dve.tensor_reduce(gmask, pick, X, ALU.add))
            link(dve.tensor_tensor(flat(masked).rearrange("p (g k) -> p g k", k=8), v8,
                                   gmask.rearrange("p t g -> p (t g)").unsqueeze(2).broadcast_to([P, G8, 8]), ALU.mult))
            link(dve.tensor_scalar(masked, masked, 0.0, None, ALU.add))
            for t in range(TILES):
                last = dve.max(etop[:, t, :], masked[:, t, :])
            link(last)
            for t in range(TILES):
                last = dve.match_replace(repl[:, t, :], etop[:, t, :], masked[:, t, :], -3.0e38)
            link(last)
            dve.tensor_tensor(M, masked, repl, ALU.not_equal).then_inc(mask_ready, 1)
            dve.wait_ge(mask_ready, 1)
            link(dve.tensor_tensor(rw, sc1, M, ALU.mult))
            link(dve.tensor_reduce(den1[:, :], rw, X, ALU.add))
            link(dve.tensor_scalar(den1[:, :], den1[:, :], 1e-20, None, ALU.add))
            link(dve.reciprocal(den1[:, :], den1[:, :]))
            link(dve.tensor_scalar(den1[:, :], den1[:, :], 2.5 * 0.5, None, ALU.mult))
            link(dve.tensor_tensor(rw, rw, den1[:, :].unsqueeze(2).broadcast_to([P, TILES, E1]), ALU.mult))
            dve.wait_ge(v_ones, 1)
            for g in range(TILES // TB):
                dve.wait_ge(v_psum, g + 1)
                for q in range(TB):
                    t = g * TB + q
                    last = dve.tensor_tensor(V[:, t, :, 0:HD], bank[4 + g % 2][:, q * P:(q + 1) * P].rearrange("p (h d) -> p h d", h=HEADS),
                                             bv_t.rearrange("p (h d) -> p h d", h=HEADS), ALU.add)
                last.then_inc(v_ready, 1)
            dve.wait_ge(bp_added, 1)
            for c in range(CHUNKS):
                dve.wait_ge(sdn_psum, c + 1)
                dve.tensor_tensor(resid[:, CT * c:CT * c + CT, :], resid[:, CT * c:CT * c + CT, :],
                                  bank[4].rearrange("p (t d) -> p t d", t=CT), ALU.add).then_inc(sdn_added, 1)
            link(dve.memset(carry[:, 0, :], 0.0))
            dve.wait_ge(rank_psum, 1)
            total = [bank[2 + t // 8][:, (t % 8) * E1:(t % 8 + 1) * E1] for t in range(TILES)]
            for t in range(1, TILES):
                link(dve.tensor_tensor(carry[:, t, :], carry[:, t - 1, :], total[t - 1], ALU.add))
            link(dve.tensor_tensor(nt, carry[:, TILES - 1, :], total[TILES - 1], ALU.add))
            link(dve.tensor_scalar(ntu[:, :], nt, float(P - 1), None, ALU.add))
            link(dve.tensor_scalar(ntu[:, :], ntu[:, :], 7, None, ALU.logical_shift_right))
            link(dve.tensor_copy(nt, ntu[:, :]))
            link(dve.memset(ones64, 1.0))
            link(dve.tensor_tensor_scan(endt, ones64, nt, 0.0, ALU.mult, ALU.add))
            link(dve.tensor_tensor(base1, endt, nt, ALU.subtract))
            link(dve.tensor_scalar(base1, base1, float(P), None, ALU.mult))
            for k in range(2):
                last = dve.tensor_tensor(slot[:, 8 * k:8 * k + 8, :], carry[:, 8 * k:8 * k + 8, :], bank[6 + k].rearrange("p (t e) -> p t e", e=E1), ALU.add)
            link(last)
            link(dve.tensor_tensor(slot, slot, base1.unsqueeze(1).broadcast_to([P, TILES, E1]), ALU.add))
            link(dve.tensor_scalar(slot, slot, -1.0, KEY, ALU.mult, ALU.add))
            link(dve.tensor_tensor(key, slot, M, ALU.mult))
            for t in range(TILES):
                last = dve.max(etop[:, t, :], key[:, t, :])
            link(last)
            dve.tensor_scalar(slots[:, :, :], etop[:, :, :], -1.0, KEY, ALU.mult, ALU.add).then_inc(slots_ready, 1)
            for c in range(2):
                link(dve.tensor_scalar(cmp8[:, c, :], endt, jcol[:, c:c + 1], None, ALU.is_le))
                link(dve.tensor_reduce(exp_of[:, c:c + 1], cmp8[:, c, :], X, ALU.add))
            dve.tensor_scalar(exp_of[:, :], exp_of[:, :], float(E1 - 1), None, ALU.min).then_inc(exp_ready, 1)
            for t in range(TILES):
                link(dve.tensor_tensor(cmp8, key[:, t, :].unsqueeze(1).broadcast_to([P, 8, E1]),
                                       etop[:, t, :].unsqueeze(2).broadcast_to([P, 8, E1]), ALU.is_equal))
                link(dve.tensor_tensor(cmp8b, cmp8, rw[:, t, :].unsqueeze(1).broadcast_to([P, 8, E1]), ALU.mult))
                link(dve.tensor_reduce(w8[:, t, :], cmp8b, X, ALU.add))
            dve.wait_ge(etab_psum, 1)
            dve.tensor_copy(etab[:, :], bank[0][0:1, 0:2 * P]).then_inc(etab_ready, 1)
            dve.memset(rec[:, :, 0:1], 0.0).then_inc(w8_ready, 1)
            dve.memset(rec[:, :, 1:2], 0.0).then_inc(my_ready, 1)
            dve.memset(rec[:, :, 2:3], 0.0).then_inc(att_free, 1)

            dve.memset(nmr, 0.0).then_inc(pair_free, 2)
            with dve.Fori(0, HEADS // 2) as hp:
                for k in range(4):
                    for q in range(QT):
                        n = 32 * hp + 8 * k + q
                        dve.wait_ge(sq_psum, n + 1)
                        dve.tensor_reduce(nm[:, bass.ds(4 * hp + k, 1), q:q + 1], psum[:, 1024 * (q % 2):1024 * (q % 2) + 1024].rearrange("p (a n) -> p a n", a=1),
                                          X, ALU.max, negate=True).then_inc(pair_free, 1)
            dve.wait_ge(nmT_psum, 1)
            nps = bank[0][:, 0:2 * P].rearrange("p (c n) -> p c n", c=2)
            dve.tensor_copy(nmT[0][:, :, :], nps).then_inc(nmT_ready, 1)
            dve.wait_ge(nmT_ready, 1)
            link(dve.tensor_tensor(nmr, nps, nmT[0][:, :, :], ALU.subtract))
            dve.tensor_copy(nmT[1][:, :, :], nmr).then_inc(nmT_ready, 1)
            dve.wait_ge(nmT_ready, 2)
            dve.tensor_tensor(nmT[2][:, :, :], nmr, nmT[1][:, :, :], ALU.subtract).then_inc(nmT_ready, 1)

            def x_copy(j, k2):
                dve.wait_ge(mxT_psum, j + 1)
                dve.tensor_copy(m_xT[:, k2, :], bank[5][:, 0:P]).then_inc(mxT_ready, 1)

            def gated(j, k2):
                g, uu = bank[6][:, 0:I1], bank[6][:, I1:2 * I1]
                dve.wait_ge(mth_ready, j + 1)
                dve.scalar_tensor_tensor(m_a[:, k2, :], m_th[:, k2, :], 1.0, g, ALU.add, ALU.mult).then_inc(ma_step, 1)
                dve.wait_ge(ma_step, j + 1)
                dve.tensor_tensor(m_b[:, k2, :], m_a[:, k2, :], uu, ALU.mult).then_inc(ma_ready, 1)

            def a_copy(k2):
                dve.tensor_copy(m_aT[0:I1, k2, :], bank[7][0:I1, 0:P]).then_inc(maT_ready, 1)

            x_copy(0, 0)
            x_copy(1, 1)
            gated(0, 0)
            x_copy(2, 0)
            gated(1, 1)
            dve.wait_ge(maT_psum, 1)
            a_copy(0)
            with dve.Fori(0, HEADS // 2) as hp:
                for k in range(4):
                    u = 4 * hp + k
                    for g in range(6):
                        i = 6 * k + g
                        j = 24 * hp + i
                        dve.wait_ge(mgu_psum, j + 2)
                        x_copy(j + 3, (i + 3) % 2)
                        dve.wait_ge(maT_psum, j + 1)
                        gated(j + 2, i % 2)
                        dve.wait_ge(my_psum, j + 1)
                        a_copy((i + 1) % 2)
                        dve.wait_ge(my_out[i % 4], 16 * (6 * hp + i // 4 + 1))
                        dve.tensor_copy(m_y[:, i % 4, :], bank[7][:, 256:256 + P]).then_inc(my_ready, 1)
                    dve.wait_ge(p_free, 2 + 8 * (u + 1))
                    dve.tensor_copy(sums[:, :, :], bank[4][:, 0:QT * 16].rearrange("p (q d) -> p q d", d=16)[:, :, 0:HD + 1]).then_inc(att_free, 1)
                    dve.wait_ge(att_free, u + 2)
                    dve.reciprocal(rec[:, 0, :].unsqueeze(2), sums[:, :, HD:HD + 1]).then_inc(rec_ready, 1)
                    dve.wait_ge(rec_ready, u + 1)
                    dve.tensor_tensor(att[:, (k % 2) * QT:(k % 2 + 1) * QT, bass.ds((2 * hp + k // 2) * HD, HD)], sums[:, :, 0:HD],
                                      rec[:, 0, :].unsqueeze(2).broadcast_to([P, QT, HD]), ALU.mult).then_inc(att_ready, 1)
            for g in range(TILES // TB):
                dve.wait_ge(fin_psum, g + 1)
                dve.tensor_tensor(resid[:, g * TB:(g + 1) * TB, :], resid[:, g * TB:(g + 1) * TB, :], bank[2 + g].rearrange("p (t d) -> p t d", t=TB), ALU.add).then_inc(routed_added, 1)
            steps_out = [TILES // TB]
            for t in range(TILES):
                dve.wait_ge(y_in[t % 2], 16 * TOPK * (t // 2 + 1))
                for k in range(TOPK):
                    dve.wait_ge(routed_added, TILES // TB + t * (TOPK - 1) + k) if k else dve.wait_ge(routed_added, TILES // TB)
                    last = dve.scalar_tensor_tensor(resid[:, t, :], ybuf[:, t % 2, k, :], w8[:, t, k:k + 1], resid[:, t, :], ALU.mult, ALU.add)
                    if k < TOPK - 1:
                        last.then_inc(routed_added, 1)
                last.then_inc(y_used, 1)


def kernel(**inputs):
    import concourse.bacc as bacc
    from concourse.bass_utils import run_bass_kernel_spmd
    import ml_dtypes

    def t(a):
        return np.ascontiguousarray(a)

    i = {k: np.asarray(v) for k, v in inputs.items()}

    def halves(a):
        return a.reshape(HALVES, P, STATES).transpose(1, 0, 2).reshape(P, CH)

    gu = [np.concatenate([i["L0_ffn_sh_gate"], i["L0_ffn_sh_up"]], 1)] + \
         [np.concatenate([i["L0_ffn_rt_gate"][e], i["L0_ffn_rt_up"][e]], 1) for e in range(E0)]
    dn = [i["L0_ffn_sh_down"]] + [i["L0_ffn_rt_down"][e] for e in range(E0)]
    arrays = {
        "x": i["L0_attn_x"].reshape(TOK, DIM),
        "ident": np.eye(P, dtype=np.float32),
        "iota8": np.tile(np.arange(8, dtype=np.float32), (P, 1)),
        "lnwb": np.stack([i["L0_attn_ln_w"], i["L0_attn_ln_b"]], 1),
        "w_gate0": i["L0_ffn_gate_w"],
        "abc": np.stack([halves(i["L0_attn_A_log"]), halves(i["L0_attn_B_mat"]), halves(i["L0_attn_C_mat"])], 1),
        "w_in": i["L0_attn_in_proj_w"].T,
        "w_out": i["L0_attn_out_proj_w"].T.reshape(2, P, DIM).transpose(1, 0, 2),
        "w_gu0": np.stack(gu),
        "w_dn0": np.stack([d.reshape(2, P, DIM).transpose(1, 0, 2) for d in dn]),
    }
    table = i["L1_attn_bias_table"]
    rows = np.arange(P)
    q_major = np.clip(rows[:, None, None] + P * np.arange(2)[None, :, None] - (np.arange(CORNER) + LEN - CORNER)[None, None, :] + LEN - 1, 0, BIASED)
    k_major = np.clip(np.arange(CORNER)[None, None, :] - (rows[:, None, None] + P * np.arange(2)[None, :, None] + LEN - CORNER) + LEN - 1, 0, BIASED)

    def corners(index):
        flat = np.concatenate([index.reshape(P, 2 * CORNER), np.full((P, 1), BIASED)], 1)
        return table.T[:, flat]

    ck = corners(k_major)
    arrays.update({
        "small": np.concatenate([i["L1_attn_bq"][:, None], i["L1_attn_bk"][:, None], np.tile(i["L1_attn_temperature"], (P, 1)),
                                 rows[:, None].astype(np.float32), rows[:, None].astype(np.float32) + P,
                                 np.tile(table[BIASED], (P, 1))], 1),
        "w_q": i["L1_attn_Wq"], "w_k": i["L1_attn_Wk"], "w_v": i["L1_attn_Wv"], "w_p": i["L1_attn_Wp"],
        "bv_t": np.tile(i["L1_attn_bv"], (P, 1)), "bp_t": np.tile(i["L1_attn_bp"], (P, 1)),
        "strict": np.triu(np.ones((P, P), np.float32), 1), "ones": np.ones((P, P), np.float32),
        "w_gate1": i["L1_ffn_gate_w"].T, "gbias": np.tile(i["L1_ffn_gate_bias"], (P, 1)),
        "w_sh": np.concatenate([i["L1_ffn_Sg"].T, i["L1_ffn_Su"].T], 1),
        "w_shd": i["L1_ffn_Sd"].T.reshape(2, I1, DIM).transpose(1, 0, 2),
        "w_gu1": np.concatenate([i["L1_ffn_Wg"].transpose(0, 2, 1), i["L1_ffn_Wu"].transpose(0, 2, 1)], 2),
        "w_dn1": i["L1_ffn_Wd"].transpose(0, 2, 1),
        "corners": np.concatenate([corners(q_major), ck, ck[-2:]]),
        "fill_q": np.zeros((16, UNITS * LEN), ml_dtypes.bfloat16),
        "fill_unit": np.zeros((KROWS, LEN), ml_dtypes.bfloat16),
        "fill_k": np.concatenate([np.ones((3, UNITS * LEN)), np.zeros((13, UNITS * LEN))]).astype(ml_dtypes.bfloat16),
    })
    arrays = {k: t(v) for k, v in arrays.items()}
    nc = bacc.Bacc("TRN2", target_bir_lowering=False, num_devices=1)
    A = {k: nc.dram_tensor("in_" + k, v.shape, mybir.dt.from_np(v.dtype), kind="ExternalInput").ap() for k, v in arrays.items()}
    A["out"] = nc.dram_tensor("out", (TOK, DIM), F32, kind="ExternalOutput").ap()
    build(nc, A)
    r = run_bass_kernel_spmd(nc, [{"in_" + k: v for k, v in arrays.items()}], core_ids=[0])
    return r.results[0]["out"].reshape(BATCH, LEN, DIM)
```

```python
import concourse.bass as bass
from concourse import mybir
from contextlib import ExitStack
import numpy as np

F32 = mybir.dt.float32
BF16 = mybir.dt.bfloat16
U32 = mybir.dt.uint32
ALU = mybir.AluOpType
ACT = mybir.ActivationFunctionType
X = mybir.AxisListType.X

P = 128
BATCH, LEN, DIM = 2, 1024, 128
TOK = BATCH * LEN
TILES = TOK // P
EPS = 1e-5

HALVES, STATES = 2, 16
SEG = 128
SEGS = TOK // SEG
WARM = 24
WIN = 8
WINDOWS = (SEG + WARM) // WIN
WARM_WINDOWS = WARM // WIN
CH = HALVES * STATES
COL = CH * SEGS
PADSEG = SEG + 2 * WARM
H_MAX = 10.0

E0, I0 = 8, 256
CHUNK = 512
CHUNKS = TOK // CHUNK
CT = CHUNK // P

HEADS, HD = 16, 8
QT = LEN // P
UNITS = HEADS * BATCH
PARTS_Q = (0, 0, 1, 1, 0, 2)
PARTS_K = (0, 1, 0, 1, 2, 0)
KROWS = 65
MAXROW = 8 * len(PARTS_Q)
BIASED = 248
CORNER = 2 * P

E1, I1, TOPK, GROUPS, TOPG = 64, 88, 8, 8, 4
MT = TOK * TOPK // P + E1
TURNS = HEADS // 2
FREE_TURNS = 3
TURN = 8
assert MT == 2 * TURN * (2 * TURNS - FREE_TURNS - 1)
SLOTS = MT + 8
KEY = 32768.0


def build(nc, A):
    ctx = ExitStack()
    with ctx:
        def sb(name, shape, dt=F32):
            return ctx.enter_context(nc.sbuf_tensor(name, shape, dt))

        def sem(name):
            return ctx.enter_context(nc.semaphore(name))

        ident = sb("ident", [P, P])
        iota8 = sb("iota8", [P, 8])
        lnwb = sb("lnwb", [P, 2])
        w_gate0 = sb("w_gate0", [P, E0])
        resid = sb("resid", [P, TILES, DIM])
        xnT = sb("xnT", [P, TOK])
        xsT = sb("xsT", [P, TOK])
        arena = sb("arena", [P, 34304])
        cursor = [0]

        def carve(n):
            cursor[0] += n
            assert cursor[0] <= 34304
            return arena[:, cursor[0] - n:cursor[0]]

        scan_flat = [carve(WIN * COL) for _ in range(4)]
        scan_f = [s.rearrange("p (m c) -> p m c", m=WIN) for s in scan_flat[:2]]
        scan_b = [s.rearrange("p (m c) -> p m c", m=WIN) for s in scan_flat[2:]]
        diagC = carve(CH * P).rearrange("p (c n) -> p c n", c=CH)
        xssm = carve(HALVES * SEGS * PADSEG).rearrange("p (h s m) -> p h s m", h=HALVES, s=SEGS)
        sgate = carve(HALVES * TOK).rearrange("p (h t) -> p h t", h=HALVES)
        y_flat = carve(HALVES * TOK)
        y = y_flat.rearrange("p (h t) -> p h t", h=HALVES)
        xn = y_flat[:, 0:TOK].rearrange("p (t d) -> p t d", t=TILES)
        xaT = y_flat[:, TOK:2 * TOK]
        xa = scan_flat[0][:, 0:TOK].rearrange("p (t d) -> p t d", t=TILES)
        sq = scan_flat[1][:, 0:TOK].rearrange("p (t d) -> p t d", t=TILES)
        xs = scan_flat[0][:, TOK:2 * TOK].rearrange("p (t d) -> p t d", t=TILES)
        w_in = scan_flat[2][:, 0:2 * HALVES * P]
        zeros = sb("zeros", [P, COL])
        ABC = sb("ABC", [P, 3, CH])
        decay = sb("decay", [P, 1])
        w_gu = sb("w_gu", [P, 2 * I0])
        w_dn = sb("w_dn", [P, 2, DIM])
        w_out = sb("w_out", [P, 2, DIM])
        silu_g = sb("silu_g", [P, 2, CHUNK])
        up = sb("up", [P, 2, CHUNK])
        act = sb("act", [P, 2, CHUNK])
        stat = sb("stat", [P, 4, TILES])
        logit = sb("logit", [P, TILES, E0])
        top = sb("top", [P, TILES, 8])
        topi = sb("topi", [P, TILES, 8], U32)
        topf = sb("topf", [P, TILES, 1])
        score = sb("score", [P, TILES])
        onehot = sb("onehot", [P, TILES, E0])

        U32W = LEN // 2
        Qs = arena[:, 0:UNITS * U32W].bitcast(BF16)
        Ks = arena[:, UNITS * U32W:2 * UNITS * U32W].bitcast(BF16)
        cursor[0] = 0
        w_q, w_k, w_v, bv_t, strict, ones, bp_t = (carve(P) for _ in range(7))
        w_gate1, gbias = carve(E1), carve(E1)
        w_sh = carve(4 * I1)
        w_shd = carve(2 * DIM).rearrange("p (k d) -> p k d", k=2)
        TE = TILES * E1

        def table():
            return carve(TE).rearrange("p (t e) -> p t e", t=TILES)

        sc1, sfc, masked, repl, M, rw, carry, slot, key = (table() for _ in range(9))
        net = [carve(TE // 2) for _ in range(3)]
        cmp8 = carve(8 * E1).rearrange("p (k e) -> p k e", k=8)
        cmp8b = carve(8 * E1).rearrange("p (k e) -> p k e", k=8)
        ones64 = carve(E1)
        nt, endt, base1 = carve(E1), carve(E1), carve(E1)
        qf, kf = carve(TOK), carve(TOK)
        parts = [carve(TOK // 2).bitcast(BF16) for _ in range(6)]
        sq1 = carve(TOK).rearrange("p (t d) -> p t d", t=TILES)
        xn1 = xsT[:, :].rearrange("p (t d) -> p t d", t=TILES)
        xn1T = xnT
        att = xnT[:, :].rearrange("p (t d) -> p t d", t=TILES)
        attT = xsT
        w_p = sb("w_p", [P, P])
        small = sb("small", [P, 32])
        bq, bk, temp, jcol, blast = small[:, 0:1], small[:, 1:2], small[:, 2:3], small[:, 3:5], small[:, 5:21]
        inv, bqi, zero = small[:, 21:22], small[:, 22:23], small[:, 23:24]
        gs, gtop, gidx, gidxf = logit, top, topi, onehot
        gmask = carve(TILES * 8).rearrange("p (t g) -> p t g", t=TILES)
        etop = sb("etop", [P, TILES, 8])
        den1 = sb("den1", [P, TILES])
        slots = sb("slots", [P, TILES, TOPK], U32)
        w8 = sb("w8", [P, TILES, TOPK])
        ntu = sb("ntu", [P, E1], U32)
        exp_of = sb("exp_of", [P, 2])
        etab = sb("etab", [1, 2 * P], U32)
        V = sb("V", [P, TILES, HEADS, HD + 1])
        nm = sb("nm", [P, UNITS, QT])
        nmT = [sb(f"nmT{k}", [P, 2, P], BF16) for k in range(3)]
        nmr = xnT[:, 0:2 * P].rearrange("p (c n) -> p c n", c=2)
        rec = sb("rec", [P, QT, 4])
        corner_f = sb("corner_f", [P, 2, 2 * CORNER + 1])
        corner_p = sb("corner_p", [P, 2, 3, 2 * CORNER], BF16)
        identb = sb("identb", [P, P], BF16)
        Pt = [silu_g, up]
        PW = 2 * P
        m_x, m_y = (act[:, k, :].rearrange("p (b a d) -> p b a d", b=2, a=2) for k in range(2))
        m_gu = sb("m_gu", [P, 2, 2, 2 * I1])
        m_dn = w_gu[:, :].rearrange("p (b a d) -> p b a d", b=2, a=2)
        m_xT = [w[:, :, :].rearrange("p a n -> p (a n)") for w in (w_dn, w_out)]
        m_th = zeros[:, :].rearrange("p (b n) -> p b n", b=2)
        tail = arena[:, 2 * UNITS * U32W:34304]
        m_u = tail[:, 0:2 * PW].rearrange("p (b n) -> p b n", b=2)
        m_h = tail[:, 4 * PW:6 * PW].rearrange("p (b n) -> p b n", b=2)
        ybuf = [tail[:, 0:TOPK * DIM].rearrange("p (k d) -> p k d", k=TOPK),
                act[:, :, :].rearrange("p a n -> p (a n)").rearrange("p (k d) -> p k d", k=TOPK)]
        OT = xsT[:, 0:LEN]
        Vh = [xsT[:, LEN + 144 * k:LEN + 144 * (k + 1)].rearrange("p (t d) -> p t d", t=TILES) for k in range(2)]
        d_parts = nc.dram_tensor("d_parts", (6, P, TOK), BF16).ap()
        d_nm = nc.dram_tensor("d_nm", (3, 2, P, P), BF16).ap()
        d_xs = nc.dram_tensor("d_xs", (SLOTS * P, DIM), F32).ap()
        d_ys = nc.dram_tensor("d_ys", (MT * P, DIM), F32).ap()

        psum = ctx.enter_context(nc.psum_tensor("psum", [P, 8 * 512], F32))
        bank = [psum[:, i * 512:(i + 1) * 512] for i in range(8)]

        s_x = sem("s_x"); s_const = sem("s_const"); s_w = sem("s_w")
        ln_step = sem("ln_step")
        var_ready = sem("var_ready"); std_ready = sem("std_ready")
        xn_ready = sem("xn_ready"); xnT_psum = sem("xnT_psum"); xnT_ready = sem("xnT_ready")
        xa_ready = sem("xa_ready"); xaT_psum = sem("xaT_psum"); xaT_ready = sem("xaT_ready")
        xs_ready = sem("xs_ready"); xsT_psum = sem("xsT_psum"); xsT_ready = sem("xsT_ready")
        logit_psum = sem("logit_psum"); logit_ready = sem("logit_ready")
        score_ready = sem("score_ready"); onehot_ready = sem("onehot_ready")
        proj_psum = sem("proj_psum"); proj_evac = sem("proj_evac")
        a_exp = sem("a_exp"); scan_consts = sem("scan_consts")
        pads = sem("pads"); halo = sem("halo"); zeros_ready = sem("zeros_ready")
        uf_ready = sem("uf_ready"); ub_ready = sem("ub_ready")
        f_step = sem("f_step"); b_step = sem("b_step")
        window_read = sem("window_read")
        y_added = sem("y_added")
        gu_psum = sem("gu_psum"); gu_evac = sem("gu_evac"); act_ready = sem("act_ready")
        dn_psum = sem("dn_psum"); dn_added = sem("dn_added")
        wgu_in = sem("wgu_in"); wdn_in = sem("wdn_in")
        o_ready = sem("o_ready"); out_psum = sem("out_psum"); x1_ready = sem("x1_ready")
        s_out = sem("s_out")
        logit_max = sem("logit_max")
        corner_idb = sem("corner_idb"); v_ones = sem("v_ones")
        l1_w = sem("l1_w"); l1_p = sem("l1_p"); xs_zero = sem("xs_zero")
        xn1_ready = sem("xn1_ready"); xn1T_psum = sem("xn1T_psum"); xn1T_ready = sem("xn1T_ready")
        lg1_psum = sem("lg1_psum"); sc1_ready = sem("sc1_ready"); inv_ready = sem("inv_ready")
        qk_psum = sem("qk_psum"); qk_ready = sem("qk_ready"); v_psum = sem("v_psum"); v_ready = sem("v_ready")
        part_ready = sem("part_ready"); rest_step = sem("rest_step"); parts_out = sem("parts_out"); stacked = sem("stacked")
        mask_ready = sem("mask_ready"); rank_psum = sem("rank_psum"); slots_ready = sem("slots_ready")
        exp_ready = sem("exp_ready"); etab_psum = sem("etab_psum"); etab_ready = sem("etab_ready"); w8_ready = sem("w8_ready")
        scattered = sem("scattered"); bp_added = sem("bp_added")
        sgu_psum = sem("sgu_psum"); sgu_evac = sem("sgu_evac"); sact_ready = sem("sact_ready")
        sdn_psum = sem("sdn_psum"); sdn_added = sem("sdn_added")
        corner_in = [sem(f"corner_in{k}") for k in range(2)]; corner_step = sem("corner_step")
        sq_psum = sem("sq_psum"); max_ready = sem("max_ready"); nmT_psum = sem("nmT_psum"); nmT_ready = sem("nmT_ready")
        nm_out = sem("nm_out"); nm_in = sem("nm_in")
        st_psum = sem("st_psum"); p_ready = sem("p_ready"); p_free = sem("p_free"); pair_free = sem("pair_free"); att_ready = sem("att_ready")
        acc_free = sem("acc_free"); v_head = sem("v_head"); OT_psum = sem("OT_psum")
        rec_ready = sem("rec_ready")
        mx_in, mgu_in, mdn_in = ([sem(f"{n}_in{k}") for k in range(2)] for n in ("mx", "mgu", "mdn")); mxT_psum = sem("mxT_psum"); mxT_ready = sem("mxT_ready"); mgu_psum = sem("mgu_psum"); mth_ready = sem("mth_ready")
        ma_step = sem("ma_step"); ma_ready = sem("ma_ready")
        my_psum = sem("my_psum"); my_ready = sem("my_ready"); my_out = [sem(f"my_out{k}") for k in range(2)]
        y_in = [sem(f"y_in{k}") for k in range(2)]; y_used = sem("y_used"); fin_ready = sem("fin_ready"); attT_psum = sem("attT_psum"); attT_ready = sem("attT_ready")
        fin_psum = sem("fin_psum")

        block = ctx.enter_context(nc.Block())
        U = STATES * 2
        TB = 4

        @block.sync
        def _(sp):
            for k in range(4):
                sp.dma_start(resid[:, 4 * k:4 * k + 4, :], A["x"][4 * k * P:4 * (k + 1) * P].rearrange("(t p) d -> p t d", p=P)).then_inc(s_x, 16)
            for dst, name in ((ident, "ident"), (iota8, "iota8"), (lnwb, "lnwb"), (w_gate0, "w_gate0")):
                sp.dma_start(dst[:, :], A[name]).then_inc(s_const, 16)
            sp.dma_start(ABC[:, :, :], A["abc"]).then_inc(s_const, 16)
            sp.dma_start(small[:, 0:21], A["small"]).then_inc(s_const, 16)
            sp.dma_start(w_in, A["w_in"]).then_inc(s_w, 16)
            sp.dma_start(w_out[:, :, :], A["w_out"]).then_inc(s_w, 16)
            sp.dma_start(w_gu[:, :], A["w_gu0"][0]).then_inc(wgu_in, 16)
            sp.dma_start(w_dn[:, :, :], A["w_dn0"][0]).then_inc(wdn_in, 16)
            sp.wait_ge(zeros_ready, 1)
            with sp.Fori(0, SLOTS // 4) as z:
                sp.dma_start(d_xs[bass.ds(z * 4 * P, 4 * P)].rearrange("(p r) d -> p (r d)", p=P), zeros[:, :]).then_inc(xs_zero, 16)
            with sp.Fori(0, E0) as e:
                sp.wait_ge(gu_psum, 2 * CHUNKS * (e + 1))
                sp.dma_start(w_gu[:, :], A["w_gu0"][bass.ds(e + 1, 1)].rearrange("a p n -> p (a n)")).then_inc(wgu_in, 16)
                sp.wait_ge(dn_psum, CHUNKS * (e + 1))
                sp.dma_start(w_dn[:, :, :], A["w_dn0"][bass.ds(e + 1, 1)].rearrange("a p k n -> p (a k) n")).then_inc(wdn_in, 16)
            sp.wait_ge(window_read, 2 * E0 + 1)
            sp.wait_ge(uf_ready, 2 * (WINDOWS + 1))
            sp.wait_ge(ub_ready, 2 * (WINDOWS + 1))
            for dst, name in ((w_q, "w_q"), (w_k, "w_k"), (w_v, "w_v"), (bv_t, "bv_t"), (strict, "strict"), (ones, "ones"),
                              (w_gate1, "w_gate1"), (gbias, "gbias"), (w_sh, "w_sh")):
                sp.dma_start(dst, A[name]).then_inc(l1_w, 16)
            sp.dma_start(w_shd[0:I1, :, :], A["w_shd"]).then_inc(l1_w, 16)
            sp.dma_start(w_p[:, :], A["w_p"]).then_inc(l1_p, 16)
            sp.dma_start(bp_t, A["bp_t"]).then_inc(l1_p, 16)
            for k, (done, count) in {0: (part_ready, 1), 3: (part_ready, 2), 1: (part_ready, 3), 4: (part_ready, 4),
                                     2: (rest_step, 3), 5: (rest_step, 4)}.items():
                sp.wait_ge(done, count)
                sp.dma_start(d_parts[k], parts[k]).then_inc(parts_out, 16)
            sp.wait_ge(parts_out, 96)
            sp.wait_ge(w8_ready, 1)
            sp.wait_ge(sdn_psum, CHUNKS)
            sp.wait_ge(v_psum, 4)
            for side, (stack, groups) in enumerate(((Qs, PARTS_Q), (Ks, PARTS_K))):
                for g, part in enumerate(groups):
                    sp.dma_start(stack[8 * g:8 * g + 8, 0:UNITS * LEN].rearrange("d (h n) -> d h n", h=HEADS),
                                 d_parts[3 * side + part].rearrange("(h d) n -> d h n", d=HD)).then_inc(stacked, 16)
            sp.dma_start(Qs[MAXROW:64, 0:UNITS * LEN], A["fill_q"][0:16]).then_inc(stacked, 16)
            sp.dma_start(Qs[64:65, 0:UNITS * LEN], A["fill_q"][15:16]).then_inc(stacked, 16)
            sp.dma_start(Ks[MAXROW:64, 0:UNITS * LEN], A["fill_k"][0:16]).then_inc(stacked, 16)
            sp.dma_start(Ks[64:65, 0:UNITS * LEN], A["fill_k"][15:16]).then_inc(stacked, 16)

            def load_corner(n, buf):
                sp.dma_start(corner_f[:, buf, :], A["corners"][bass.ds(n, 1)].rearrange("a p n -> p (a n)")).then_inc(corner_in[buf], 16)

            for k in range(2):
                load_corner(k, k)
            def next_corner(n, buf):
                sp.wait_ge(corner_step, 6 * (n + 1))
                load_corner(n + 2, buf)

            with sp.Fori(0, FREE_TURNS) as hp:
                for k in range(2):
                    next_corner(2 * hp + k, k)

            def expert(j):
                return bass.ds(sp.value_load(etab[0:1, bass.ds(j, 1)], min_val=0, max_val=E1 - 1), 1)

            def load_x(j, buf):
                sp.dma_start(m_x[:, buf, :, :], d_xs[bass.ds(j * PW, PW)].rearrange("(a p) d -> p a d", a=2)).then_inc(mx_in[buf], 16)

            def load_gu(experts, buf):
                for a in range(2):
                    sp.dma_start(m_gu[:, buf, a, :], A["w_gu1"][experts[a]].rearrange("a p n -> p (a n)")).then_inc(mgu_in[buf], 16)

            def load_dn(experts, buf):
                for a in range(2):
                    sp.dma_start(m_dn[0:I1, buf, a, :], A["w_dn1"][experts[a]].rearrange("a p n -> p (a n)")).then_inc(mdn_in[buf], 16)

            def experts(j):
                return [expert(2 * j + a) for a in range(2)]

            def pair_loads(it, i):
                j = TURN * it + i
                e_gu, e_dn = experts(j + 3), experts(j + 2)
                sp.wait_ge(mxT_psum, j + 3)
                load_x(j + 4, i % 2)
                sp.wait_ge(mgu_psum, j + 2)
                load_gu(e_gu, (i + 1) % 2)
                sp.wait_ge(my_psum, j + 1)
                load_dn(e_dn, i % 2)
                sp.wait_ge(my_ready, j + 2)
                sp.dma_start(d_ys[bass.ds(j * PW, PW)].rearrange("(a p) d -> p a d", a=2), m_y[:, i % 2, :, :]).then_inc(my_out[i % 2], 16)

            sp.wait_ge(etab_ready, 1)
            for j in range(2):
                load_dn(experts(j), j)
                load_gu(experts(j), j)
            sp.wait_ge(scattered, 16 * TILES * TOPK)
            sp.wait_ge(sdn_psum, CHUNKS)
            load_x(0, 0)
            load_x(1, 1)
            sp.wait_ge(mxT_psum, 1)
            load_x(2, 0)
            sp.wait_ge(mxT_psum, 2)
            load_x(3, 1)
            e2 = experts(2)
            sp.wait_ge(mgu_psum, 1)
            load_gu(e2, 0)
            with sp.Fori(0, TURNS - FREE_TURNS) as it:
                for i in range(TURN):
                    if i % 4 == 0:
                        next_corner(2 * it + 2 * FREE_TURNS + i // 4, i // 4)
                    pair_loads(it, i)
            for k in range(3):
                sp.wait_ge(nmT_ready, k + 1)
                sp.dma_start(d_nm[k].rearrange("c p n -> p c n"), nmT[k][:, :, :]).then_inc(nm_out, 16)
            sp.wait_ge(nm_out, 48)
            sp.dma_start(Qs[MAXROW:MAXROW + 3, 0:UNITS * LEN], d_nm.rearrange("k c p n -> k (c p n)")).then_inc(nm_in, 16)
            with sp.Fori(TURNS - FREE_TURNS, MT // 2 // TURN) as it:
                for i in range(TURN):
                    if i % 4 == 0:
                        next_corner(2 * it + 2 * FREE_TURNS + i // 4, i // 4)
                    pair_loads(it, i)
            for k in range(4):
                sp.wait_ge(y_used, 4 * k + 4)
                sp.wait_ge(fin_ready, k + 1)
                sp.dma_start(A["out"][4 * k * P:4 * (k + 1) * P].rearrange("(t p) d -> p t d", p=P), resid[:, 4 * k:4 * k + 4, :]).then_inc(s_out, 16)
            sp.wait_ge(s_out, 64)
            for k in range(2):
                sp.wait_ge(mx_in[k], 16 * (MT // 4 + 2))
                sp.wait_ge(mgu_in[k], 32 * (MT // 4 + 2 - k))
                sp.wait_ge(mdn_in[k], 32 * (MT // 4 + 1))

        @block.gpsimd
        def _(pool):
            pool.memset(zeros[:, :], 0.0).then_inc(zeros_ready, 1)
            pool.memset(xssm[:, :, 0:1, 0:WARM], 0.0).then_inc(window_read, 1)
            pool.memset(xssm[:, :, SEGS // 2:SEGS // 2 + 1, 0:WARM], 0.0)
            pool.memset(xssm[:, :, SEGS // 2 - 1:SEGS // 2, WARM + SEG:PADSEG], 0.0)
            pool.memset(xssm[:, :, SEGS - 1:SEGS, WARM + SEG:PADSEG], 0.0).then_inc(pads, 1)
            for h in range(HALVES):
                pool.wait_ge(proj_evac, CHUNKS * (h + 1))
                for b in range(BATCH):
                    s0, s1 = b * SEGS // 2, (b + 1) * SEGS // 2
                    pool.tensor_copy(xssm[:, h, s0 + 1:s1, 0:WARM], xssm[:, h, s0:s1 - 1, SEG:SEG + WARM]).then_inc(halo, 1)
                    pool.tensor_copy(xssm[:, h, s0:s1 - 1, WARM + SEG:PADSEG], xssm[:, h, s0 + 1:s1, WARM:2 * WARM]).then_inc(halo, 1)
            pool.wait_ge(halo, 8)
            pool.wait_ge(pads, 1)
            pool.wait_ge(s_const, 96)

            def window_inputs(w, buf, h):
                base = SEG + 2 * WARM - WIN - WIN * w
                for m in range(WIN):
                    x_in = xssm[:, h, :, bass.ds(base + m, 1)].rearrange("p s a -> p a s").broadcast_to([P, STATES, SEGS])
                    b_in = ABC[:, 1, h * STATES:(h + 1) * STATES].unsqueeze(2).broadcast_to([P, STATES, SEGS])
                    out = buf[:, m, h * STATES * SEGS:(h + 1) * STATES * SEGS].rearrange("p (d s) -> p d s", d=STATES)
                    last = pool.tensor_tensor(out, x_in, b_in, ALU.mult)
                last.then_inc(ub_ready, 1)

            def gate_mul(n):
                pool.wait_ge(gu_evac, n + 1)
                pool.tensor_tensor(act[:, :, :], silu_g[:, :, :], up[:, :, :], ALU.mult).then_inc(act_ready, 1)

            pool.wait_ge(proj_psum, 4 * CHUNKS)
            for h in range(HALVES):
                window_inputs(0, scan_b[0], h)
            for h in range(HALVES):
                window_inputs(1, scan_b[1], h)
            for c in range(CHUNKS):
                if c:
                    pool.wait_ge(dn_psum, c)
                gate_mul(c)
                pool.wait_ge(b_step, 2 * WIN * (1 + c // 2) + 1)
                window_inputs(2 + c // 2, scan_b[c // 2], c % 2)
            with pool.Fori(0, E0) as e:
                for c in range(CHUNKS):
                    i, n = c // 2, CHUNKS * (e + 1) + c
                    if c % 2 == 0:
                        pool.wait_ge(b_step, 2 * WIN * (2 * e + 3 + i) + 1)
                        pool.wait_ge(window_read, 2 * e + i + 1)
                    window_inputs(2 * e + 4 + i, scan_b[i], c % 2)
                    pool.wait_ge(dn_psum, n)
                    gate_mul(n)

            pool.tensor_copy(identb[:, :], ident[:, :]).then_inc(corner_idb, 1)
            pool.memset(V[:, :, :, HD:HD + 1], 1.0).then_inc(v_ones, 1)
            pool.memset(zero, 0.0).then_inc(v_ones, 1)
            for k in range(2):
                pool.memset(small[:, 24 + k:25 + k], 0.0).then_inc(my_out[k], 16)
            pool.wait_ge(v_ones, 2)
            pool.wait_ge(xn1_ready, 1)
            pool.wait_ge(l1_p, 32)
            pool.tensor_tensor(resid[:, :, :], resid[:, :, :], bp_t.unsqueeze(1).broadcast_to([P, TILES, DIM]), ALU.add).then_inc(bp_added, 1)

            def rest(n, out, whole, part):
                pool.wait_ge(part_ready, n)
                pool.tensor_tensor(out, whole, part, ALU.subtract).then_inc(rest_step, 1)

            rest(1, qf, qf, parts[0])
            rest(2, kf, kf, parts[3])
            for c in range(CHUNKS):
                pool.wait_ge(sgu_evac, c + 1)
                if c:
                    pool.wait_ge(sdn_psum, c)
                pool.tensor_tensor(act[0:I1, :, :], silu_g[0:I1, :, :], up[0:I1, :, :], ALU.mult).then_inc(sact_ready, 1)
            rest(3, parts[2], qf, parts[1])
            rest(4, parts[5], kf, parts[4])

            def split_corner(n, buf, loads):
                f, p = corner_f[:, buf, 0:2 * CORNER], corner_p[:, buf]
                last_row = corner_f[:, buf, 2 * CORNER:].broadcast_to([P, 2 * CORNER])
                pool.wait_ge(corner_in[buf], loads)
                pool.tensor_tensor(f, f, last_row, ALU.subtract).then_inc(corner_step, 1)
                pool.wait_ge(corner_step, 6 * n + 1)
                pool.tensor_tensor(f, f, inv.broadcast_to([P, 2 * CORNER]), ALU.mult).then_inc(corner_step, 1)
                pool.wait_ge(corner_step, 6 * n + 2)
                pool.tensor_tensor(p[:, 0, :], f, zero.broadcast_to([P, 2 * CORNER]), ALU.add).then_inc(corner_step, 1)
                pool.wait_ge(corner_step, 6 * n + 3)
                pool.tensor_tensor(f, f, p[:, 0, :], ALU.subtract).then_inc(corner_step, 1)
                pool.wait_ge(corner_step, 6 * n + 4)
                pool.tensor_tensor(p[:, 1, :], f, zero.broadcast_to([P, 2 * CORNER]), ALU.add).then_inc(corner_step, 1)
                pool.wait_ge(corner_step, 6 * n + 5)
                pool.tensor_tensor(p[:, 2, :], f, p[:, 1, :], ALU.subtract).then_inc(corner_step, 1)

            pool.wait_ge(inv_ready, 1)
            pool.wait_ge(xs_zero, 16 * (SLOTS // 4))
            pool.wait_ge(slots_ready, 1)
            rows = [(t, k) for t in range(TILES) for k in range(TOPK)]

            def dispatch(count):
                for _ in range(min(count, len(rows))):
                    t, k = rows.pop(0)
                    pool.indirect_dma_start(d_xs, bass.IndirectOffsetOnAxis(ap=slots[:, t, k:k + 1], axis=0),
                                            xn1[:, t, :], None).then_inc(scattered, 16)

            split_corner(0, 0, 16)
            split_corner(1, 1, 16)
            dispatch(24)
            for n in range(2 * FREE_TURNS):
                dispatch(21)
                pool.wait_ge(sq_psum, 8 * (2 * n + 1) + 2)
                split_corner(n + 2, n % 2, 16 * (n // 2 + 2))
            assert not rows

            def silu_mul(j, k2):
                pool.wait_ge(mth_ready, j + 1)
                pool.tensor_tensor(m_h[0:I1, k2, :], m_th[0:I1, k2, :], m_u[0:I1, k2, :], ALU.mult).then_inc(ma_ready, 1)

            silu_mul(0, 0)
            with pool.Fori(0, TURNS - FREE_TURNS) as it:
                for i in range(TURN):
                    if i % 4 == 2:
                        n = 2 * it + 2 * FREE_TURNS + i // 4
                        pool.wait_ge(sq_psum, 8 * (2 * n + 1) + 2)
                        split_corner(n + 2, i // 4, 16 * (it + FREE_TURNS + 2))
                    silu_mul(TURN * it + i + 1, (i + 1) % 2)
            with pool.Fori(0, TURNS - 1) as hp:
                for k in range(2):
                    pool.wait_ge(st_psum, 8 * (4 * hp + 2 * k + 1) + 4)
                    split_corner(HEADS + 2 * hp + k + 2, k, 16 * (HEADS // 2 + hp + 2))
            for b in range(2):
                pool.wait_ge(my_out[b], 16 * (MT // 4 + 1))
                pool.wait_ge(mx_in[b], 16 * (MT // 4 + 2))
            for t in range(TILES):
                if t >= 2:
                    pool.wait_ge(y_used, t - 1)
                for k in range(TOPK):
                    pool.indirect_dma_start(ybuf[t % 2][:, k, :], None, d_ys,
                                            bass.IndirectOffsetOnAxis(ap=slots[:, t, k:k + 1], axis=0)).then_inc(y_in[t % 2], 16)

        @block.scalar
        def _(sc):
            for k in range(2):
                sc.wait_ge(var_ready, k + 1)
                sc.activation(stat[:, 2, :], stat[:, 1, :], ACT.Sqrt).then_inc(std_ready, 1)
            for g in range(TILES // TB):
                sc.wait_ge(xnT_psum, g + 1)
                sc.activation(xnT[:, g * 512:(g + 1) * 512], bank[g % 2][:, :], ACT.Copy).then_inc(xnT_ready, 1)
            sc.wait_ge(logit_psum, 1)
            sc.activation(logit[:, :, :], bank[7][:, 0:TILES * E0], ACT.Copy).then_inc(logit_ready, 1)
            sc.wait_ge(s_const, 96)
            for g in range(TILES // TB):
                sc.wait_ge(xaT_psum, g + 1)
                sc.activation(xaT[:, g * 512:(g + 1) * 512], bank[2 + g % 2][:, :], ACT.Identity,
                              scale=lnwb[:, 0:1], bias=lnwb[:, 1:2]).then_inc(xaT_ready, 1)
            sc.wait_ge(pads, 1)
            for k in range(HALVES * CHUNKS):
                h, c = k // CHUNKS, k % CHUNKS
                sc.wait_ge(proj_psum, k + 1)
                sc.activation(xssm[:, h, CT * c:CT * c + CT, WARM:WARM + SEG],
                              bank[4 + k % 2][:, :], ACT.Copy).then_inc(proj_evac, 1)
            sc.activation(ABC[:, 0, :], ABC[:, 0, :], ACT.Exp).then_inc(a_exp, 1)
            sc.wait_ge(logit_max, 1)
            sc.activation(score[:, :], top[:, :, 0:1], ACT.Sigmoid).then_inc(score_ready, 1)
            for g in range(TILES // TB):
                sc.wait_ge(xsT_psum, g + 1)
                sc.activation(xsT[:, g * 512:(g + 1) * 512], bank[g % 2][:, :], ACT.Copy).then_inc(xsT_ready, 1)
            for k in range(HALVES * CHUNKS, 2 * HALVES * CHUNKS):
                h, c = k // CHUNKS - HALVES, k % CHUNKS
                sc.wait_ge(proj_psum, k + 1)
                sc.activation(sgate[:, h, c * CHUNK:(c + 1) * CHUNK], bank[4 + k % 2][:, :], ACT.Silu).then_inc(proj_evac, 1)
            sc.wait_ge(halo, 8)
            sc.wait_ge(proj_psum, 4 * CHUNKS)

            def window_inputs(w, buf, h):
                for ch in range(h * STATES, (h + 1) * STATES):
                    x_in = xssm[:, h, :, bass.ds(WIN * w, WIN)].rearrange("p s m -> p m s")
                    last = sc.activation(buf[:, :, ch * SEGS:(ch + 1) * SEGS], x_in, ACT.Copy, scale=ABC[:, 1, ch:ch + 1])
                last.then_inc(uf_ready, 1)

            def evac_gu(n):
                for m in range(2):
                    sc.wait_ge(gu_psum, 2 * n + m + 1)
                    sc.activation(silu_g[:, m, :], bank[m][:, :], ACT.Silu)
                    last = sc.activation(up[:, m, :], bank[2 + m][:, :], ACT.Copy)
                last.then_inc(gu_evac, 1)

            for h in range(HALVES):
                window_inputs(0, scan_f[0], h)
            for h in range(HALVES):
                window_inputs(1, scan_f[1], h)
            for c in range(CHUNKS):
                if c:
                    sc.wait_ge(act_ready, c)
                evac_gu(c)
                sc.wait_ge(f_step, 2 * WIN * (1 + c // 2) + 1)
                window_inputs(2 + c // 2, scan_f[c // 2], c % 2)
            with sc.Fori(0, E0) as e:
                for c in range(CHUNKS):
                    i, n = c // 2, CHUNKS * (e + 1) + c
                    if c % 2 == 0:
                        sc.wait_ge(f_step, 2 * WIN * (2 * e + 3 + i) + 1)
                        sc.wait_ge(window_read, 2 * e + i + 1)
                    window_inputs(2 * e + 4 + i, scan_f[i], c % 2)
                    sc.wait_ge(act_ready, n)
                    evac_gu(n)

            sc.wait_ge(var_ready, 3)
            sc.activation(stat[:, 2, :], stat[:, 1, :], ACT.Sqrt).then_inc(std_ready, 1)
            for g in range(TILES // TB):
                sc.wait_ge(xn1T_psum, g + 1)
                sc.activation(xn1T[:, g * 512:(g + 1) * 512], bank[g % 2], ACT.Copy).then_inc(xn1T_ready, 1)
            sc.wait_ge(inv_ready, 1)
            for k in range(2 * CHUNKS):
                sc.wait_ge(qk_psum, k + 1)
                c = k % CHUNKS
                out = (qf if k < CHUNKS else kf)[:, c * CHUNK:(c + 1) * CHUNK]
                if k < CHUNKS:
                    sc.activation(out, bank[2 + k % 2], ACT.Identity, scale=inv, bias=bqi).then_inc(qk_ready, 1)
                else:
                    sc.activation(out, bank[2 + k % 2], ACT.Identity, bias=bk).then_inc(qk_ready, 1)
            for k in range(2):
                sc.wait_ge(lg1_psum, k + 1)
                sc.activation(sc1[:, 8 * k:8 * k + 8, :], bank[6 + k].rearrange("p (t e) -> p t e", e=E1), ACT.Sigmoid).then_inc(sc1_ready, 1)
            sc.wait_ge(qk_ready, 2 * CHUNKS)
            sc.activation(parts[0], qf, ACT.Copy).then_inc(part_ready, 1)
            sc.activation(parts[3], kf, ACT.Copy).then_inc(part_ready, 1)
            for c in range(CHUNKS):
                if c:
                    sc.wait_ge(sact_ready, c)
                for m in range(2):
                    sc.wait_ge(sgu_psum, 2 * c + m + 1)
                    sc.activation(silu_g[0:I1, m, :], bank[m][0:I1, :], ACT.Silu)
                    last = sc.activation(up[0:I1, m, :], bank[2 + m][0:I1, :], ACT.Copy)
                last.then_inc(sgu_evac, 1)
            sc.wait_ge(rest_step, 1)
            sc.activation(parts[1], qf, ACT.Copy).then_inc(part_ready, 1)
            sc.wait_ge(rest_step, 2)
            sc.activation(parts[4], kf, ACT.Copy).then_inc(part_ready, 1)

            def x_copy(j, k2):
                sc.wait_ge(mxT_psum, j + 1)
                sc.activation(m_xT[k2], bank[5][:, 0:PW], ACT.Copy).then_inc(mxT_ready, 1)

            def silu_up(j, k2):
                sc.wait_ge(mgu_psum, j + 1)
                sc.activation(m_th[0:I1, k2, :], bank[6][0:I1, 0:PW], ACT.Silu)
                sc.activation(m_u[0:I1, k2, :], bank[6][0:I1, PW:2 * PW], ACT.Copy, scale=2.0).then_inc(mth_ready, 1)

            sc.wait_ge(stacked, 16 * 16)
            x_copy(0, 0)
            x_copy(1, 1)
            silu_up(0, 0)
            with sc.Fori(0, TURNS - FREE_TURNS) as it:
                for i in range(TURN):
                    j = TURN * it + i
                    x_copy(j + 2, i % 2)
                    silu_up(j + 1, (i + 1) % 2)
                    sc.wait_ge(my_psum, j + 1)
                    sc.wait_ge(my_out[i % 2], 16 * (TURN // 2 * it + i // 2 + 1))
                    sc.activation(m_y[:, i % 2, :, :].rearrange("p a d -> p (a d)"), bank[7][:, 0:PW], ACT.Copy).then_inc(my_ready, 1)

            sc.activation(stat[:, 0, :], stat[:, 1, :], ACT.Copy).then_inc(p_free, 2)

            def exponentials(hp, experts_too):
                for k in range(4):
                    for g in range(8):
                        G = 32 * hp + 8 * k + g
                        sc.wait_ge(st_psum, G + 1)
                        sc.wait_ge(p_free, G + 1)
                        sc.activation(Pt[g % 2][:, :, :], psum[:, 1024 * (g % 2):1024 * (g % 2) + 1024].rearrange("p (a n) -> p a n", a=2),
                                      ACT.Exp).then_inc(p_ready, 1)
                        if experts_too and g % 4 == 1:
                            i = 2 * k + g // 4
                            sc.wait_ge(mgu_psum, TURN * (hp + TURNS - FREE_TURNS) + i + 2)
                            sc.activation(m_th[0:I1, (i + 1) % 2, :], bank[6][0:I1, 0:PW], ACT.Tanh, scale=0.5).then_inc(mth_ready, 1)

            with sc.Fori(0, TURNS - 1) as hp:
                exponentials(hp, True)
            exponentials(TURNS - 1, False)
            for g in range(TILES // TB):
                sc.wait_ge(attT_psum, g + 1)
                sc.activation(attT[:, g * 512:(g + 1) * 512], bank[g % 2], ACT.Copy).then_inc(attT_ready, 1)

        @block.tensor
        def _(pe):
            pe.wait_ge(s_const, 96)
            pe.wait_ge(xn_ready, 1)
            for g in range(TILES // TB):
                if g >= 2:
                    pe.wait_ge(xnT_ready, g - 1)
                for i in range(TB):
                    last = pe.transpose(bank[g % 2][:, i * P:(i + 1) * P], xn[:, g * TB + i, :], ident[:, :])
                last.then_inc(xnT_psum, 1)
            pe.wait_ge(xnT_ready, 4)
            for t in range(TILES):
                last = pe.matmul(bank[7][:, t * E0:(t + 1) * E0], xnT[:, t * P:(t + 1) * P], w_gate0[:, :], start=True, stop=True)
            last.then_inc(logit_psum, 1)
            pe.wait_ge(xa_ready, 1)
            for g in range(TILES // TB):
                if g >= 2:
                    pe.wait_ge(xaT_ready, g - 1)
                for i in range(TB):
                    last = pe.transpose(bank[2 + g % 2][:, i * P:(i + 1) * P], xa[:, g * TB + i, :], ident[:, :])
                last.then_inc(xaT_psum, 1)
            pe.wait_ge(s_w, 32)
            for k in range(2 * HALVES * CHUNKS):
                if k == HALVES * CHUNKS:
                    pe.wait_ge(xs_ready, 1)
                    for g in range(TILES // TB):
                        if g >= 2:
                            pe.wait_ge(xsT_ready, g - 1)
                        for i in range(TB):
                            last = pe.transpose(bank[g % 2][:, i * P:(i + 1) * P], xs[:, g * TB + i, :], ident[:, :])
                        last.then_inc(xsT_psum, 1)
                m, c = k // CHUNKS, k % CHUNKS
                pe.wait_ge(xaT_ready, min(c + 1, 4))
                if k >= 2:
                    pe.wait_ge(proj_evac, k - 1)
                pe.matmul(bank[4 + k % 2][:, :], w_in[:, m * P:(m + 1) * P], xaT[:, c * CHUNK:(c + 1) * CHUNK],
                          start=True, stop=True).then_inc(proj_psum, 1)

            def gate_up(src, c, n):
                pe.wait_ge(gu_evac, n) if not (isinstance(n, int) and n == 0) else None
                for m in range(2):
                    pe.matmul(bank[m][:, :], w_gu[:, m * P:(m + 1) * P], src[:, c * CHUNK:(c + 1) * CHUNK], start=True, stop=True)
                    pe.matmul(bank[2 + m][:, :], w_gu[:, I0 + m * P:I0 + (m + 1) * P], src[:, c * CHUNK:(c + 1) * CHUNK],
                              start=True, stop=True).then_inc(gu_psum, 1)

            def down(n):
                pe.wait_ge(act_ready, n + 1)
                if not (isinstance(n, int) and n == 0):
                    pe.wait_ge(dn_added, n)
                for q in range(CT):
                    for m in range(2):
                        last = pe.matmul(bank[4][:, q * P:(q + 1) * P], act[:, m, q * P:(q + 1) * P], w_dn[:, m, :],
                                         start=(m == 0), stop=(m == 1))
                last.then_inc(dn_psum, 1)

            def contract(w, i, d):
                step, scan = (f_step, scan_f) if d == 0 else (b_step, scan_b)
                pe.wait_ge(step, 2 * WIN * (w + 1))
                for h in range(HALVES):
                    for s in range(STATES):
                        ch = h * STATES + s
                        last = pe.matmul(bank[5 + i][:, (2 * d + h) * P:(2 * d + h + 1) * P], diagC[:, ch, :],
                                         scan[(3 + i) % 2][:, :, ch * SEGS:(ch + 1) * SEGS],
                                         start=(s == 0), stop=(s == STATES - 1))
                return last

            pe.wait_ge(wgu_in, 16)
            pe.wait_ge(wdn_in, 16)
            pe.wait_ge(xsT_ready, 4)
            for c in range(CHUNKS):
                gate_up(xnT, c, c)
                down(c)
            pe.wait_ge(scan_consts, 1)
            with pe.Fori(0, E0) as e:
                pe.wait_ge(wgu_in, 16 * e + 32)
                for c in range(CHUNKS):
                    gate_up(xsT, c, CHUNKS * (e + 1) + c)
                    i, d = c // 2, c % 2
                    if d == 0:
                        pe.wait_ge(y_added, 2 * e + 1)
                    last = contract(2 * e + 3 + i, i, d)
                    if d == 1:
                        last.then_inc(window_read, 1)
                    if c == 0:
                        pe.wait_ge(wdn_in, 16 * e + 32)
                    down(CHUNKS * (e + 1) + c)
            pe.wait_ge(o_ready, 1)
            pe.wait_ge(gu_evac, CHUNKS * (E0 + 1))
            for g in range(TILES // TB):
                for q in range(TB):
                    t = g * TB + q
                    for h in range(HALVES):
                        last = pe.matmul(bank[g][:, q * P:(q + 1) * P], sgate[:, h, t * P:(t + 1) * P], w_out[:, h, :],
                                         start=(h == 0), stop=(h == 1))
                last.then_inc(out_psum, 1)

            def transposes(src, dst, done, free):
                for g in range(TILES // TB):
                    if g >= 2:
                        pe.wait_ge(free, g - 1)
                    for i in range(TB):
                        last = pe.transpose(bank[g % 2][:, i * P:(i + 1) * P], src[:, g * TB + i, :], ident[:, :])
                    last.then_inc(done, 1)

            pe.wait_ge(xn1_ready, 1)
            transposes(xn1, xn1T, xn1T_psum, xn1T_ready)
            pe.wait_ge(xn1T_ready, 4)
            pe.wait_ge(l1_w, 160)
            for t in range(TILES):
                last = pe.matmul(bank[6 + t // 8][:, (t % 8) * E1:(t % 8 + 1) * E1], xn1T[:, t * P:(t + 1) * P], w_gate1, start=True, stop=True)
                if t % 8 == 7:
                    last.then_inc(lg1_psum, 1)
            for k in range(2 * CHUNKS):
                if k >= 2:
                    pe.wait_ge(qk_ready, k - 1)
                c = k % CHUNKS
                pe.matmul(bank[2 + k % 2], w_q if k < CHUNKS else w_k, xn1T[:, c * CHUNK:(c + 1) * CHUNK], start=True, stop=True).then_inc(qk_psum, 1)
            for g in range(TILES // TB):
                if g >= 2:
                    pe.wait_ge(v_ready, g - 1)
                for q in range(TB):
                    t = g * TB + q
                    last = pe.matmul(bank[4 + g % 2][:, q * P:(q + 1) * P], xn1T[:, t * P:(t + 1) * P], w_v, start=True, stop=True)
                last.then_inc(v_psum, 1)
            pe.wait_ge(qk_ready, 2 * CHUNKS)
            pe.wait_ge(v_ready, 4)
            for c in range(CHUNKS):
                if c:
                    pe.wait_ge(sgu_evac, c)
                for m in range(2):
                    pe.matmul(bank[m][0:I1, :], w_sh[:, m * I1:(m + 1) * I1], xn1T[:, c * CHUNK:(c + 1) * CHUNK], start=True, stop=True)
                    pe.matmul(bank[2 + m][0:I1, :], w_sh[:, (2 + m) * I1:(3 + m) * I1], xn1T[:, c * CHUNK:(c + 1) * CHUNK],
                              start=True, stop=True).then_inc(sgu_psum, 1)
                pe.wait_ge(sact_ready, c + 1)
                if c:
                    pe.wait_ge(sdn_added, c)
                for q in range(CT):
                    for m in range(2):
                        last = pe.matmul(bank[4][:, q * P:(q + 1) * P], act[0:I1, m, q * P:(q + 1) * P], w_shd[0:I1, m, :],
                                         start=(m == 0), stop=(m == 1))
                last.then_inc(sdn_psum, 1)
            pe.wait_ge(mask_ready, 1)
            pe.wait_ge(sgu_evac, CHUNKS)
            pe.wait_ge(sc1_ready, 2)
            for k in range(2):
                pe.matmul(bank[6 + k], strict, M[:, 8 * k:8 * k + 8, :], start=True, stop=True)
                last = pe.matmul(bank[2 + k], ones, M[:, 8 * k:8 * k + 8, :], start=True, stop=True)
            last.then_inc(rank_psum, 1)
            pe.wait_ge(exp_ready, 1)
            for c in range(2):
                last = pe.matmul(bank[0][0:1, c * P:(c + 1) * P], exp_of[:, c:c + 1], ident[:, :], start=True, stop=True)
            last.then_inc(etab_psum, 1)

            pe.wait_ge(stacked, 16 * 16)
            pe.wait_ge(corner_idb, 1)
            pe.wait_ge(etab_ready, 1)
            pe.wait_ge(slots_ready, 1)

            def x_transpose(buf, loads):
                pe.wait_ge(mx_in[buf], 16 * loads)
                for a in range(2):
                    last = pe.transpose(bank[5][:, a * P:(a + 1) * P], m_x[:, buf, a, :], ident[:, :])
                last.then_inc(mxT_psum, 1)

            def pair_gate_up(buf, loads):
                pe.wait_ge(mgu_in[buf], 32 * loads)
                for m in range(2):
                    for a in range(2):
                        last = pe.matmul(bank[6][0:I1, m * PW + a * P:m * PW + (a + 1) * P], m_gu[:, buf, a, m * I1:(m + 1) * I1],
                                         m_xT[buf][:, a * P:(a + 1) * P], start=True, stop=True)
                last.then_inc(mgu_psum, 1)

            def pair_turn(it, i):
                j = TURN * it + i
                half = TURN // 2 * it
                pe.wait_ge(mxT_ready, j + 2)
                x_transpose(i % 2, half + (i + 2) // 2 + 1)
                pe.wait_ge(ma_ready, j + 1)
                pair_gate_up((i + 1) % 2, half + (i + 1) // 2 + 1)
                pe.wait_ge(mdn_in[i % 2], 32 * (half + i // 2 + 1))
                pe.wait_ge(my_ready, j + 1)
                for a in range(2):
                    last = pe.matmul(bank[7][:, a * P:(a + 1) * P], m_h[0:I1, i % 2, a * P:(a + 1) * P], m_dn[0:I1, i % 2, a, :],
                                     start=True, stop=True)
                last.then_inc(my_psum, 1)

            def largest(hp, it):
                for k in range(4):
                    u = 4 * hp + k
                    for q in range(QT):
                        pair = bank[2 * (q % 2):2 * (q % 2) + 2]
                        pe.wait_ge(pair_free, 32 * hp + 8 * k + q + 1)
                        queries = Qs[0:KROWS, bass.ds(u * LEN + q * P, P)]
                        for a in range(2):
                            biased = a == 1 and q < 2
                            last = pe.matmul(pair[a], queries, Ks[0:KROWS, bass.ds(u * LEN + a * 512, 512)], start=True, stop=not biased)
                            if biased:
                                if k % 2 == 0 and q == 0:
                                    pe.wait_ge(corner_step, 6 * (2 * hp + k // 2 + 1))
                                for p in range(3):
                                    last = pe.matmul(pair[1][:, CORNER:], identb[:, :], corner_p[:, k // 2, p, q * CORNER:(q + 1) * CORNER],
                                                     start=False, stop=(p == 2))
                        last.then_inc(sq_psum, 1)
                        if it is not None and q % 4 == 2:
                            pair_turn(it, 2 * k + q // 4)

            with pe.Fori(0, FREE_TURNS) as hp:
                largest(hp, None)
            x_transpose(0, 1)
            pe.wait_ge(mxT_ready, 1)
            x_transpose(1, 1)
            pair_gate_up(0, 1)
            with pe.Fori(FREE_TURNS, TURNS) as hp:
                largest(hp, hp - FREE_TURNS)
            pe.wait_ge(pair_free, 2 + 8 * UNITS)
            for c in range(2):
                last = pe.transpose(bank[0][:, c * P:(c + 1) * P], nm[:, 16 * c:16 * c + 16, :].rearrange("p u q -> p (u q)"), ident[:, :])
            last.then_inc(nmT_psum, 1)

            def keys_scores(u, k, g):
                qh, kp = g // 4, g % 4
                for a in range(2):
                    kt = 2 * kp + a
                    out = bank[2 * (g % 2) + a]
                    biased = g == 3
                    last = pe.matmul(out, Ks[0:KROWS, bass.ds(u * LEN + kt * P, P)], Qs[0:KROWS, bass.ds(u * LEN + qh * 512, 512)],
                                     start=True, stop=not biased)
                    if biased:
                        for p in range(3):
                            last = pe.matmul(out[:, 0:CORNER], identb[:, :], corner_p[:, k // 2, p, a * CORNER:(a + 1) * CORNER],
                                             start=False, stop=(p == 2))
                last.then_inc(st_psum, 1)

            def attend(hp, it):
                for k in range(4):
                    u = 4 * hp + k
                    for g in range(8):
                        G = 32 * hp + 8 * k + g
                        pe.wait_ge(p_ready, G + 1)
                        if g == 1 and k % 2 == 0:
                            pe.wait_ge(corner_step, 6 * (HEADS + 2 * hp + k // 2 + 1))
                        if it is not None or k < 3 or g < 6:
                            keys_scores(u if g < 6 else u + 1, k, (g + 2) % 8)
                        if k == 0 and g == 0:
                            pe.wait_ge(att_ready, 4 * hp + 1)
                        if it is not None and g % 4 == 0:
                            pair_turn(it, 2 * k + g // 4)
                        if g == 0 and k % 2 == 0:
                            pe.wait_ge(v_head, 2 * hp + k // 2 + 1)
                        if g % 4 == 0:
                            pe.wait_ge(acc_free, 2 * u + g // 4 + 1)
                        for a in range(2):
                            kt = 2 * (g % 4) + a
                            last = pe.matmul(bank[4][0:HD + 1, :], Vh[k // 2][:, (k % 2) * QT + kt, :], Pt[g % 2][:, a, :],
                                             start=(kt == 0), stop=(kt == QT - 1))
                        last.then_inc(p_free, 1)
                pe.wait_ge(acc_free, 8 * hp + 9)
                if it is not None:
                    pe.wait_ge(mxT_ready, TURN * it + TURN + 2)
                    pe.wait_ge(my_ready, TURN * it + TURN + 1)
                for b in range(2):
                    for q in range(4):
                        last = pe.transpose(bank[5 + 2 * b][:, q * P:(q + 1) * P], OT[:, (4 * b + q) * P:(4 * b + q + 1) * P], ident[:, :])
                    last.then_inc(OT_psum, 1)

            pe.wait_ge(nm_in, 16)
            pe.wait_ge(nmT_ready, 3)
            keys_scores(0, 0, 0)
            keys_scores(0, 0, 1)
            with pe.Fori(0, TURNS - 1) as hp:
                attend(hp, hp + TURNS - FREE_TURNS)
            attend(TURNS - 1, None)
            pe.wait_ge(att_ready, 4 * TURNS + 1)
            transposes(att, attT, attT_psum, attT_ready)
            for g in range(TILES // TB):
                pe.wait_ge(attT_ready, g + 1)
                for q in range(TB):
                    t = g * TB + q
                    last = pe.matmul(bank[2 + g][:, q * P:(q + 1) * P], attT[:, t * P:(t + 1) * P], w_p[:, :], start=True, stop=True)
                last.then_inc(fin_psum, 1)

        @block.vector
        def _(dve):
            steps = [0]

            def link(ins):
                steps[0] += 1
                ins.then_inc(ln_step, 1)
                dve.wait_ge(ln_step, steps[0])

            norms = [0]
            sq_of = [sq]

            def bcast(v):
                return v.unsqueeze(2).broadcast_to([P, TILES, DIM])

            def norm(src, dst, done):
                link(dve.tensor_reduce(stat[:, 0, :], src, X, ALU.add))
                link(dve.tensor_scalar(stat[:, 0, :], stat[:, 0, :], 1.0 / DIM, None, ALU.mult))
                link(dve.tensor_tensor(dst, src, bcast(stat[:, 0, :]), ALU.subtract))
                link(dve.tensor_tensor(sq_of[0], dst, dst, ALU.mult))
                link(dve.tensor_reduce(stat[:, 1, :], sq_of[0], X, ALU.add))
                dve.tensor_scalar(stat[:, 1, :], stat[:, 1, :], 1.0 / DIM, EPS, ALU.mult, ALU.add).then_inc(var_ready, 1)
                norms[0] += 1
                dve.wait_ge(std_ready, norms[0])
                link(dve.reciprocal(stat[:, 3, :], stat[:, 2, :]))
                dve.tensor_tensor(dst, dst, bcast(stat[:, 3, :]), ALU.mult).then_inc(done, 1)

            dve.wait_ge(s_x, 64)
            norm(resid[:, :, :], xn, xn_ready)
            dve.wait_ge(xn_ready, 1)
            norm(xn, xa, xa_ready)
            dve.wait_ge(logit_ready, 1)
            for t in range(TILES):
                last = dve.max(top[:, t, :], logit[:, t, :])
            last.then_inc(logit_max, 1)
            dve.wait_ge(logit_max, 1)
            for t in range(TILES):
                last = dve.max_index(topi[:, t, :], top[:, t, :], logit[:, t, :])
            link(last)
            link(dve.tensor_copy(topf[:, :, :], topi[:, :, 0:1]))
            dve.wait_ge(s_const, 96)
            dve.tensor_tensor(onehot[:, :, :], iota8[:, :].unsqueeze(1).broadcast_to([P, TILES, 8]),
                              topf[:, :, :].broadcast_to([P, TILES, 8]), ALU.is_equal).then_inc(onehot_ready, 1)
            dve.wait_ge(score_ready, 1)
            dve.tensor_tensor(xs, xn, bcast(score[:, :]), ALU.mult).then_inc(xs_ready, 1)
            dve.wait_ge(a_exp, 1)
            link(dve.tensor_scalar(ABC[:, 0, :], ABC[:, 0, :], -10.0, -0.01, ALU.max, ALU.min))
            link(dve.tensor_reduce(decay[:, :], ABC[:, 0, :], X, ALU.max))
            link(dve.tensor_scalar(decay[:, :], decay[:, :], -1.0, None, ALU.mult))
            for ch in range(CH):
                last = dve.tensor_scalar(diagC[:, ch, :], ident[:, :], ABC[:, 2, ch:ch + 1], None, ALU.mult)
            last.then_inc(scan_consts, 1)
            dve.wait_ge(proj_psum, 4 * CHUNKS)
            dve.memset(y_flat, 0.0).then_inc(y_added, 1)
            dve.wait_ge(zeros_ready, 1)
            dve.wait_ge(y_added, 1)

            def window(w, p, first=False, extra=()):
                extra = dict(extra)
                dve.wait_ge(uf_ready, 2 * w + 2)
                dve.wait_ge(ub_ready, 2 * w + 2)
                for j in range(WIN):
                    prev_f = scan_f[p][:, j - 1, :] if j else scan_f[1 - p][:, WIN - 1, :]
                    prev_b = scan_b[p][:, WIN - j, :] if j else scan_b[1 - p][:, 0, :]
                    if first and j == 0:
                        prev_f = prev_b = zeros[:, :]
                    cur_f, cur_b = scan_f[p][:, j, :], scan_b[p][:, WIN - 1 - j, :]
                    for step, prev, cur in ((f_step, prev_f, cur_f), (b_step, prev_b, cur_b)):
                        if not (first and j == 0):
                            dve.wait_ge(step, 2 * WIN * w + 2 * j)
                        dve.scalar_tensor_tensor(cur, prev, decay[:, 0:1], cur, ALU.mult, ALU.add).then_inc(step, 1)
                    for step, cur in ((f_step, cur_f), (b_step, cur_b)):
                        dve.wait_ge(step, 2 * WIN * w + 2 * j + 1)
                        dve.tensor_scalar(cur, cur, -H_MAX, H_MAX, ALU.max, ALU.min).then_inc(step, 1)
                    if j in extra:
                        extra[j]()

            def add_down(n, c, weight):
                dve.wait_ge(dn_psum, n + 1)
                for q in range(CT):
                    t = c * CT + q
                    out = bank[4][:, q * P:(q + 1) * P]
                    if weight is None:
                        last = dve.tensor_tensor(resid[:, t, :], resid[:, t, :], out, ALU.add)
                    else:
                        last = dve.scalar_tensor_tensor(resid[:, t, :], out, onehot[:, t, weight], resid[:, t, :], ALU.mult, ALU.add)
                last.then_inc(dn_added, 1)

            def add_y(n, i):
                dve.wait_ge(window_read, n + 2)
                lo = WIN * n
                for d, base in ((0, lo), (1, SEG - WIN - lo)):
                    for h in range(HALVES):
                        dst = y[:, h, :].rearrange("p (s t) -> p s t", s=SEGS)[:, :, bass.ds(base, WIN)]
                        src = bank[5 + i][:, (2 * d + h) * P:(2 * d + h + 1) * P].rearrange("p (m s) -> p s m", m=WIN)
                        last = dve.tensor_tensor(dst, dst, src, ALU.add)
                last.then_inc(y_added, 1)

            window(0, 0, first=True)
            window(1, 1, extra={7: lambda: (add_down(0, 0, None), add_down(1, 1, None))})
            window(2, 0, extra={7: lambda: (add_down(2, 2, None), add_down(3, 3, None))})
            with dve.Fori(0, E0) as e:
                def lag(n):
                    return lambda: add_down(CHUNKS * (e + 1) + n, n, bass.ds(e, 1))
                window(2 * e + 3, 1)
                window(2 * e + 4, 0, extra={1: lag(0), 5: lag(1), 7: lambda: add_y(2 * e, 0)})
                lag(2)()
                lag(3)()
                add_y(2 * e + 1, 1)
            dve.wait_ge(y_added, 2 * E0 + 1)
            dve.scalar_tensor_tensor(sgate[:, :, :], y[:, :, :], 0.5, sgate[:, :, :], ALU.mult, ALU.mult).then_inc(o_ready, 1)
            for g in range(TILES // TB):
                dve.wait_ge(out_psum, g + 1)
                dve.tensor_tensor(resid[:, g * TB:(g + 1) * TB, :], resid[:, g * TB:(g + 1) * TB, :], bank[g][:, :].rearrange("p (t d) -> p t d", t=TB), ALU.add).then_inc(x1_ready, 1)

            link(dve.tensor_scalar(inv, temp, 0.1, 10.0, ALU.max, ALU.min))
            link(dve.tensor_scalar(inv, inv, float(np.sqrt(np.float32(DIM))), None, ALU.mult))
            link(dve.reciprocal(inv, inv))
            dve.tensor_tensor(bqi, bq, inv, ALU.mult).then_inc(inv_ready, 1)
            sq_of[0] = sq1
            dve.wait_ge(x1_ready, 4)
            norm(resid[:, :, :], xn1, xn1_ready)
            dve.wait_ge(sc1_ready, 2)
            flat = lambda a: a.rearrange("p t e -> p (t e)")
            link(dve.tensor_tensor(sfc, sc1, gbias.unsqueeze(1).broadcast_to([P, TILES, E1]), ALU.add))
            G8 = TILES * GROUPS
            v8 = flat(sfc).rearrange("p (g k) -> p g k", k=8)

            def three(a, n):
                return a[:, 0:G8 * n].rearrange("p (g k) -> p g k", k=n)

            hi, lo, lo2 = three(net[0], 4), three(net[1], 4), None
            dve.tensor_tensor(hi, v8[:, :, 0:4], v8[:, :, 4:8], ALU.max)
            link(dve.tensor_tensor(lo, v8[:, :, 0:4], v8[:, :, 4:8], ALU.min))
            for n in (2, 1):
                mid, top_lo = three(net[2], n), net[2][:, G8 * n:2 * G8 * n].rearrange("p (g k) -> p g k", k=n)
                dve.tensor_tensor(mid, hi[:, :, 0:n], hi[:, :, n:2 * n], ALU.min)
                link(dve.tensor_tensor(top_lo, lo[:, :, 0:n], lo[:, :, n:2 * n], ALU.max))
                dve.tensor_tensor(hi[:, :, 0:n], hi[:, :, 0:n], hi[:, :, n:2 * n], ALU.max)
                link(dve.tensor_tensor(lo[:, :, 0:n], mid, top_lo, ALU.max))
            link(dve.tensor_tensor(gs[:, :, :].rearrange("p t g -> p (t g)").unsqueeze(2), hi[:, :, 0:1], lo[:, :, 0:1], ALU.add))
            for t in range(TILES):
                last = dve.max(gtop[:, t, :], gs[:, t, :])
            link(last)
            for t in range(TILES):
                last = dve.max_index(gidx[:, t, :], gtop[:, t, :], gs[:, t, :])
            link(last)
            link(dve.tensor_copy(gidxf[:, :, :], gidx[:, :, :]))
            pick = net[0][:, 0:G8 * TOPG].rearrange("p (t g k) -> p t g k", t=TILES, g=GROUPS)
            link(dve.tensor_tensor(pick, iota8[:, :].unsqueeze(1).unsqueeze(3).broadcast_to([P, TILES, GROUPS, TOPG]),
                                   gidxf[:, :, 0:TOPG].unsqueeze(2).broadcast_to([P, TILES, GROUPS, TOPG]), ALU.is_equal))
            link(dve.tensor_reduce(gmask, pick, X, ALU.add))
            link(dve.tensor_tensor(flat(masked).rearrange("p (g k) -> p g k", k=8), v8,
                                   gmask.rearrange("p t g -> p (t g)").unsqueeze(2).broadcast_to([P, G8, 8]), ALU.mult))
            link(dve.tensor_scalar(masked, masked, 0.0, None, ALU.add))
            for t in range(TILES):
                last = dve.max(etop[:, t, :], masked[:, t, :])
            link(last)
            for t in range(TILES):
                last = dve.match_replace(repl[:, t, :], etop[:, t, :], masked[:, t, :], -3.0e38)
            link(last)
            dve.tensor_tensor(M, masked, repl, ALU.not_equal).then_inc(mask_ready, 1)
            dve.wait_ge(mask_ready, 1)
            link(dve.tensor_tensor(rw, sc1, M, ALU.mult))
            link(dve.tensor_reduce(den1[:, :], rw, X, ALU.add))
            link(dve.tensor_scalar(den1[:, :], den1[:, :], 1e-20, None, ALU.add))
            link(dve.reciprocal(den1[:, :], den1[:, :]))
            link(dve.tensor_scalar(den1[:, :], den1[:, :], 2.5 * 0.5, None, ALU.mult))
            link(dve.tensor_tensor(rw, rw, den1[:, :].unsqueeze(2).broadcast_to([P, TILES, E1]), ALU.mult))
            dve.wait_ge(v_ones, 1)
            for g in range(TILES // TB):
                dve.wait_ge(v_psum, g + 1)
                for q in range(TB):
                    t = g * TB + q
                    last = dve.tensor_tensor(V[:, t, :, 0:HD], bank[4 + g % 2][:, q * P:(q + 1) * P].rearrange("p (h d) -> p h d", h=HEADS),
                                             bv_t.rearrange("p (h d) -> p h d", h=HEADS), ALU.add)
                last.then_inc(v_ready, 1)
            dve.wait_ge(bp_added, 1)
            for c in range(CHUNKS):
                dve.wait_ge(sdn_psum, c + 1)
                dve.tensor_tensor(resid[:, CT * c:CT * c + CT, :], resid[:, CT * c:CT * c + CT, :],
                                  bank[4].rearrange("p (t d) -> p t d", t=CT), ALU.add).then_inc(sdn_added, 1)
            link(dve.memset(carry[:, 0, :], 0.0))
            dve.wait_ge(rank_psum, 1)
            total = [bank[2 + t // 8][:, (t % 8) * E1:(t % 8 + 1) * E1] for t in range(TILES)]
            for t in range(1, TILES):
                link(dve.tensor_tensor(carry[:, t, :], carry[:, t - 1, :], total[t - 1], ALU.add))
            link(dve.tensor_tensor(nt, carry[:, TILES - 1, :], total[TILES - 1], ALU.add))
            link(dve.tensor_scalar(ntu[:, :], nt, float(P - 1), None, ALU.add))
            link(dve.tensor_scalar(ntu[:, :], ntu[:, :], 7, None, ALU.logical_shift_right))
            link(dve.tensor_copy(nt, ntu[:, :]))
            link(dve.memset(ones64, 1.0))
            link(dve.tensor_tensor_scan(endt, ones64, nt, 0.0, ALU.mult, ALU.add))
            link(dve.tensor_tensor(base1, endt, nt, ALU.subtract))
            link(dve.tensor_scalar(base1, base1, float(P), None, ALU.mult))
            for k in range(2):
                last = dve.tensor_tensor(slot[:, 8 * k:8 * k + 8, :], carry[:, 8 * k:8 * k + 8, :], bank[6 + k].rearrange("p (t e) -> p t e", e=E1), ALU.add)
            link(last)
            link(dve.tensor_tensor(slot, slot, base1.unsqueeze(1).broadcast_to([P, TILES, E1]), ALU.add))
            link(dve.tensor_scalar(slot, slot, -1.0, KEY, ALU.mult, ALU.add))
            link(dve.tensor_tensor(key, slot, M, ALU.mult))
            for t in range(TILES):
                last = dve.max(etop[:, t, :], key[:, t, :])
            link(last)
            dve.tensor_scalar(slots[:, :, :], etop[:, :, :], -1.0, KEY, ALU.mult, ALU.add).then_inc(slots_ready, 1)
            for c in range(2):
                link(dve.tensor_scalar(cmp8[:, c, :], endt, jcol[:, c:c + 1], None, ALU.is_le))
                link(dve.tensor_reduce(exp_of[:, c:c + 1], cmp8[:, c, :], X, ALU.add))
            dve.tensor_scalar(exp_of[:, :], exp_of[:, :], float(E1 - 1), None, ALU.min).then_inc(exp_ready, 1)
            for t in range(TILES):
                link(dve.tensor_tensor(cmp8, key[:, t, :].unsqueeze(1).broadcast_to([P, 8, E1]),
                                       etop[:, t, :].unsqueeze(2).broadcast_to([P, 8, E1]), ALU.is_equal))
                link(dve.tensor_tensor(cmp8b, cmp8, rw[:, t, :].unsqueeze(1).broadcast_to([P, 8, E1]), ALU.mult))
                link(dve.tensor_reduce(w8[:, t, :], cmp8b, X, ALU.add))
            dve.wait_ge(etab_psum, 1)
            dve.tensor_copy(etab[:, :], bank[0][0:1, 0:2 * P]).then_inc(etab_ready, 1)
            dve.memset(rec[:, :, 0:1], 0.0).then_inc(w8_ready, 1)
            dve.memset(rec[:, :, 1:2], 0.0).then_inc(my_ready, 1)
            dve.memset(rec[:, :, 2:3], 0.0).then_inc(acc_free, 1)
            dve.memset(rec[:, :, 3:4], 0.0).then_inc(att_ready, 1)

            dve.memset(nmr, 0.0).then_inc(pair_free, 2)
            with dve.Fori(0, HEADS // 2) as hp:
                for k in range(4):
                    for q in range(QT):
                        n = 32 * hp + 8 * k + q
                        dve.wait_ge(sq_psum, n + 1)
                        dve.tensor_reduce(nm[:, bass.ds(4 * hp + k, 1), q:q + 1], psum[:, 1024 * (q % 2):1024 * (q % 2) + 1024].rearrange("p (a n) -> p a n", a=1),
                                          X, ALU.max, negate=True).then_inc(pair_free, 1)
            dve.wait_ge(nmT_psum, 1)
            nps = bank[0][:, 0:2 * P].rearrange("p (c n) -> p c n", c=2)
            dve.tensor_copy(nmT[0][:, :, :], nps).then_inc(nmT_ready, 1)
            dve.wait_ge(nmT_ready, 1)
            link(dve.tensor_tensor(nmr, nps, nmT[0][:, :, :], ALU.subtract))
            dve.tensor_copy(nmT[1][:, :, :], nmr).then_inc(nmT_ready, 1)
            dve.wait_ge(nmT_ready, 2)
            dve.tensor_tensor(nmT[2][:, :, :], nmr, nmT[1][:, :, :], ALU.subtract).then_inc(nmT_ready, 1)

            def head_v(n, buf):
                dve.tensor_copy(Vh[buf], V[:, :, bass.ds(n, 1), :].rearrange("p t a d -> p t (a d)")).then_inc(v_head, 1)

            def pair_steps(it, i):
                j = TURN * it + i
                dve.wait_ge(mxT_psum, j + 3)
                dve.tensor_copy(m_xT[i % 2], bank[5][:, 0:PW]).then_inc(mxT_ready, 1)
                k2 = (i + 1) % 2
                dve.wait_ge(mth_ready, j + 2)
                dve.scalar_tensor_tensor(m_th[0:I1, k2, :], m_th[0:I1, k2, :], 1.0, bank[6][0:I1, 0:PW], ALU.add, ALU.mult).then_inc(ma_step, 1)
                dve.wait_ge(ma_step, j - TURN * (TURNS - FREE_TURNS) + 1)
                dve.tensor_tensor(m_h[0:I1, k2, :], m_th[0:I1, k2, :], bank[6][0:I1, PW:2 * PW], ALU.mult).then_inc(ma_ready, 1)
                dve.wait_ge(my_psum, j + 1)
                dve.wait_ge(my_out[i % 2], 16 * (TURN // 2 * it + i // 2 + 1))
                dve.tensor_copy(m_y[:, i % 2, :, :].rearrange("p a d -> p (a d)"), bank[7][:, 0:PW]).then_inc(my_ready, 1)

            def routed(t):
                dve.wait_ge(y_in[t % 2], 16 * TOPK * (t // 2 + 1))
                for k in range(TOPK):
                    last = dve.scalar_tensor_tensor(resid[:, t, :], ybuf[t % 2][:, k, :], w8[:, t, k:k + 1], resid[:, t, :], ALU.mult, ALU.add)
                    if k < TOPK - 1:
                        link(last)
                last.then_inc(y_used, 1)

            def units(hp, it):
                for k in range(4):
                    for qh in range(2):
                        if it is not None:
                            pair_steps(it, 2 * k + qh)
                        dve.wait_ge(p_free, 32 * hp + 8 * k + 4 * qh + 6)
                        dve.tensor_copy(OT[32 * k:32 * k + HD + 1, qh * 512:(qh + 1) * 512], bank[4][0:HD + 1, :]).then_inc(acc_free, 1)
                        if it is None:
                            routed(2 * k + qh)
                    if k % 2 == 1 and it is not None:
                        head_v(2 * hp + 2 + k // 2, k // 2)
                for b in range(2):
                    t_psum = bank[5 + 2 * b].rearrange("p (q k c) -> p q k c", q=4, k=4)
                    dve.wait_ge(OT_psum, 2 * hp + b + 1)
                    dve.reciprocal(rec[:, 4 * b:4 * b + 4, :].unsqueeze(3), t_psum[:, :, :, HD:HD + 1]).then_inc(rec_ready, 1)
                    dve.wait_ge(rec_ready, 2 * hp + b + 1)
                    for n in range(2):
                        out = att[:, n * QT + 4 * b:n * QT + 4 * b + 4, bass.ds(2 * hp * HD, 2 * HD)].rearrange("p q (h d) -> p q h d", h=2)
                        last = dve.tensor_tensor(out, bank[5 + 2 * b].rearrange("p (q h n c) -> p q h n c", q=4, h=2, n=2)[:, :, :, n, 0:HD],
                                                 rec[:, 4 * b:4 * b + 4, :].rearrange("p q (h n) -> p q h n", h=2)[:, :, :, n:n + 1].broadcast_to([P, 4, 2, HD]),
                                                 ALU.mult)
                        last.then_inc(att_ready, 1)

            dve.wait_ge(scattered, 16 * TILES * TOPK)
            for k in range(2):
                head_v(k, k)
            with dve.Fori(0, TURNS - 1) as hp:
                units(hp, hp + TURNS - FREE_TURNS)
            units(TURNS - 1, None)
            for g in range(TILES // TB):
                dve.wait_ge(fin_psum, g + 1)
                dve.tensor_tensor(resid[:, g * TB:(g + 1) * TB, :], resid[:, g * TB:(g + 1) * TB, :], bank[2 + g].rearrange("p (t d) -> p t d", t=TB), ALU.add).then_inc(fin_ready, 1)
            dve.wait_ge(fin_ready, TILES // TB)
            for t in range(QT, TILES):
                routed(t)


def kernel(**inputs):
    import concourse.bacc as bacc
    from concourse.bass_utils import run_bass_kernel_spmd
    import ml_dtypes

    def t(a):
        return np.ascontiguousarray(a)

    i = {k: np.asarray(v) for k, v in inputs.items()}

    def halves(a):
        return a.reshape(HALVES, P, STATES).transpose(1, 0, 2).reshape(P, CH)

    gu = [np.concatenate([i["L0_ffn_sh_gate"], i["L0_ffn_sh_up"]], 1)] + \
         [np.concatenate([i["L0_ffn_rt_gate"][e], i["L0_ffn_rt_up"][e]], 1) for e in range(E0)]
    dn = [i["L0_ffn_sh_down"]] + [i["L0_ffn_rt_down"][e] for e in range(E0)]
    arrays = {
        "x": i["L0_attn_x"].reshape(TOK, DIM),
        "ident": np.eye(P, dtype=np.float32),
        "iota8": np.tile(np.arange(8, dtype=np.float32), (P, 1)),
        "lnwb": np.stack([i["L0_attn_ln_w"], i["L0_attn_ln_b"]], 1),
        "w_gate0": i["L0_ffn_gate_w"],
        "abc": np.stack([halves(i["L0_attn_A_log"]), halves(i["L0_attn_B_mat"]), halves(i["L0_attn_C_mat"])], 1),
        "w_in": i["L0_attn_in_proj_w"].T,
        "w_out": i["L0_attn_out_proj_w"].T.reshape(2, P, DIM).transpose(1, 0, 2),
        "w_gu0": np.stack(gu),
        "w_dn0": np.stack([d.reshape(2, P, DIM).transpose(1, 0, 2) for d in dn]),
    }
    table = i["L1_attn_bias_table"]
    rows = np.arange(P)
    q_major = np.clip(rows[:, None, None] + P * np.arange(2)[None, :, None] - (np.arange(CORNER) + LEN - CORNER)[None, None, :] + LEN - 1, 0, BIASED)
    k_major = np.clip(np.arange(CORNER)[None, None, :] - (rows[:, None, None] + P * np.arange(2)[None, :, None] + LEN - CORNER) + LEN - 1, 0, BIASED)

    def corners(index):
        flat = np.concatenate([index.reshape(P, 2 * CORNER), np.full((P, 1), BIASED)], 1)
        return table.T[:, flat]

    ck = corners(k_major)
    arrays.update({
        "small": np.concatenate([i["L1_attn_bq"][:, None], i["L1_attn_bk"][:, None], np.tile(i["L1_attn_temperature"], (P, 1)),
                                 rows[:, None].astype(np.float32), rows[:, None].astype(np.float32) + P,
                                 np.tile(table[BIASED], (P, 1))], 1),
        "w_q": i["L1_attn_Wq"], "w_k": i["L1_attn_Wk"], "w_v": i["L1_attn_Wv"], "w_p": i["L1_attn_Wp"],
        "bv_t": np.tile(i["L1_attn_bv"], (P, 1)), "bp_t": np.tile(i["L1_attn_bp"], (P, 1)),
        "strict": np.triu(np.ones((P, P), np.float32), 1), "ones": np.ones((P, P), np.float32),
        "w_gate1": i["L1_ffn_gate_w"].T, "gbias": np.tile(i["L1_ffn_gate_bias"], (P, 1)),
        "w_sh": np.concatenate([i["L1_ffn_Sg"].T, i["L1_ffn_Su"].T], 1),
        "w_shd": i["L1_ffn_Sd"].T.reshape(2, I1, DIM).transpose(1, 0, 2),
        "w_gu1": np.concatenate([i["L1_ffn_Wg"].transpose(0, 2, 1), i["L1_ffn_Wu"].transpose(0, 2, 1)], 2),
        "w_dn1": i["L1_ffn_Wd"].transpose(0, 2, 1),
        "corners": np.concatenate([corners(q_major), ck]),
        "fill_q": np.zeros((16, UNITS * LEN), ml_dtypes.bfloat16),
        "fill_k": np.concatenate([np.ones((3, UNITS * LEN)), np.zeros((13, UNITS * LEN))]).astype(ml_dtypes.bfloat16),
    })
    arrays = {k: t(v) for k, v in arrays.items()}
    nc = bacc.Bacc("TRN2", target_bir_lowering=False, num_devices=1)
    A = {k: nc.dram_tensor("in_" + k, v.shape, mybir.dt.from_np(v.dtype), kind="ExternalInput").ap() for k, v in arrays.items()}
    A["out"] = nc.dram_tensor("out", (TOK, DIM), F32, kind="ExternalOutput").ap()
    build(nc, A)
    r = run_bass_kernel_spmd(nc, [{"in_" + k: v for k, v in arrays.items()}], core_ids=[0])
    return r.results[0]["out"].reshape(BATCH, LEN, DIM)
```

```python
import concourse.bass as bass
from concourse import mybir
from contextlib import ExitStack
import numpy as np

F32 = mybir.dt.float32
BF16 = mybir.dt.bfloat16
F16 = mybir.dt.float16
U32 = mybir.dt.uint32
ALU = mybir.AluOpType
ACT = mybir.ActivationFunctionType
X = mybir.AxisListType.X

P = 128
BATCH, LEN, DIM = 2, 1024, 128
TOK = BATCH * LEN
TILES = TOK // P
EPS = 1e-5

HALVES, STATES = 2, 16
SEG = 128
SEGS = TOK // SEG
WARM = 24
WIN = 8
WINDOWS = (SEG + WARM) // WIN
CH = HALVES * STATES
COL = CH * SEGS
PADSEG = SEG + 2 * WARM
H_MAX = 10.0

E0, I0 = 8, 256
CHUNK = 512
CHUNKS = TOK // CHUNK
CT = CHUNK // P

HEADS, HD = 16, 8
QT = LEN // P
UNITS = HEADS * BATCH
PARTS_Q = (0, 0, 1, 1, 0, 2)
PARTS_K = (0, 1, 0, 1, 2, 0)
KROWS = 65
MAXROW = 8 * len(PARTS_Q)
BIASED = 248
CORNER = 3 * P
STRIPS = ((0, 2 * P), (2 * P, P))
P_SCALE = 8 * float(np.log(2.0))

E1, I1, TOPK, GROUPS, TOPG = 64, 88, 8, 8, 4
MT = TOK * TOPK // P + E1
TURNS = HEADS // 2
FREE_TURNS = 4
PAIRS1, PAIRS2 = 10, 8
FIRST = PAIRS1 * (TURNS - FREE_TURNS)
LO_SPLIT = 640
LATE = 5
assert MT == 2 * (FIRST + PAIRS2 * (TURNS - 1))


def last_turn(hp):
    return isinstance(hp, int) and hp == TURNS - 1


def in_first(it):
    return PAIRS1 * it, PAIRS1 // 2 * it


def in_second(hp):
    return FIRST + PAIRS2 * hp, FIRST // 2 + PAIRS2 // 2 * hp


SLOTS = MT + 8
KEY = 32768.0


def build(nc, A):
    ctx = ExitStack()
    with ctx:
        def sb(name, shape, dt=F32):
            return ctx.enter_context(nc.sbuf_tensor(name, shape, dt))

        def sem(name):
            return ctx.enter_context(nc.semaphore(name))

        ident = sb("ident", [P, P])
        iota8 = sb("iota8", [P, 8])
        lnwb = sb("lnwb", [P, 2])
        w_gate0 = sb("w_gate0", [P, E0])
        resid = sb("resid", [P, TILES, DIM])
        xnT = sb("xnT", [P, TOK])
        xsT = sb("xsT", [P, TOK])
        arena = sb("arena", [P, 34304])
        cursor = [0]

        def carve(n):
            cursor[0] += n
            assert cursor[0] <= 34304
            return arena[:, cursor[0] - n:cursor[0]]

        scan_flat = [carve(WIN * COL) for _ in range(4)]
        scan_f = [s.rearrange("p (m c) -> p m c", m=WIN) for s in scan_flat[:2]]
        scan_b = [s.rearrange("p (m c) -> p m c", m=WIN) for s in scan_flat[2:]]
        diagC = carve(CH * P).rearrange("p (c n) -> p c n", c=CH)
        xssm = carve(HALVES * SEGS * PADSEG).rearrange("p (h s m) -> p h s m", h=HALVES, s=SEGS)
        sgate = carve(HALVES * TOK).rearrange("p (h t) -> p h t", h=HALVES)
        y_flat = carve(HALVES * TOK)
        y = y_flat.rearrange("p (h t) -> p h t", h=HALVES)
        xn = y_flat[:, 0:TOK].rearrange("p (t d) -> p t d", t=TILES)
        xaT = y_flat[:, TOK:2 * TOK]
        xa = scan_flat[0][:, 0:TOK].rearrange("p (t d) -> p t d", t=TILES)
        sq = scan_flat[1][:, 0:TOK].rearrange("p (t d) -> p t d", t=TILES)
        xs = scan_flat[0][:, TOK:2 * TOK].rearrange("p (t d) -> p t d", t=TILES)
        w_in = scan_flat[2][:, 0:2 * HALVES * P]
        zeros = sb("zeros", [P, COL])
        ABC = sb("ABC", [P, 3, CH])
        decay = sb("decay", [P, 1])
        w_gu = sb("w_gu", [P, 2 * I0])
        w_dn = sb("w_dn", [P, 2, DIM])
        w_out = sb("w_out", [P, 2, DIM])
        silu_g = sb("silu_g", [P, 2, CHUNK])
        up = sb("up", [P, 2, CHUNK])
        act = sb("act", [P, 2, CHUNK])
        stat = sb("stat", [P, 4, TILES])
        logit = sb("logit", [P, TILES, E0])
        top = sb("top", [P, TILES, 8])
        topi = sb("topi", [P, TILES, 8], U32)
        topf = sb("topf", [P, TILES, 1])
        score = sb("score", [P, TILES])
        onehot = sb("onehot", [P, TILES, E0])

        U32W = LEN // 2
        Qs = arena[:, 0:UNITS * U32W].bitcast(BF16)
        Ks = arena[:, UNITS * U32W:2 * UNITS * U32W].bitcast(BF16)

        QUARTER = UNITS * U32W // 2
        cursor[0] = 0
        qf, kf = carve(TOK), carve(TOK)
        parts = [carve(TOK // 2).bitcast(BF16) for _ in range(4)]
        assert cursor[0] <= QUARTER
        cursor[0] = 2 * QUARTER
        w_q, w_k, w_v, bv_t, bp_t = (carve(P) for _ in range(5))
        parts += [carve(TOK // 2).bitcast(BF16) for _ in range(2)]
        sq1 = carve(TOK).rearrange("p (t d) -> p t d", t=TILES)
        assert cursor[0] <= 3 * QUARTER
        cursor[0] = QUARTER
        strict, ones, w_gate1, gbias = carve(P), carve(P), carve(E1), carve(E1)
        w_sh = carve(4 * I1)
        w_shd = carve(2 * DIM).rearrange("p (k d) -> p k d", k=2)
        TE = TILES * E1

        def table():
            return carve(TE).rearrange("p (t e) -> p t e", t=TILES)

        sc1, sfc, masked, repl, M, rw, carry = (table() for _ in range(7))
        assert cursor[0] <= 2 * QUARTER
        cursor[0] = 3 * QUARTER
        slot, key = table(), table()
        net = [carve(TE // 2) for _ in range(3)]
        cmp8 = carve(8 * E1).rearrange("p (k e) -> p k e", k=8)
        cmp8b = [carve(16 * E1).rearrange("p (t k e) -> p t k e", t=2, k=8) for _ in range(4)]
        ones64 = carve(E1)
        nt, endt, base1 = carve(E1), carve(E1), carve(E1)
        xn1 = xsT[:, :].rearrange("p (t d) -> p t d", t=TILES)
        xn1T = xnT
        att = xnT[:, :].rearrange("p (t d) -> p t d", t=TILES)
        attT = xsT
        w_p = sb("w_p", [P, P])
        small = sb("small", [P, 32])
        bq, bk, temp, jcol = small[:, 0:1], small[:, 1:2], small[:, 2:3], small[:, 3:5]
        inv, bqi, zero = small[:, 21:22], small[:, 22:23], small[:, 23:24]
        gs, gtop, gidx, gidxf = logit, top, topi, onehot
        gmask = carve(TILES * 8).rearrange("p (t g) -> p t g", t=TILES)
        etop = sb("etop", [P, TILES, 8])
        den1 = sb("den1", [P, TILES])
        slots = sb("slots", [P, TILES, TOPK], U32)
        w8 = sb("w8", [P, TILES, TOPK])
        ntu = sb("ntu", [P, E1], U32)
        exp_of = sb("exp_of", [P, 2])
        etab = sb("etab", [1, 2 * P], U32)
        V = sb("V", [P, TILES, HEADS, HD + 1])
        nm = sb("nm", [P, UNITS, QT])
        nmT = [sb(f"nmT{k}", [P, 2, P], BF16) for k in range(3)]
        nmr = xnT[:, 0:2 * P].rearrange("p (c n) -> p c n", c=2)
        rec = sb("rec", [P, QT, 4])
        corner_f = sb("corner_f", [P, CORNER + 1])
        corner_p = sb("corner_p", [P, 2, 3, CORNER], BF16)
        identb = sb("identb", [P, P], BF16)
        Pt = [silu_g, up]
        PW = 2 * P
        m_x, m_y = (act[:, k, :].rearrange("p (b a d) -> p b a d", b=2, a=2) for k in range(2))
        m_gu = sb("m_gu", [P, 2, 2, 2 * I1])
        m_dn = w_gu[:, :].rearrange("p (b a d) -> p b a d", b=2, a=2)
        m_xT = [w[:, :, :].rearrange("p a n -> p (a n)") for w in (w_dn, w_out)]
        m_th = zeros[:, :].rearrange("p (b n) -> p b n", b=2)
        tail = arena[:, 2 * UNITS * U32W:34304]
        m_u = tail[:, 0:2 * PW].rearrange("p (b n) -> p b n", b=2)
        m_h = tail[:, 4 * PW:6 * PW].rearrange("p (b n) -> p b n", b=2)
        ybuf = [[m_gu[:, :, :, :].rearrange("p b a n -> p (b a n)")[:, k * DIM:(k + 1) * DIM] for k in range(5)] +
                [w_gu[:, k * DIM:(k + 1) * DIM] for k in range(3)],
                [act[:, :, :].rearrange("p a n -> p (a n)")[:, k * DIM:(k + 1) * DIM] for k in range(8)]]
        OT = xsT[:, 0:LEN]
        VW = 3 * (HD + 1)
        Vh = [xsT[:, LEN + 216 * k:LEN + 216 * (k + 1)].bitcast(BF16).rearrange("p (t d) -> p t d", t=TILES) for k in range(2)]
        v_rest = nm[:, :, :].rearrange("p u q -> p (u q)")[:, 0:TILES * (HD + 1)].rearrange("p (t d) -> p t d", t=TILES)
        v_sum = [sb(f"v_sum{k}", [P, 4, 4, HD + 1]) for k in range(2)]
        p_hi_a = sb("p_hi_a", [P, 512])
        p_hi = [a.bitcast(F16).rearrange("p (a n) -> p a n", a=2) for a in (p_hi_a[:, :], xsT[:, LEN + 512:2 * LEN])]
        p_lo = [tail[:, 512 * k:512 * (k + 1)].bitcast(F16).rearrange("p (a n) -> p a n", a=2) for k in range(2)]

        def cols(a, lo, hi):
            return a.rearrange("p a n -> p (a n)")[:, lo:hi]

        d_parts = nc.dram_tensor("d_parts", (6, P, TOK), BF16).ap()
        d_nm = nc.dram_tensor("d_nm", (3, 2, P, P), BF16).ap()
        d_xs = nc.dram_tensor("d_xs", (SLOTS * P, DIM), F32).ap()
        d_ys = nc.dram_tensor("d_ys", (MT * P, DIM), F32).ap()

        psum = ctx.enter_context(nc.psum_tensor("psum", [P, 8 * 512], F32))
        bank = [psum[:, i * 512:(i + 1) * 512] for i in range(8)]

        s_x = sem("s_x"); s_const = sem("s_const"); s_w = sem("s_w")
        ln_step = sem("ln_step")
        var_ready = sem("var_ready"); std_ready = sem("std_ready")
        xn_ready = sem("xn_ready"); xnT_psum = sem("xnT_psum"); xnT_ready = sem("xnT_ready")
        xa_ready = sem("xa_ready"); xaT_psum = sem("xaT_psum"); xaT_ready = sem("xaT_ready")
        xs_ready = sem("xs_ready"); xsT_psum = sem("xsT_psum"); xsT_ready = sem("xsT_ready")
        logit_psum = sem("logit_psum"); logit_ready = sem("logit_ready")
        score_ready = sem("score_ready"); onehot_ready = sem("onehot_ready")
        proj_psum = sem("proj_psum"); proj_evac = sem("proj_evac")
        a_exp = sem("a_exp"); scan_consts = sem("scan_consts")
        pads = sem("pads"); halo = sem("halo"); zeros_ready = sem("zeros_ready")
        uf_ready = sem("uf_ready"); ub_ready = sem("ub_ready")
        f_step = sem("f_step"); b_step = sem("b_step")
        read_f = sem("read_f"); read_b = sem("read_b")
        y_added = sem("y_added")
        gu_psum = sem("gu_psum"); gu_evac = sem("gu_evac"); act_ready = sem("act_ready")
        dn_psum = sem("dn_psum"); dn_added = sem("dn_added")
        wgu_in = sem("wgu_in"); wdn_in = sem("wdn_in")
        o_ready = sem("o_ready"); out_psum = sem("out_psum"); x1_ready = sem("x1_ready")
        s_out = sem("s_out")
        logit_max = sem("logit_max")
        corner_idb = sem("corner_idb"); v_ones = sem("v_ones")
        l1_w = sem("l1_w"); l1_p = sem("l1_p"); xs_zero = sem("xs_zero")
        xn1_ready = sem("xn1_ready"); xn1T_psum = sem("xn1T_psum"); xn1T_ready = sem("xn1T_ready")
        lg1_psum = sem("lg1_psum"); sc1_ready = sem("sc1_ready"); inv_ready = sem("inv_ready")
        qk_psum = sem("qk_psum"); qk_ready = sem("qk_ready"); v_psum = sem("v_psum"); v_ready = sem("v_ready")
        part_ready = sem("part_ready"); rest_step = sem("rest_step"); parts_out = sem("parts_out")
        stacked = [sem(f"stacked{k}") for k in range(2)]; v_copied = sem("v_copied")
        mask_ready = sem("mask_ready"); rank_psum = sem("rank_psum"); rank_read = sem("rank_read"); slots_ready = sem("slots_ready")
        exp_ready = sem("exp_ready"); etab_psum = sem("etab_psum"); etab_ready = sem("etab_ready"); w8_ready = sem("w8_ready")
        scattered = sem("scattered"); bp_added = sem("bp_added")
        sgu_psum = sem("sgu_psum"); sgu_evac = sem("sgu_evac"); sact_ready = sem("sact_ready")
        sdn_psum = sem("sdn_psum")
        corner_in = sem("corner_in"); corner_step = sem("corner_step")
        sq_psum = sem("sq_psum"); nmT_psum = sem("nmT_psum"); nmT_ready = sem("nmT_ready")
        nm_out = sem("nm_out"); nm_in = sem("nm_in")
        st_psum = sem("st_psum"); p_ready = sem("p_ready"); pv_done = sem("pv_done"); hi0_ready = sem("hi0_ready")
        hi1_ready = sem("hi1_ready")
        lo0_ready = sem("lo0_ready"); lo1_ready = sem("lo1_ready"); v_step = sem("v_step"); OT_read = sem("OT_read")
        pair_free = sem("pair_free"); att_ready = sem("att_ready")
        acc_free = sem("acc_free"); OT_psum = sem("OT_psum")
        rec_ready = sem("rec_ready")
        mx_in, mgu_in, mdn_in = ([sem(f"{n}_in{k}") for k in range(2)] for n in ("mx", "mgu", "mdn"))
        mxT_psum = sem("mxT_psum"); mxT_ready = sem("mxT_ready"); mgu_psum = sem("mgu_psum")
        mth_ready = sem("mth_ready")
        ma_step = sem("ma_step"); ma_ready = sem("ma_ready")
        my_psum = sem("my_psum"); my_ready = sem("my_ready"); my_out = [sem(f"my_out{k}") for k in range(2)]
        y_in = [sem(f"y_in{k}") for k in range(2)]; y_used = sem("y_used"); fin_ready = sem("fin_ready")
        attT_psum = sem("attT_psum"); attT_ready = sem("attT_ready")
        fin_psum = sem("fin_psum")

        block = ctx.enter_context(nc.Block())
        TB = 4

        @block.sync
        def _(sp):
            for k in range(4):
                sp.dma_start(resid[:, 4 * k:4 * k + 4, :], A["x"][4 * k * P:4 * (k + 1) * P].rearrange("(t p) d -> p t d", p=P)).then_inc(s_x, 16)
            for dst, name in ((ident, "ident"), (iota8, "iota8"), (lnwb, "lnwb"), (w_gate0, "w_gate0")):
                sp.dma_start(dst[:, :], A[name]).then_inc(s_const, 16)
            sp.dma_start(ABC[:, :, :], A["abc"]).then_inc(s_const, 16)
            sp.dma_start(small[:, 0:21], A["small"]).then_inc(s_const, 16)
            sp.dma_start(w_in, A["w_in"]).then_inc(s_w, 16)
            sp.dma_start(w_out[:, :, :], A["w_out"]).then_inc(s_w, 16)
            sp.dma_start(w_gu[:, :], A["w_gu0"][0]).then_inc(wgu_in, 16)
            sp.dma_start(w_dn[:, :, :], A["w_dn0"][0]).then_inc(wdn_in, 16)
            sp.wait_ge(zeros_ready, 1)
            with sp.Fori(0, SLOTS // 4) as z:
                sp.dma_start(d_xs[bass.ds(z * 4 * P, 4 * P)].rearrange("(p r) d -> p (r d)", p=P), zeros[:, :]).then_inc(xs_zero, 16)
            with sp.Fori(0, E0) as e:
                sp.wait_ge(gu_psum, 2 * CHUNKS * (e + 1))
                sp.dma_start(w_gu[:, :], A["w_gu0"][bass.ds(e + 1, 1)].rearrange("a p n -> p (a n)")).then_inc(wgu_in, 16)
                sp.wait_ge(dn_psum, CHUNKS * (e + 1))
                sp.dma_start(w_dn[:, :, :], A["w_dn0"][bass.ds(e + 1, 1)].rearrange("a p k n -> p (a k) n")).then_inc(wdn_in, 16)
            sp.wait_ge(read_f, 2 * E0 + 1)
            sp.wait_ge(read_b, 2 * E0 + 1)
            sp.wait_ge(uf_ready, 2 * (WINDOWS + 1))
            sp.wait_ge(ub_ready, 2 * (WINDOWS + 1))
            for dst, name in ((w_q, "w_q"), (w_k, "w_k"), (w_v, "w_v"), (bv_t, "bv_t"), (strict, "strict"), (ones, "ones"),
                              (w_gate1, "w_gate1"), (gbias, "gbias"), (w_sh, "w_sh")):
                sp.dma_start(dst, A[name]).then_inc(l1_w, 16)
            sp.dma_start(w_shd[0:I1, :, :], A["w_shd"]).then_inc(l1_w, 16)
            sp.dma_start(w_p[:, :], A["w_p"]).then_inc(l1_p, 16)
            sp.dma_start(bp_t, A["bp_t"]).then_inc(l1_p, 16)
            def load_corner(n):
                sp.dma_start(corner_f[:, :], A["corners"][bass.ds(n, 1)].rearrange("a p n -> p (a n)")).then_inc(corner_in, 16)

            def next_corner(n):
                sp.wait_ge(corner_step, 6 * (n + 2))
                load_corner(n + 2)

            load_corner(0)
            for k, (done, count) in {0: (part_ready, 1), 3: (part_ready, 2), 1: (part_ready, 3), 4: (part_ready, 4),
                                     2: (rest_step, 3), 5: (rest_step, 4)}.items():
                sp.wait_ge(done, count)
                sp.dma_start(d_parts[k], parts[k]).then_inc(parts_out, 16)
            sp.wait_ge(parts_out, 96)
            sp.wait_ge(v_psum, 4)
            sp.wait_ge(v_ready, 1)
            sp.wait_ge(bp_added, 1)
            sp.wait_ge(xn1_ready, 1)

            def stacks(half):
                heads = slice(half * HEADS // 2, (half + 1) * HEADS // 2)
                cols = slice(half * UNITS * LEN // 2, (half + 1) * UNITS * LEN // 2)
                for side, (stack, groups, fill) in enumerate(((Qs, PARTS_Q, "fill_q"), (Ks, PARTS_K, "fill_k"))):
                    for g, part in enumerate(groups):
                        sp.dma_start(stack[8 * g:8 * g + 8, cols].rearrange("d (h n) -> d h n", h=HEADS // 2),
                                     d_parts[3 * side + part].rearrange("(h d) n -> d h n", d=HD)[:, heads, :]).then_inc(stacked[half], 16)
                    sp.dma_start(stack[MAXROW:64, cols], A[fill][0:16, cols]).then_inc(stacked[half], 16)
                    sp.dma_start(stack[64:65, cols], A[fill][15:16, cols]).then_inc(stacked[half], 16)

            stacks(0)
            sp.wait_ge(corner_step, 6)
            load_corner(1)
            sp.wait_ge(w8_ready, 1)
            sp.wait_ge(sdn_psum, CHUNKS)
            stacks(1)

            with sp.Fori(0, FREE_TURNS) as hp:
                for k in range(2):
                    next_corner(2 * hp + k)

            def expert(j):
                return bass.ds(sp.value_load(etab[0:1, bass.ds(j, 1)], min_val=0, max_val=E1 - 1), 1)

            def load_x(j, buf):
                sp.dma_start(m_x[:, buf, :, :], d_xs[bass.ds(j * PW, PW)].rearrange("(a p) d -> p a d", a=2)).then_inc(mx_in[buf], 16)

            def load_gu(experts, buf):
                for a in range(2):
                    sp.dma_start(m_gu[:, buf, a, :], A["w_gu1"][experts[a]].rearrange("a p n -> p (a n)")).then_inc(mgu_in[buf], 16)

            def load_dn(experts, buf):
                for a in range(2):
                    sp.dma_start(m_dn[0:I1, buf, a, :], A["w_dn1"][experts[a]].rearrange("a p n -> p (a n)")).then_inc(mdn_in[buf], 16)

            def experts(j):
                return [expert(2 * j + a) for a in range(2)]

            def pair_loads(j0, i, rows, e_dn):
                j = j0 + i
                e_gu = experts(j + 3)
                if e_dn is None:
                    e_dn = experts(j + 2)
                if rows:
                    sp.wait_ge(mxT_psum, j + 3)
                    load_x(j + 4, i % 2)
                sp.wait_ge(mgu_psum, j + 2)
                load_gu(e_gu, (i + 1) % 2)
                sp.wait_ge(my_psum, j + 1)
                load_dn(e_dn, i % 2)
                if rows:
                    sp.wait_ge(my_ready, j + 2)
                    sp.dma_start(d_ys[bass.ds(j * PW, PW)].rearrange("(a p) d -> p a d", a=2), m_y[:, i % 2, :, :]).then_inc(my_out[i % 2], 16)
                return e_gu

            sp.wait_ge(etab_ready, 1)
            for j in range(2):
                load_dn(experts(j), j)
                load_gu(experts(j), j)
            sp.wait_ge(scattered, 16 * TILES * TOPK)
            sp.wait_ge(sdn_psum, CHUNKS)
            load_x(0, 0)
            load_x(1, 1)
            sp.wait_ge(mxT_psum, 1)
            load_x(2, 0)
            sp.wait_ge(mxT_psum, 2)
            load_x(3, 1)
            e2 = experts(2)
            sp.wait_ge(mgu_psum, 1)
            load_gu(e2, 0)
            with sp.Fori(0, TURNS - FREE_TURNS) as it:
                known = None
                for i in range(PAIRS1):
                    if i == 4 or i == 9:
                        next_corner(2 * it + 2 * FREE_TURNS + i // 5)
                    known = pair_loads(in_first(it)[0], i, False, known)
            for k in range(3):
                sp.wait_ge(nmT_ready, k + 1)
                sp.dma_start(d_nm[k].rearrange("c p n -> p c n"), nmT[k][:, :, :]).then_inc(nm_out, 16)
            sp.wait_ge(nm_out, 48)
            sp.dma_start(Qs[MAXROW:MAXROW + 3, 0:UNITS * LEN], d_nm.rearrange("k c p n -> k (c p n)")).then_inc(nm_in, 16)
            with sp.Fori(0, TURNS - 1) as hp:
                known = None
                for i in range(PAIRS2):
                    if i % 4 == 3:
                        next_corner(HEADS + 2 * hp + i // 4)
                    known = pair_loads(in_second(hp)[0], i, True, known)
            for k in range(4):
                sp.wait_ge(y_used, 4 * k + 4)
                sp.wait_ge(fin_ready, k + 1)
                sp.dma_start(A["out"][4 * k * P:4 * (k + 1) * P].rearrange("(t p) d -> p t d", p=P), resid[:, 4 * k:4 * k + 4, :]).then_inc(s_out, 16)
            sp.wait_ge(s_out, 64)
            for k in range(2):
                sp.wait_ge(mx_in[k], 16 * (MT // 4 + 2))
                sp.wait_ge(mgu_in[k], 32 * (MT // 4 + 2 - k))
                sp.wait_ge(mdn_in[k], 32 * (MT // 4 + 1))

        @block.gpsimd
        def _(pool):
            pool.memset(zeros[:, :], 0.0).then_inc(zeros_ready, 1)
            pool.memset(xssm[:, :, 0:1, 0:WARM], 0.0).then_inc(read_f, 1)
            pool.memset(xssm[:, :, SEGS // 2:SEGS // 2 + 1, 0:WARM], 0.0).then_inc(read_b, 1)
            pool.memset(xssm[:, :, SEGS // 2 - 1:SEGS // 2, WARM + SEG:PADSEG], 0.0)
            pool.memset(xssm[:, :, SEGS - 1:SEGS, WARM + SEG:PADSEG], 0.0).then_inc(pads, 1)
            for h in range(HALVES):
                pool.wait_ge(proj_evac, CHUNKS * (h + 1))
                for b in range(BATCH):
                    s0, s1 = b * SEGS // 2, (b + 1) * SEGS // 2
                    pool.tensor_copy(xssm[:, h, s0 + 1:s1, 0:WARM], xssm[:, h, s0:s1 - 1, SEG:SEG + WARM]).then_inc(halo, 1)
                    pool.tensor_copy(xssm[:, h, s0:s1 - 1, WARM + SEG:PADSEG], xssm[:, h, s0 + 1:s1, WARM:2 * WARM]).then_inc(halo, 1)
            pool.wait_ge(halo, 8)
            pool.wait_ge(pads, 1)
            pool.wait_ge(s_const, 96)

            def window_inputs(w, buf, h):
                base = SEG + 2 * WARM - WIN - WIN * w
                for m in range(WIN):
                    x_in = xssm[:, h, :, bass.ds(base + m, 1)].rearrange("p s a -> p a s").broadcast_to([P, STATES, SEGS])
                    b_in = ABC[:, 1, h * STATES:(h + 1) * STATES].unsqueeze(2).broadcast_to([P, STATES, SEGS])
                    out = buf[:, m, h * STATES * SEGS:(h + 1) * STATES * SEGS].rearrange("p (d s) -> p d s", d=STATES)
                    last = pool.tensor_tensor(out, x_in, b_in, ALU.mult)
                last.then_inc(ub_ready, 1)

            def gate_mul(n):
                pool.wait_ge(gu_evac, n + 1)
                pool.tensor_tensor(act[:, :, :], silu_g[:, :, :], up[:, :, :], ALU.mult).then_inc(act_ready, 1)

            pool.wait_ge(proj_psum, 4 * CHUNKS)

            def early_window(w):
                if w >= 2:
                    pool.wait_ge(b_step, 2 * WIN * (w - 1) + 1)
                for h in range(HALVES):
                    window_inputs(w, scan_b[w % 2], h)

            def early_mul(c):
                if c:
                    pool.wait_ge(dn_psum, c)
                gate_mul(c)

            early_window(0)
            early_mul(0)
            early_window(1)
            early_mul(1)
            early_window(2)
            early_mul(2)
            early_window(3)
            early_mul(3)
            with pool.Fori(0, E0) as e:
                for i in range(2):
                    pool.wait_ge(b_step, 2 * WIN * (2 * e + 3 + i) + 1)
                    pool.wait_ge(read_b, 2 * e + i + 1)
                    for h in range(HALVES):
                        window_inputs(2 * e + 4 + i, scan_b[i], h)
                    for c in (2 * i, 2 * i + 1):
                        pool.wait_ge(dn_psum, CHUNKS * (e + 1) + c)
                        gate_mul(CHUNKS * (e + 1) + c)

            pool.tensor_copy(identb[:, :], ident[:, :]).then_inc(corner_idb, 1)
            pool.memset(V[:, :, :, HD:HD + 1], 1.0).then_inc(v_ones, 1)
            pool.memset(zero, 0.0).then_inc(v_ones, 1)
            for k in range(2):
                pool.memset(small[:, 24 + k:25 + k], 0.0).then_inc(my_out[k], 16)
            pool.wait_ge(v_ones, 2)
            pool.wait_ge(xn1_ready, 1)
            pool.wait_ge(l1_p, 32)
            pool.tensor_tensor(resid[:, :, :], resid[:, :, :], bp_t.unsqueeze(1).broadcast_to([P, TILES, DIM]), ALU.add).then_inc(bp_added, 1)

            def rest(n, out, whole, part):
                pool.wait_ge(part_ready, n)
                pool.tensor_tensor(out, whole, part, ALU.subtract).then_inc(rest_step, 1)

            def shared_mul(c):
                pool.wait_ge(sgu_evac, c + 1)
                if c:
                    pool.wait_ge(sdn_psum, c)
                pool.tensor_tensor(act[0:I1, :, :], silu_g[0:I1, :, :], up[0:I1, :, :], ALU.mult).then_inc(sact_ready, 1)

            rest(1, qf, qf, parts[0])
            rest(2, kf, kf, parts[3])
            shared_mul(0)
            rest(3, parts[2], qf, parts[1])
            shared_mul(1)
            rest(4, parts[5], kf, parts[4])
            shared_mul(2)
            pool.wait_ge(v_copied, 4)
            pool.wait_ge(l1_w, 160)
            pool.tensor_tensor(V[:, :, :, 0:HD], V[:, :, :, 0:HD],
                               bv_t.rearrange("p (h d) -> p h d", h=HEADS).unsqueeze(1).broadcast_to([P, TILES, HEADS, HD]), ALU.add).then_inc(v_ready, 1)
            shared_mul(3)

            def split_step(n, buf, step):
                f, p = corner_f[:, 0:CORNER], corner_p[:, buf]

                def wide(a):
                    return a.broadcast_to([P, CORNER])

                if step == 0:
                    pool.wait_ge(corner_in, 16 * (n + 1))
                else:
                    pool.wait_ge(corner_step, 6 * n + step)
                out, a, b, op = [(f, f, wide(corner_f[:, CORNER:]), ALU.subtract),
                                 (f, f, wide(inv), ALU.mult),
                                 (p[:, 0, :], f, wide(zero), ALU.add),
                                 (f, f, p[:, 0, :], ALU.subtract),
                                 (p[:, 1, :], f, wide(zero), ALU.add),
                                 (p[:, 2, :], f, p[:, 1, :], ALU.subtract)][step]
                pool.tensor_tensor(out, a, b, op).then_inc(corner_step, 1)

            def split_corner(n, buf):
                for step in range(6):
                    split_step(n, buf, step)

            pool.wait_ge(inv_ready, 1)
            split_corner(0, 0)
            pool.wait_ge(xs_zero, 16 * (SLOTS // 4))
            pool.wait_ge(slots_ready, 1)
            rows = [(t, k) for t in range(TILES) for k in range(TOPK)]

            def dispatch(count):
                for _ in range(min(count, len(rows))):
                    t, k = rows.pop(0)
                    pool.indirect_dma_start(d_xs, bass.IndirectOffsetOnAxis(ap=slots[:, t, k:k + 1], axis=0),
                                            xn1[:, t, :], None).then_inc(scattered, 16)

            dispatch(40)
            for n in range(2 * FREE_TURNS):
                pool.wait_ge(sq_psum, 16 * n + 1)
                split_corner(n + 1, (n + 1) % 2)
                dispatch(11)
            assert not rows

            def silu_mul(j, k2):
                pool.wait_ge(mth_ready, j + 1)
                pool.tensor_tensor(m_h[0:I1, k2, :], m_th[0:I1, k2, :], m_u[0:I1, k2, :], ALU.mult).then_inc(ma_ready, 1)

            silu_mul(0, 0)
            with pool.Fori(0, TURNS - FREE_TURNS) as it:
                for i in range(PAIRS1):
                    if i % 5 == 0:
                        n = 2 * it + 2 * FREE_TURNS + i // 5
                        pool.wait_ge(sq_psum, 16 * n + 1)
                    silu_mul(in_first(it)[0] + i + 1, (i + 1) % 2)
                    for step in ((0, 1), (2,), (3,), (4,), (5,))[i % 5]:
                        split_step(n + 1, 1 - i // 5, step)

            def head_v(n, buf, step):
                v_n = V[:, :, bass.ds(n, 1), :].rearrange("p t a d -> p t (a d)")
                parts = [Vh[buf][:, :, k * (HD + 1):(k + 1) * (HD + 1)] for k in range(3)]
                nil = zero.unsqueeze(2).broadcast_to([P, TILES, HD + 1])
                if step >= 2:
                    pool.wait_ge(v_step, 5 * n + step)
                out, a, b, op = [(parts[0], v_n, nil, ALU.add),
                                 (v_rest, v_n, nil, ALU.add),
                                 (v_rest, v_rest, parts[0], ALU.subtract),
                                 (parts[1], v_rest, nil, ALU.add),
                                 (parts[2], v_rest, parts[1], ALU.subtract)][step]
                pool.tensor_tensor(out, a, b, op).then_inc(v_step, 1)

            def low_parts(hp, final):
                for k in range(4):
                    for g in range(8):
                        G = 32 * hp + 8 * k + g
                        s = 8 * k + g
                        if g == 4 and k % 2 == 0:
                            pool.wait_ge(pv_done, G - 2)
                        if not final or s < LATE:
                            pool.wait_ge(hi1_ready, G + 1)
                            pool.tensor_tensor(*(cols(a, LO_SPLIT, 1024) for a in (p_lo[g % 2], Pt[g % 2], p_hi[g % 2])), ALU.subtract).then_inc(lo1_ready, 1)
                        r = 8 * (k % 2) + g
                        if r % 2 == 1 and r < 12 and not (final and k >= 2):
                            split_step(HEADS + 2 * hp + 1 + k // 2, 1 - k // 2, r // 2)
                        if final and s == LATE:
                            experts_through()
                        if final and s >= LATE:
                            gather()
                        if r in (4, 6, 8, 10, 12) and not (final and k >= 2):
                            head_v(2 * hp + 1 + k // 2, 1 - k // 2, (r - 4) // 2)

            pool.wait_ge(v_ready, 1)
            pool.wait_ge(nmT_psum, 1)
            for step in range(5):
                head_v(0, 0, step)
            with pool.Fori(0, TURNS - 1) as hp:
                low_parts(hp, False)
            returns = [(t, k) for t in range(TILES) for k in range(TOPK)]

            def gather():
                t, k = returns.pop(0)
                if t >= 2 and k == 0:
                    pool.wait_ge(y_used, t - 1)
                pool.indirect_dma_start(ybuf[t % 2][k], None, d_ys, bass.IndirectOffsetOnAxis(ap=slots[:, t, k:k + 1], axis=0)).then_inc(y_in[t % 2], 16)

            def experts_through():
                for b in range(2):
                    pool.wait_ge(my_out[b], 16 * (MT // 4 + 1))
                    pool.wait_ge(mx_in[b], 16 * (MT // 4 + 2))
                    pool.wait_ge(mgu_in[b], 32 * (MT // 4 + 2 - b))
                    pool.wait_ge(mdn_in[b], 32 * (MT // 4 + 1))
                pool.wait_ge(my_ready, MT // 2 + 2)

            low_parts(TURNS - 1, True)
            while returns:
                gather()

        @block.scalar
        def _(sc):
            for k in range(2):
                sc.wait_ge(var_ready, k + 1)
                sc.activation(stat[:, 2, :], stat[:, 1, :], ACT.Sqrt).then_inc(std_ready, 1)
            for g in range(TILES // TB):
                sc.wait_ge(xnT_psum, g + 1)
                sc.activation(xnT[:, g * 512:(g + 1) * 512], bank[g % 2][:, :], ACT.Copy).then_inc(xnT_ready, 1)
            sc.wait_ge(logit_psum, 1)
            sc.activation(logit[:, :, :], bank[7][:, 0:TILES * E0], ACT.Copy).then_inc(logit_ready, 1)
            sc.wait_ge(s_const, 96)
            for g in range(TILES // TB):
                sc.wait_ge(xaT_psum, g + 1)
                sc.activation(xaT[:, g * 512:(g + 1) * 512], bank[2 + g % 2][:, :], ACT.Identity,
                              scale=lnwb[:, 0:1], bias=lnwb[:, 1:2]).then_inc(xaT_ready, 1)
            sc.wait_ge(pads, 1)
            for k in range(HALVES * CHUNKS):
                h, c = k // CHUNKS, k % CHUNKS
                sc.wait_ge(proj_psum, k + 1)
                sc.activation(xssm[:, h, CT * c:CT * c + CT, WARM:WARM + SEG],
                              bank[4 + k % 2][:, :], ACT.Copy).then_inc(proj_evac, 1)
            sc.activation(ABC[:, 0, :], ABC[:, 0, :], ACT.Exp).then_inc(a_exp, 1)
            sc.wait_ge(logit_max, 1)
            sc.activation(score[:, :], top[:, :, 0:1], ACT.Sigmoid).then_inc(score_ready, 1)
            for g in range(TILES // TB):
                sc.wait_ge(xsT_psum, g + 1)
                sc.activation(xsT[:, g * 512:(g + 1) * 512], bank[g % 2][:, :], ACT.Copy).then_inc(xsT_ready, 1)
            for k in range(HALVES * CHUNKS, 2 * HALVES * CHUNKS):
                h, c = k // CHUNKS - HALVES, k % CHUNKS
                sc.wait_ge(proj_psum, k + 1)
                sc.activation(sgate[:, h, c * CHUNK:(c + 1) * CHUNK], bank[4 + k % 2][:, :], ACT.Silu).then_inc(proj_evac, 1)
            sc.wait_ge(halo, 8)
            sc.wait_ge(proj_psum, 4 * CHUNKS)

            def window_inputs(w, buf, h):
                for ch in range(h * STATES, (h + 1) * STATES):
                    x_in = xssm[:, h, :, bass.ds(WIN * w, WIN)].rearrange("p s m -> p m s")
                    last = sc.activation(buf[:, :, ch * SEGS:(ch + 1) * SEGS], x_in, ACT.Copy, scale=ABC[:, 1, ch:ch + 1])
                last.then_inc(uf_ready, 1)

            def evac_gu(n):
                for m in range(2):
                    sc.wait_ge(gu_psum, 2 * n + m + 1)
                    sc.activation(silu_g[:, m, :], bank[m][:, :], ACT.Silu)
                    last = sc.activation(up[:, m, :], bank[2 + m][:, :], ACT.Copy)
                last.then_inc(gu_evac, 1)

            def early_window(w):
                if w >= 2:
                    sc.wait_ge(f_step, 2 * WIN * (w - 1) + 1)
                for h in range(HALVES):
                    window_inputs(w, scan_f[w % 2], h)

            def early_evac(c):
                if c:
                    sc.wait_ge(act_ready, c)
                evac_gu(c)

            early_window(0)
            early_evac(0)
            early_window(1)
            early_evac(1)
            early_window(2)
            early_evac(2)
            early_window(3)
            early_evac(3)
            with sc.Fori(0, E0) as e:
                for c in range(CHUNKS):
                    i, n = c // 2, CHUNKS * (e + 1) + c
                    if c % 2 == 0:
                        sc.wait_ge(f_step, 2 * WIN * (2 * e + 3 + i) + 1)
                        sc.wait_ge(read_f, 2 * e + i + 1)
                    window_inputs(2 * e + 4 + i, scan_f[i], c % 2)
                    sc.wait_ge(act_ready, n)
                    evac_gu(n)

            sc.wait_ge(var_ready, 3)
            sc.activation(stat[:, 2, :], stat[:, 1, :], ACT.Sqrt).then_inc(std_ready, 1)
            for g in range(TILES // TB):
                sc.wait_ge(xn1T_psum, g + 1)
                sc.activation(xn1T[:, g * 512:(g + 1) * 512], bank[g % 2], ACT.Copy).then_inc(xn1T_ready, 1)
            for k in range(2):
                sc.wait_ge(lg1_psum, k + 1)
                sc.activation(sc1[:, 8 * k:8 * k + 8, :], bank[6 + k].rearrange("p (t e) -> p t e", e=E1), ACT.Sigmoid).then_inc(sc1_ready, 1)
            sc.wait_ge(inv_ready, 1)
            for k in range(2 * CHUNKS):
                sc.wait_ge(qk_psum, k + 1)
                c = k % CHUNKS
                out = (qf if k < CHUNKS else kf)[:, c * CHUNK:(c + 1) * CHUNK]
                if k < CHUNKS:
                    sc.activation(out, bank[2 + k % 2], ACT.Identity, scale=inv, bias=bqi).then_inc(qk_ready, 1)
                else:
                    sc.activation(out, bank[2 + k % 2], ACT.Identity, bias=bk).then_inc(qk_ready, 1)
            for g in range(TILES // TB):
                sc.wait_ge(v_psum, g + 1)
                sc.activation(V[:, TB * g:TB * g + TB, :, 0:HD], bank[4 + g % 2].rearrange("p (t h d) -> p t h d", t=TB, h=HEADS), ACT.Copy).then_inc(v_copied, 1)
            sc.wait_ge(qk_ready, 2 * CHUNKS)
            sc.activation(parts[0], qf, ACT.Copy).then_inc(part_ready, 1)
            sc.activation(parts[3], kf, ACT.Copy).then_inc(part_ready, 1)
            for c in range(CHUNKS):
                if c:
                    sc.wait_ge(sact_ready, c)
                for m in range(2):
                    sc.wait_ge(sgu_psum, 2 * c + m + 1)
                    sc.activation(silu_g[0:I1, m, :], bank[m][0:I1, :], ACT.Silu)
                    last = sc.activation(up[0:I1, m, :], bank[2 + m][0:I1, :], ACT.Copy)
                last.then_inc(sgu_evac, 1)
                if c < 2:
                    sc.wait_ge(rest_step, c + 1)
                    sc.activation(parts[1 + 3 * c], (qf, kf)[c], ACT.Copy).then_inc(part_ready, 1)

            def x_copy(j, k2):
                sc.wait_ge(mxT_psum, j + 1)
                sc.activation(m_xT[k2], bank[7][:, 0:PW], ACT.Copy).then_inc(mxT_ready, 1)

            def silu_up(j, k2):
                sc.wait_ge(mgu_psum, j + 1)
                sc.activation(m_th[0:I1, k2, :], bank[6][0:I1, 0:PW], ACT.Silu)
                sc.activation(m_u[0:I1, k2, :], bank[6][0:I1, PW:2 * PW], ACT.Copy, scale=2.0).then_inc(mth_ready, 1)

            sc.wait_ge(stacked[1], 16 * 16)
            x_copy(0, 0)
            x_copy(1, 1)
            silu_up(0, 0)
            with sc.Fori(0, TURNS - FREE_TURNS) as it:
                for i in range(PAIRS1):
                    j0, h0 = in_first(it)
                    j = j0 + i
                    x_copy(j + 2, i % 2)
                    sc.dma_start(m_x[:, i % 2, :, :], d_xs[bass.ds((j + 4) * PW, PW)].rearrange("(a p) d -> p a d", a=2)).then_inc(mx_in[i % 2], 16)
                    silu_up(j + 1, (i + 1) % 2)
                    sc.wait_ge(my_psum, j + 1)
                    sc.wait_ge(my_out[i % 2], 16 * (h0 + i // 2 + 1))
                    sc.activation(m_y[:, i % 2, :, :].rearrange("p a d -> p (a d)"), bank[7][:, PW:2 * PW], ACT.Copy).then_inc(my_ready, 1)
                    sc.wait_ge(my_ready, j + 2)
                    sc.dma_start(d_ys[bass.ds(j * PW, PW)].rearrange("(a p) d -> p a d", a=2), m_y[:, i % 2, :, :]).then_inc(my_out[i % 2], 16)

            sc.activation(stat[:, 0, :], stat[:, 1, :], ACT.Copy).then_inc(pv_done, 2)

            def exponentials(hp, pairs):
                for k in range(4):
                    for g in range(8):
                        G = 32 * hp + 8 * k + g
                        sc.wait_ge(st_psum, G + 1)
                        sc.wait_ge(lo0_ready, G + 1)
                        if not last_turn(hp) or 8 * k + g < LATE + 2:
                            sc.wait_ge(lo1_ready, G + 1)
                        sc.activation(Pt[g % 2][:, :, :], psum[:, 1024 * (g % 2):1024 * (g % 2) + 1024].rearrange("p (a n) -> p a n", a=2),
                                      ACT.Exp).then_inc(p_ready, 1)
                        sc.wait_ge(p_ready, G + 1)
                        sc.wait_ge(pv_done, G + 1)
                        sc.activation(p_hi[g % 2][:, 0, :], Pt[g % 2][:, 0, :], ACT.Copy).then_inc(hi0_ready, 1)
                        i = 2 * k + g // 4
                        if g % 4 == 3 and i < pairs:
                            sc.wait_ge(mgu_psum, in_second(hp)[0] + i + 2)
                            sc.activation(m_th[0:I1, (i + 1) % 2, :], bank[6][0:I1, 0:PW], ACT.Tanh, scale=0.5).then_inc(mth_ready, 1)

            with sc.Fori(0, TURNS - 1) as hp:
                exponentials(hp, PAIRS2)
            exponentials(TURNS - 1, 1)
            for g in range(TILES // TB):
                sc.wait_ge(attT_psum, g + 1)
                sc.activation(attT[:, g * 512:(g + 1) * 512], bank[g % 2], ACT.Copy).then_inc(attT_ready, 1)

        @block.tensor
        def _(pe):
            pe.wait_ge(s_const, 96)
            pe.wait_ge(xn_ready, 1)
            for g in range(TILES // TB):
                if g >= 2:
                    pe.wait_ge(xnT_ready, g - 1)
                for i in range(TB):
                    last = pe.transpose(bank[g % 2][:, i * P:(i + 1) * P], xn[:, g * TB + i, :], ident[:, :])
                last.then_inc(xnT_psum, 1)
            pe.wait_ge(xnT_ready, 4)
            for t in range(TILES):
                last = pe.matmul(bank[7][:, t * E0:(t + 1) * E0], xnT[:, t * P:(t + 1) * P], w_gate0[:, :], start=True, stop=True)
            last.then_inc(logit_psum, 1)
            pe.wait_ge(xa_ready, 1)
            for g in range(TILES // TB):
                if g >= 2:
                    pe.wait_ge(xaT_ready, g - 1)
                for i in range(TB):
                    last = pe.transpose(bank[2 + g % 2][:, i * P:(i + 1) * P], xa[:, g * TB + i, :], ident[:, :])
                last.then_inc(xaT_psum, 1)
            pe.wait_ge(s_w, 32)
            for k in range(2 * HALVES * CHUNKS):
                if k == HALVES * CHUNKS:
                    pe.wait_ge(xs_ready, 1)
                    for g in range(TILES // TB):
                        if g >= 2:
                            pe.wait_ge(xsT_ready, g - 1)
                        for i in range(TB):
                            last = pe.transpose(bank[g % 2][:, i * P:(i + 1) * P], xs[:, g * TB + i, :], ident[:, :])
                        last.then_inc(xsT_psum, 1)
                m, c = k // CHUNKS, k % CHUNKS
                pe.wait_ge(xaT_ready, min(c + 1, 4))
                if k >= 2:
                    pe.wait_ge(proj_evac, k - 1)
                pe.matmul(bank[4 + k % 2][:, :], w_in[:, m * P:(m + 1) * P], xaT[:, c * CHUNK:(c + 1) * CHUNK],
                          start=True, stop=True).then_inc(proj_psum, 1)

            def gate_up(src, c, n):
                pe.wait_ge(gu_evac, n) if not (isinstance(n, int) and n == 0) else None
                for m in range(2):
                    pe.matmul(bank[m][:, :], w_gu[:, m * P:(m + 1) * P], src[:, c * CHUNK:(c + 1) * CHUNK], start=True, stop=True)
                    pe.matmul(bank[2 + m][:, :], w_gu[:, I0 + m * P:I0 + (m + 1) * P], src[:, c * CHUNK:(c + 1) * CHUNK],
                              start=True, stop=True).then_inc(gu_psum, 1)

            def down(n):
                pe.wait_ge(act_ready, n + 1)
                if not (isinstance(n, int) and n == 0):
                    pe.wait_ge(dn_added, n)
                for q in range(CT):
                    for m in range(2):
                        last = pe.matmul(bank[4][:, q * P:(q + 1) * P], act[:, m, q * P:(q + 1) * P], w_dn[:, m, :],
                                         start=(m == 0), stop=(m == 1))
                last.then_inc(dn_psum, 1)

            def contract(w, i, d):
                step, scan = (f_step, scan_f) if d == 0 else (b_step, scan_b)
                pe.wait_ge(step, 2 * WIN * (w + 1))
                for h in range(HALVES):
                    for s in range(STATES):
                        ch = h * STATES + s
                        last = pe.matmul(bank[5 + i][:, (2 * d + h) * P:(2 * d + h + 1) * P], diagC[:, ch, :],
                                         scan[(3 + i) % 2][:, :, ch * SEGS:(ch + 1) * SEGS],
                                         start=(s == 0), stop=(s == STATES - 1))
                return last

            pe.wait_ge(wgu_in, 16)
            pe.wait_ge(wdn_in, 16)
            pe.wait_ge(xsT_ready, 4)
            for c in range(CHUNKS):
                gate_up(xnT, c, c)
                down(c)
            pe.wait_ge(scan_consts, 1)
            with pe.Fori(0, E0) as e:
                pe.wait_ge(wgu_in, 16 * e + 32)
                for c in range(CHUNKS):
                    gate_up(xsT, c, CHUNKS * (e + 1) + c)
                    i, d = c // 2, c % 2
                    if d == 0:
                        pe.wait_ge(y_added, 2 * e + 1)
                    contract(2 * e + 3 + i, i, 1 - d).then_inc((read_b, read_f)[d], 1)
                    if c == 0:
                        pe.wait_ge(wdn_in, 16 * e + 32)
                    down(CHUNKS * (e + 1) + c)
            pe.wait_ge(o_ready, 1)
            pe.wait_ge(gu_evac, CHUNKS * (E0 + 1))
            for g in range(TILES // TB):
                for q in range(TB):
                    t = g * TB + q
                    for h in range(HALVES):
                        last = pe.matmul(bank[g][:, q * P:(q + 1) * P], sgate[:, h, t * P:(t + 1) * P], w_out[:, h, :],
                                         start=(h == 0), stop=(h == 1))
                last.then_inc(out_psum, 1)

            def transposes(src, dst, done, free):
                for g in range(TILES // TB):
                    if g >= 2:
                        pe.wait_ge(free, g - 1)
                    for i in range(TB):
                        last = pe.transpose(bank[g % 2][:, i * P:(i + 1) * P], src[:, g * TB + i, :], ident[:, :])
                    last.then_inc(done, 1)

            pe.wait_ge(xn1_ready, 1)
            transposes(xn1, xn1T, xn1T_psum, xn1T_ready)
            pe.wait_ge(xn1T_ready, 4)
            pe.wait_ge(l1_w, 160)
            for t in range(TILES):
                last = pe.matmul(bank[6 + t // 8][:, (t % 8) * E1:(t % 8 + 1) * E1], xn1T[:, t * P:(t + 1) * P], w_gate1, start=True, stop=True)
                if t % 8 == 7:
                    last.then_inc(lg1_psum, 1)
            for k in range(2 * CHUNKS):
                if k >= 2:
                    pe.wait_ge(qk_ready, k - 1)
                c = k % CHUNKS
                pe.matmul(bank[2 + k % 2], w_q if k < CHUNKS else w_k, xn1T[:, c * CHUNK:(c + 1) * CHUNK], start=True, stop=True).then_inc(qk_psum, 1)
            for g in range(TILES // TB):
                if g >= 2:
                    pe.wait_ge(v_copied, g - 1)
                for q in range(TB):
                    t = g * TB + q
                    last = pe.matmul(bank[4 + g % 2][:, q * P:(q + 1) * P], xn1T[:, t * P:(t + 1) * P], w_v, start=True, stop=True)
                last.then_inc(v_psum, 1)
            pe.wait_ge(v_copied, 4)
            pe.wait_ge(sc1_ready, 2)
            pe.wait_ge(mask_ready, 1)
            for k in range(2):
                pe.matmul(bank[6 + k], strict, M[:, 8 * k:8 * k + 8, :], start=True, stop=True)
                last = pe.matmul(bank[4 + k], ones, M[:, 8 * k:8 * k + 8, :], start=True, stop=True)
            last.then_inc(rank_psum, 1)

            def shared_down(c):
                pe.wait_ge(sact_ready, c + 1)
                pe.wait_ge(rank_read, 1)
                for q in range(CT):
                    for m in range(2):
                        last = pe.matmul(bank[4 + c][:, q * P:(q + 1) * P], act[0:I1, m, q * P:(q + 1) * P], w_shd[0:I1, m, :],
                                         start=(m == 0), stop=(m == 1))
                last.then_inc(sdn_psum, 1)

            pe.wait_ge(qk_ready, 2 * CHUNKS)
            for c in range(CHUNKS):
                if c:
                    pe.wait_ge(sgu_evac, c)
                for m in range(2):
                    pe.matmul(bank[m][0:I1, :], w_sh[:, m * I1:(m + 1) * I1], xn1T[:, c * CHUNK:(c + 1) * CHUNK], start=True, stop=True)
                    pe.matmul(bank[2 + m][0:I1, :], w_sh[:, (2 + m) * I1:(3 + m) * I1], xn1T[:, c * CHUNK:(c + 1) * CHUNK],
                              start=True, stop=True).then_inc(sgu_psum, 1)
                if c:
                    shared_down(c - 1)
            shared_down(CHUNKS - 1)
            pe.wait_ge(exp_ready, 1)
            for c in range(2):
                last = pe.matmul(bank[0][0:1, c * P:(c + 1) * P], exp_of[:, c:c + 1], ident[:, :], start=True, stop=True)
            last.then_inc(etab_psum, 1)

            pe.wait_ge(stacked[0], 16 * 16)
            pe.wait_ge(corner_idb, 1)
            pe.wait_ge(etab_ready, 1)
            pe.wait_ge(slots_ready, 1)

            def x_transpose(buf, loads):
                pe.wait_ge(mx_in[buf], 16 * loads)
                for a in range(2):
                    last = pe.transpose(bank[7][:, a * P:(a + 1) * P], m_x[:, buf, a, :], ident[:, :])
                last.then_inc(mxT_psum, 1)

            def pair_gate_up(buf, loads):
                pe.wait_ge(mgu_in[buf], 32 * loads)
                for m in range(2):
                    for a in range(2):
                        last = pe.matmul(bank[6][0:I1, m * PW + a * P:m * PW + (a + 1) * P], m_gu[:, buf, a, m * I1:(m + 1) * I1],
                                         m_xT[buf][:, a * P:(a + 1) * P], start=True, stop=True)
                last.then_inc(mgu_psum, 1)

            def pair_x(it, i):
                pe.wait_ge(my_ready, it[0] + i + 1)
                x_transpose(i % 2, it[1] + (i + 2) // 2 + 1)

            def pair_gu(it, i):
                pe.wait_ge(mxT_ready, it[0] + i + 2)
                pe.wait_ge(ma_ready, it[0] + i + 1)
                pair_gate_up((i + 1) % 2, it[1] + (i + 1) // 2 + 1)

            def pair_down(it, i):
                pe.wait_ge(mdn_in[i % 2], 32 * (it[1] + i // 2 + 1))
                pe.wait_ge(mxT_ready, it[0] + i + 3)
                for a in range(2):
                    last = pe.matmul(bank[7][:, PW + a * P:PW + (a + 1) * P], m_h[0:I1, i % 2, a * P:(a + 1) * P], m_dn[0:I1, i % 2, a, :],
                                     start=True, stop=True)
                last.then_inc(my_psum, 1)

            def largest(hp, it):
                for k in range(4):
                    u = 4 * hp + k
                    for q in range(QT):
                        r = 8 * k + q
                        pair = bank[2 * (r % 3):2 * (r % 3) + 2]
                        pe.wait_ge(pair_free, 32 * hp + (r - 3 if r >= 3 else (-2, -1, -3)[r]) + 4)
                        queries = Qs[0:KROWS, bass.ds(u * LEN + q * P, P)]
                        for a in range(2):
                            biased = a == 1 and q < 2
                            last = pe.matmul(pair[a], queries, Ks[0:KROWS, bass.ds(u * LEN + a * 512, 512)], start=True, stop=not biased)
                            if biased:
                                if k % 2 == 0 and q == 0:
                                    pe.wait_ge(corner_step, 6 * (2 * hp + k // 2 + 1))
                                off, w = STRIPS[q]
                                for p in range(3):
                                    last = pe.matmul(pair[1][:, 512 - w:], identb[:, :], corner_p[:, k // 2, p, off:off + w],
                                                     start=False, stop=(p == 2))
                        last.then_inc(sq_psum, 1)
                        if it is not None and r < 3 * PAIRS1:
                            (pair_x, pair_gu, pair_down)[r % 3](it, r // 3)

            with pe.Fori(0, FREE_TURNS) as hp:
                largest(hp, None)
            pe.wait_ge(stacked[1], 16 * 16)
            x_transpose(0, 1)
            pe.wait_ge(mxT_ready, 1)
            x_transpose(1, 1)
            pair_gate_up(0, 1)
            pe.wait_ge(mxT_ready, 2)
            with pe.Fori(FREE_TURNS, TURNS) as hp:
                largest(hp, in_first(hp - FREE_TURNS))
            pe.wait_ge(pair_free, 3 + 8 * UNITS)
            for c in range(2):
                last = pe.transpose(bank[0][:, c * P:(c + 1) * P], nm[:, 16 * c:16 * c + 16, :].rearrange("p u q -> p (u q)"), ident[:, :])
            last.then_inc(nmT_psum, 1)

            def keys_scores(u, k, g):
                qh, kp = g // 4, g % 4
                for a in range(2):
                    kt = 2 * kp + a
                    out = bank[2 * (g % 2) + a]
                    biased = g == 3
                    last = pe.matmul(out, Ks[0:KROWS, bass.ds(u * LEN + kt * P, P)], Qs[0:KROWS, bass.ds(u * LEN + qh * 512, 512)],
                                     start=True, stop=not biased)
                    if biased:
                        off, w = STRIPS[1 - a]
                        for p in range(3):
                            last = pe.matmul(out[:, 0:w], identb[:, :], corner_p[:, k // 2, p, off:off + w],
                                             start=False, stop=(p == 2))
                last.then_inc(st_psum, 1)

            def with_v(hp, k, g):
                G = 32 * hp + 8 * k + g
                for a in range(2):
                    kt = 2 * (g % 4) + a
                    alone = last_turn(hp) and 8 * k + g >= LATE
                    pe.wait_ge(lo1_ready if a and not alone else lo0_ready, G + 3)
                    for half in (p_hi, p_lo):
                        last = pe.matmul(bank[4 + g // 4][0:VW, :], Vh[k // 2 % 2][:, (k % 2) * QT + kt, :], half[g % 2][:, a, :],
                                         start=(kt == 0 and half is p_hi), stop=(kt == QT - 1 and half is p_lo))
                last.then_inc(pv_done, 1)

            def products_back(out, qh):
                for q in range(4):
                    last = pe.transpose(out[:, q * P:(q + 1) * P], OT[:, (4 * qh + q) * P:(4 * qh + q + 1) * P], ident[:, :])
                last.then_inc(OT_psum, 1)

            def step(hp, it, s, final=False):
                G = 32 * hp + s
                k, g = s // 8, s % 8
                u, i = 4 * hp + k, s // 4
                pe.wait_ge(p_ready, G + 1)
                if s == 36:
                    pe.wait_ge(my_ready, it[0] + PAIRS2 + 2)
                    pe.wait_ge(acc_free, 8 * hp + 10)
                    products_back(bank[7], 1)
                if g == 1 and k % 2 == 0:
                    pe.wait_ge(corner_step, 6 * (HEADS + 2 * hp + k // 2 + 1))
                if not (final and s >= 30):
                    keys_scores(u if g < 6 else u + 1, k % 4, (g + 2) % 8)
                if s == 32:
                    pe.wait_ge(ma_ready, it[0] + PAIRS2 + 1)
                    pe.wait_ge(acc_free, 8 * hp + 9)
                    products_back(bank[6], 0)
                if s == LATE:
                    pe.wait_ge(OT_read, 2 * hp + 1)
                if s == 34:
                    pe.wait_ge(OT_read, 2 * hp + 2)
                if not final and g % 4 == 1:
                    pair_x(it, i)
                if g == 1 and k % 2 == 0:
                    pe.wait_ge(v_step, 5 * (2 * hp + k // 2 + 1))
                if g == 1 or g == 5:
                    pe.wait_ge(acc_free, 2 * u + g // 4 + 1)
                if s > 0:
                    with_v(hp, (s - 1) // 8, (s - 1) % 8)
                if not final and g % 4 == 2:
                    pair_gu(it, i)
                    pair_down(it, i)

            pe.wait_ge(nm_in, 16)
            pe.wait_ge(nmT_ready, 3)
            keys_scores(0, 0, 0)
            keys_scores(0, 0, 1)
            for s in range(LATE):
                step(0, in_second(0), s)
            with pe.Fori(0, TURNS - 1) as hp:
                for s in range(LATE, 32 + LATE):
                    step(hp, in_second(hp), s)
            for s in range(LATE, 32):
                step(TURNS - 1, None, s, final=True)
            with_v(TURNS - 1, 3, 7)
            pe.wait_ge(OT_read, 2 * TURNS - 1)
            pe.wait_ge(acc_free, 8 * TURNS + 1)
            products_back(bank[6], 0)
            pe.wait_ge(acc_free, 8 * TURNS + 2)
            products_back(bank[7], 1)
            pe.wait_ge(att_ready, 4 * TURNS + 1)
            transposes(att, attT, attT_psum, attT_ready)
            for g in range(TILES // TB):
                pe.wait_ge(attT_ready, g + 1)
                for q in range(TB):
                    t = g * TB + q
                    last = pe.matmul(bank[2 + g][:, q * P:(q + 1) * P], attT[:, t * P:(t + 1) * P], w_p[:, :], start=True, stop=True)
                last.then_inc(fin_psum, 1)

        @block.vector
        def _(dve):
            steps = [0]

            def link(ins):
                steps[0] += 1
                ins.then_inc(ln_step, 1)
                dve.wait_ge(ln_step, steps[0])

            norms = [0]
            sq_of = [sq]

            def bcast(v):
                return v.unsqueeze(2).broadcast_to([P, TILES, DIM])

            def norm(src, dst, done):
                link(dve.tensor_reduce(stat[:, 0, :], src, X, ALU.add))
                link(dve.tensor_scalar(stat[:, 0, :], stat[:, 0, :], 1.0 / DIM, None, ALU.mult))
                link(dve.tensor_tensor(dst, src, bcast(stat[:, 0, :]), ALU.subtract))
                link(dve.tensor_tensor(sq_of[0], dst, dst, ALU.mult))
                link(dve.tensor_reduce(stat[:, 1, :], sq_of[0], X, ALU.add))
                dve.tensor_scalar(stat[:, 1, :], stat[:, 1, :], 1.0 / DIM, EPS, ALU.mult, ALU.add).then_inc(var_ready, 1)
                norms[0] += 1
                dve.wait_ge(std_ready, norms[0])
                link(dve.reciprocal(stat[:, 3, :], stat[:, 2, :]))
                dve.tensor_tensor(dst, dst, bcast(stat[:, 3, :]), ALU.mult).then_inc(done, 1)

            dve.wait_ge(s_x, 64)
            norm(resid[:, :, :], xn, xn_ready)
            dve.wait_ge(xn_ready, 1)
            norm(xn, xa, xa_ready)
            dve.wait_ge(logit_ready, 1)
            for t in range(TILES):
                last = dve.max(top[:, t, :], logit[:, t, :])
            last.then_inc(logit_max, 1)
            dve.wait_ge(logit_max, 1)
            for t in range(TILES):
                last = dve.max_index(topi[:, t, :], top[:, t, :], logit[:, t, :])
            link(last)
            link(dve.tensor_copy(topf[:, :, :], topi[:, :, 0:1]))
            dve.wait_ge(s_const, 96)
            dve.tensor_tensor(onehot[:, :, :], iota8[:, :].unsqueeze(1).broadcast_to([P, TILES, 8]),
                              topf[:, :, :].broadcast_to([P, TILES, 8]), ALU.is_equal).then_inc(onehot_ready, 1)
            dve.wait_ge(score_ready, 1)
            dve.tensor_tensor(xs, xn, bcast(score[:, :]), ALU.mult).then_inc(xs_ready, 1)
            dve.wait_ge(a_exp, 1)
            link(dve.tensor_scalar(ABC[:, 0, :], ABC[:, 0, :], -10.0, -0.01, ALU.max, ALU.min))
            link(dve.tensor_reduce(decay[:, :], ABC[:, 0, :], X, ALU.max))
            link(dve.tensor_scalar(decay[:, :], decay[:, :], -1.0, None, ALU.mult))
            for ch in range(CH):
                last = dve.tensor_scalar(diagC[:, ch, :], ident[:, :], ABC[:, 2, ch:ch + 1], None, ALU.mult)
            last.then_inc(scan_consts, 1)
            dve.wait_ge(proj_psum, 4 * CHUNKS)
            dve.memset(y_flat, 0.0).then_inc(y_added, 1)
            dve.wait_ge(zeros_ready, 1)
            dve.wait_ge(y_added, 1)

            def window(w, p, first=False, extra=()):
                extra = dict(extra)
                dve.wait_ge(uf_ready, 2 * w + 2)
                dve.wait_ge(ub_ready, 2 * w + 2)
                for j in range(WIN):
                    prev_f = scan_f[p][:, j - 1, :] if j else scan_f[1 - p][:, WIN - 1, :]
                    prev_b = scan_b[p][:, WIN - j, :] if j else scan_b[1 - p][:, 0, :]
                    if first and j == 0:
                        prev_f = prev_b = zeros[:, :]
                    cur_f, cur_b = scan_f[p][:, j, :], scan_b[p][:, WIN - 1 - j, :]
                    for step, prev, cur in ((f_step, prev_f, cur_f), (b_step, prev_b, cur_b)):
                        if not (first and j == 0):
                            dve.wait_ge(step, 2 * WIN * w + 2 * j)
                        dve.scalar_tensor_tensor(cur, prev, decay[:, 0:1], cur, ALU.mult, ALU.add).then_inc(step, 1)
                    for step, cur in ((f_step, cur_f), (b_step, cur_b)):
                        dve.wait_ge(step, 2 * WIN * w + 2 * j + 1)
                        dve.tensor_scalar(cur, cur, -H_MAX, H_MAX, ALU.max, ALU.min).then_inc(step, 1)
                    if j in extra:
                        extra[j]()

            def add_down(n, c, weight):
                dve.wait_ge(dn_psum, n + 1)
                for q in range(CT):
                    t = c * CT + q
                    out = bank[4][:, q * P:(q + 1) * P]
                    if weight is None:
                        last = dve.tensor_tensor(resid[:, t, :], resid[:, t, :], out, ALU.add)
                    else:
                        last = dve.scalar_tensor_tensor(resid[:, t, :], out, onehot[:, t, weight], resid[:, t, :], ALU.mult, ALU.add)
                last.then_inc(dn_added, 1)

            def add_y(n, i):
                dve.wait_ge(read_b, n + 2)
                dve.wait_ge(read_f, n + 2)
                lo = WIN * n
                for d, base in ((0, lo), (1, SEG - WIN - lo)):
                    for h in range(HALVES):
                        dst = y[:, h, :].rearrange("p (s t) -> p s t", s=SEGS)[:, :, bass.ds(base, WIN)]
                        src = bank[5 + i][:, (2 * d + h) * P:(2 * d + h + 1) * P].rearrange("p (m s) -> p s m", m=WIN)
                        last = dve.tensor_tensor(dst, dst, src, ALU.add)
                last.then_inc(y_added, 1)

            window(0, 0, first=True, extra={7: lambda: add_down(0, 0, None)})
            window(1, 1, extra={5: lambda: add_down(1, 1, None)})
            window(2, 0, extra={4: lambda: add_down(2, 2, None)})
            window(3, 1, extra={WIN - 1: lambda: add_down(3, 3, None)})

            def behind(e, i):
                def down(c):
                    return lambda: add_down(CHUNKS * (e + 1) + c, c, bass.ds(e, 1))
                return {5: down(2 * i), WIN - 1: lambda: (add_y(2 * e + i, i), down(2 * i + 1)())}

            with dve.Fori(0, E0 - 1) as e:
                window(2 * e + 4, 0, extra=behind(e, 0))
                window(2 * e + 5, 1, extra=behind(e, 1))
            window(2 * E0 + 2, 0, extra=behind(E0 - 1, 0))
            for work in behind(E0 - 1, 1).values():
                work()
            dve.wait_ge(y_added, 2 * E0 + 1)
            dve.scalar_tensor_tensor(sgate[:, :, :], y[:, :, :], 0.5, sgate[:, :, :], ALU.mult, ALU.mult).then_inc(o_ready, 1)
            for g in range(TILES // TB):
                dve.wait_ge(out_psum, g + 1)
                dve.tensor_tensor(resid[:, g * TB:(g + 1) * TB, :], resid[:, g * TB:(g + 1) * TB, :], bank[g][:, :].rearrange("p (t d) -> p t d", t=TB), ALU.add).then_inc(x1_ready, 1)

            link(dve.tensor_scalar(inv, temp, 0.1, 10.0, ALU.max, ALU.min))
            link(dve.tensor_scalar(inv, inv, float(np.sqrt(np.float32(DIM))), None, ALU.mult))
            link(dve.reciprocal(inv, inv))
            dve.tensor_tensor(bqi, bq, inv, ALU.mult).then_inc(inv_ready, 1)
            sq_of[0] = sq1
            dve.wait_ge(uf_ready, 2 * (WINDOWS + 1))
            dve.wait_ge(ub_ready, 2 * (WINDOWS + 1))
            dve.wait_ge(x1_ready, 4)
            norm(resid[:, :, :], xn1, xn1_ready)
            dve.wait_ge(sc1_ready, 2)
            flat = lambda a: a.rearrange("p t e -> p (t e)")
            link(dve.tensor_tensor(sfc, sc1, gbias.unsqueeze(1).broadcast_to([P, TILES, E1]), ALU.add))
            G8 = TILES * GROUPS
            v8 = flat(sfc).rearrange("p (g k) -> p g k", k=8)

            def three(a, n):
                return a[:, 0:G8 * n].rearrange("p (g k) -> p g k", k=n)

            hi, lo = three(net[0], 4), three(net[1], 4)
            dve.tensor_tensor(hi, v8[:, :, 0:4], v8[:, :, 4:8], ALU.max)
            link(dve.tensor_tensor(lo, v8[:, :, 0:4], v8[:, :, 4:8], ALU.min))
            for n in (2, 1):
                mid, top_lo = three(net[2], n), net[2][:, G8 * n:2 * G8 * n].rearrange("p (g k) -> p g k", k=n)
                dve.tensor_tensor(mid, hi[:, :, 0:n], hi[:, :, n:2 * n], ALU.min)
                link(dve.tensor_tensor(top_lo, lo[:, :, 0:n], lo[:, :, n:2 * n], ALU.max))
                dve.tensor_tensor(hi[:, :, 0:n], hi[:, :, 0:n], hi[:, :, n:2 * n], ALU.max)
                link(dve.tensor_tensor(lo[:, :, 0:n], mid, top_lo, ALU.max))
            link(dve.tensor_tensor(gs[:, :, :].rearrange("p t g -> p (t g)").unsqueeze(2), hi[:, :, 0:1], lo[:, :, 0:1], ALU.add))
            for t in range(TILES):
                last = dve.max(gtop[:, t, :], gs[:, t, :])
            link(last)
            for t in range(TILES):
                last = dve.max_index(gidx[:, t, :], gtop[:, t, :], gs[:, t, :])
            link(last)
            link(dve.tensor_copy(gidxf[:, :, :], gidx[:, :, :]))
            pick = net[0][:, 0:G8 * TOPG].rearrange("p (t g k) -> p t g k", t=TILES, g=GROUPS)
            link(dve.tensor_tensor(pick, iota8[:, :].unsqueeze(1).unsqueeze(3).broadcast_to([P, TILES, GROUPS, TOPG]),
                                   gidxf[:, :, 0:TOPG].unsqueeze(2).broadcast_to([P, TILES, GROUPS, TOPG]), ALU.is_equal))
            link(dve.tensor_reduce(gmask, pick, X, ALU.add))
            link(dve.tensor_tensor(flat(masked).rearrange("p (g k) -> p g k", k=8), v8,
                                   gmask.rearrange("p t g -> p (t g)").unsqueeze(2).broadcast_to([P, G8, 8]), ALU.mult))
            link(dve.tensor_scalar(masked, masked, 0.0, None, ALU.add))
            for t in range(TILES):
                last = dve.max(etop[:, t, :], masked[:, t, :])
            link(last)
            for t in range(TILES):
                last = dve.match_replace(repl[:, t, :], etop[:, t, :], masked[:, t, :], -3.0e38)
            link(last)
            dve.tensor_tensor(M, masked, repl, ALU.not_equal).then_inc(mask_ready, 1)
            dve.wait_ge(mask_ready, 1)
            link(dve.memset(carry[:, 0, :], 0.0))
            dve.wait_ge(rank_psum, 1)
            total = [bank[4 + t // 8][:, (t % 8) * E1:(t % 8 + 1) * E1] for t in range(TILES)]
            for t in range(1, TILES):
                link(dve.tensor_tensor(carry[:, t, :], carry[:, t - 1, :], total[t - 1], ALU.add))
            link(dve.tensor_tensor(nt, carry[:, TILES - 1, :], total[TILES - 1], ALU.add))
            link(dve.tensor_scalar(ntu[:, :], nt, float(P - 1), None, ALU.add))
            link(dve.tensor_scalar(ntu[:, :], ntu[:, :], 7, None, ALU.logical_shift_right))
            link(dve.tensor_copy(nt, ntu[:, :]))
            link(dve.memset(ones64, 1.0))
            link(dve.tensor_tensor_scan(endt, ones64, nt, 0.0, ALU.mult, ALU.add))
            link(dve.tensor_tensor(base1, endt, nt, ALU.subtract))
            link(dve.tensor_scalar(base1, base1, float(P), None, ALU.mult))
            for k in range(2):
                last = dve.tensor_tensor(slot[:, 8 * k:8 * k + 8, :], carry[:, 8 * k:8 * k + 8, :], bank[6 + k].rearrange("p (t e) -> p t e", e=E1), ALU.add)
            last.then_inc(rank_read, 1)
            dve.wait_ge(rank_read, 1)
            link(dve.tensor_tensor(slot, slot, base1.unsqueeze(1).broadcast_to([P, TILES, E1]), ALU.add))
            link(dve.tensor_scalar(slot, slot, -1.0, KEY, ALU.mult, ALU.add))
            link(dve.tensor_tensor(key, slot, M, ALU.mult))
            for t in range(TILES):
                last = dve.max(etop[:, t, :], key[:, t, :])
            link(last)
            dve.tensor_scalar(slots[:, :, :], etop[:, :, :], -1.0, KEY, ALU.mult, ALU.add).then_inc(slots_ready, 1)
            dve.wait_ge(bp_added, 1)
            for c in range(CHUNKS):
                dve.wait_ge(sdn_psum, c + 1)
                dve.tensor_tensor(resid[:, CT * c:CT * c + CT, :], resid[:, CT * c:CT * c + CT, :],
                                  bank[4 + c].rearrange("p (t d) -> p t d", t=CT), ALU.add)
            for c in range(2):
                link(dve.tensor_scalar(cmp8[:, c, :], endt, jcol[:, c:c + 1], None, ALU.is_le))
                link(dve.tensor_reduce(exp_of[:, c:c + 1], cmp8[:, c, :], X, ALU.add))
            dve.tensor_scalar(exp_of[:, :], exp_of[:, :], float(E1 - 1), None, ALU.min).then_inc(exp_ready, 1)
            link(dve.tensor_tensor(rw, sc1, M, ALU.mult))
            link(dve.tensor_reduce(den1[:, :], rw, X, ALU.add))
            link(dve.tensor_scalar(den1[:, :], den1[:, :], 1e-20, None, ALU.add))
            link(dve.reciprocal(den1[:, :], den1[:, :]))
            link(dve.tensor_scalar(den1[:, :], den1[:, :], 2.5 * 0.5, None, ALU.mult))
            link(dve.tensor_tensor(rw, rw, den1[:, :].unsqueeze(2).broadcast_to([P, TILES, E1]), ALU.mult))
            def pick_weight(t, step, buf):
                eq, eq_rw = cmp8b[2 * buf:2 * buf + 2]
                if step == 0:
                    return dve.tensor_tensor(eq, key[:, t:t + 2, :].unsqueeze(2).broadcast_to([P, 2, 8, E1]),
                                             etop[:, t:t + 2, :].unsqueeze(3).broadcast_to([P, 2, 8, E1]), ALU.is_equal)
                if step == 1:
                    return dve.tensor_tensor(eq_rw, eq, rw[:, t:t + 2, :].unsqueeze(2).broadcast_to([P, 2, 8, E1]), ALU.mult)
                return dve.tensor_reduce(w8[:, t:t + 2, :], eq_rw, X, ALU.add)

            for t in range(0, TILES, 4):
                for step in range(3):
                    for buf in range(2):
                        last = pick_weight(t + 2 * buf, step, buf)
                    link(last)
            dve.wait_ge(etab_psum, 1)
            dve.tensor_copy(etab[:, :], bank[0][0:1, 0:2 * P]).then_inc(etab_ready, 1)
            dve.memset(rec[:, :, 0:1], 0.0).then_inc(w8_ready, 1)
            dve.memset(rec[:, :, 1:2], 0.0).then_inc(my_ready, 1)
            dve.memset(rec[:, 4:6, 2:3], 0.0).then_inc(OT_read, 1)
            dve.memset(rec[:, 0:2, 2:3], 0.0).then_inc(lo0_ready, 2)
            dve.memset(rec[:, 2:4, 2:3], 0.0).then_inc(lo1_ready, 2)
            dve.memset(rec[:, 6:8, 2:3], 0.0).then_inc(acc_free, 2)
            dve.memset(rec[:, :, 3:4], 0.0).then_inc(att_ready, 1)

            dve.memset(nmr, 0.0).then_inc(pair_free, 3)
            with dve.Fori(0, HEADS // 2) as hp:
                for k in range(4):
                    for q in range(QT):
                        n, r = 32 * hp + 8 * k + q, 8 * k + q
                        dve.wait_ge(sq_psum, n + 1)
                        dve.tensor_reduce(nm[:, bass.ds(4 * hp + k, 1), q:q + 1], psum[:, 1024 * (r % 3):1024 * (r % 3) + 1024].rearrange("p (a n) -> p a n", a=1),
                                          X, ALU.max, negate=True).then_inc(pair_free, 1)
            dve.wait_ge(nmT_psum, 1)
            nps = bank[0][:, 0:2 * P].rearrange("p (c n) -> p c n", c=2)
            link(dve.tensor_scalar(nmr, nps, P_SCALE, None, ALU.add))
            dve.tensor_copy(nmT[0][:, :, :], nmr).then_inc(nmT_ready, 1)
            dve.wait_ge(nmT_ready, 1)
            link(dve.tensor_tensor(nmr, nmr, nmT[0][:, :, :], ALU.subtract))
            dve.tensor_copy(nmT[1][:, :, :], nmr).then_inc(nmT_ready, 1)
            dve.wait_ge(nmT_ready, 2)
            dve.tensor_tensor(nmT[2][:, :, :], nmr, nmT[1][:, :, :], ALU.subtract).then_inc(nmT_ready, 1)

            def pair_x(it, i):
                dve.wait_ge(mxT_psum, it[0] + i + 3)
                dve.tensor_copy(m_xT[i % 2], bank[7][:, 0:PW]).then_inc(mxT_ready, 1)

            def pair_h(hp, it, i):
                k2 = (i + 1) % 2
                dve.wait_ge(mth_ready, it[0] + i + 2)
                dve.scalar_tensor_tensor(m_th[0:I1, k2, :], m_th[0:I1, k2, :], 1.0, bank[6][0:I1, 0:PW], ALU.add, ALU.mult).then_inc(ma_step, 1)
                dve.wait_ge(ma_step, PAIRS2 * hp + i + 1)
                dve.tensor_tensor(m_h[0:I1, k2, :], m_th[0:I1, k2, :], bank[6][0:I1, PW:2 * PW], ALU.mult).then_inc(ma_ready, 1)

            def pair_y(it, i):
                dve.wait_ge(my_psum, it[0] + i + 1)
                dve.wait_ge(my_out[i % 2], 16 * (it[1] + i // 2 + 1))
                dve.tensor_copy(m_y[:, i % 2, :, :].rearrange("p a d -> p (a d)"), bank[7][:, PW:2 * PW]).then_inc(my_ready, 1)

            def routed(t):
                dve.wait_ge(y_in[t % 2], 16 * TOPK * (t // 2 + 1))
                for k in range(TOPK):
                    last = dve.scalar_tensor_tensor(resid[:, t, :], ybuf[t % 2][k], w8[:, t, k:k + 1], resid[:, t, :], ALU.mult, ALU.add)
                    if k < TOPK - 1:
                        link(last)
                last.then_inc(y_used, 1)

            def out_of_bank(hp, k, qh):
                dve.wait_ge(pv_done, 32 * hp + 8 * k + 4 * qh + 6)
                dve.tensor_copy(OT[32 * k:32 * k + VW, qh * 512:(qh + 1) * 512], bank[4 + qh][0:VW, :]).then_inc(acc_free, 1)

            def divide(hp, qh):
                dve.wait_ge(OT_psum, 2 * hp + qh + 1)
                dve.wait_ge(att_ready, 4 * hp + 2 * qh + 1)
                dve.tensor_reduce(v_sum[qh][:, :, :, :], bank[6 + qh].rearrange("p (q k c) -> p q k c", q=4, k=4)[:, :, :, 0:VW]
                                  .rearrange("p q k (s d) -> p q k d s", s=3), X, ALU.add).then_inc(OT_read, 1)
                dve.wait_ge(OT_read, 2 * hp + qh + 2)
                dve.reciprocal(rec[:, 4 * qh:4 * qh + 4, :].unsqueeze(3), v_sum[qh][:, :, :, HD:HD + 1]).then_inc(rec_ready, 1)
                dve.wait_ge(rec_ready, 2 * hp + qh + 1)
                for n in range(2):
                    out = att[:, n * QT + 4 * qh:n * QT + 4 * qh + 4, bass.ds(2 * hp * HD, 2 * HD)].rearrange("p q (h d) -> p q h d", h=2)
                    dve.tensor_tensor(out, v_sum[qh][:, :, :, 0:HD].rearrange("p q (h n) d -> p q h n d", h=2)[:, :, :, n, :],
                                      rec[:, 4 * qh:4 * qh + 4, :].rearrange("p q (h n) -> p q h n", h=2)[:, :, :, n:n + 1].broadcast_to([P, 4, 2, HD]),
                                      ALU.mult).then_inc(att_ready, 1)

            def step(hp, it, s, final=False):
                G = 32 * hp + s
                k, g, i = s // 8, s % 8, s // 4
                dve.wait_ge(p_ready, G + 1)
                dve.wait_ge(pv_done, G + 1)
                dve.tensor_copy(p_hi[g % 2][:, 1, :], Pt[g % 2][:, 1, :]).then_inc(hi1_ready, 1)
                dve.wait_ge(hi0_ready, G + 1)
                dve.wait_ge(hi1_ready, G + 1)
                dve.tensor_tensor(*(cols(a, 0, 1024 if final else LO_SPLIT) for a in (p_lo[g % 2], Pt[g % 2], p_hi[g % 2])), ALU.subtract).then_inc(lo0_ready, 1)
                if g == 1 and k > 0:
                    out_of_bank(hp, k - 1, 1)
                if g == 5:
                    out_of_bank(hp, k, 0)
                if not final and g % 4 == 1:
                    pair_x(it, i)
                if not final and g % 4 == 3:
                    pair_y(it, i)
                    pair_h(hp, it, i)
                if s == 32 or s == 36:
                    divide(hp, (s - 32) // 4)
                if final and s >= 14 and s % 4 == 2:
                    routed((s - 14) // 4)

            dve.wait_ge(scattered, 16 * TILES * TOPK)
            dve.wait_ge(ma_ready, FIRST + 1)
            for s in range(LATE):
                step(0, in_second(0), s)
            with dve.Fori(0, TURNS - 1) as hp:
                for s in range(LATE, 32 + LATE):
                    step(hp, in_second(hp), s)
            for s in range(LATE, 32):
                step(TURNS - 1, None, s, final=True)
            out_of_bank(TURNS - 1, 3, 1)
            divide(TURNS - 1, 0)
            divide(TURNS - 1, 1)
            for g in range(TILES // TB):
                dve.wait_ge(fin_psum, g + 1)
                dve.tensor_tensor(resid[:, g * TB:(g + 1) * TB, :], resid[:, g * TB:(g + 1) * TB, :], bank[2 + g].rearrange("p (t d) -> p t d", t=TB), ALU.add).then_inc(fin_ready, 1)
            dve.wait_ge(fin_ready, TILES // TB)
            for t in range(5, TILES):
                routed(t)


def kernel(**inputs):
    import concourse.bacc as bacc
    from concourse.bass_utils import run_bass_kernel_spmd
    import ml_dtypes

    def t(a):
        return np.ascontiguousarray(a)

    i = {k: np.asarray(v) for k, v in inputs.items()}

    def halves(a):
        return a.reshape(HALVES, P, STATES).transpose(1, 0, 2).reshape(P, CH)

    gu = [np.concatenate([i["L0_ffn_sh_gate"], i["L0_ffn_sh_up"]], 1)] + \
         [np.concatenate([i["L0_ffn_rt_gate"][e], i["L0_ffn_rt_up"][e]], 1) for e in range(E0)]
    dn = [i["L0_ffn_sh_down"]] + [i["L0_ffn_rt_down"][e] for e in range(E0)]
    arrays = {
        "x": i["L0_attn_x"].reshape(TOK, DIM),
        "ident": np.eye(P, dtype=np.float32),
        "iota8": np.tile(np.arange(8, dtype=np.float32), (P, 1)),
        "lnwb": np.stack([i["L0_attn_ln_w"], i["L0_attn_ln_b"]], 1),
        "w_gate0": i["L0_ffn_gate_w"],
        "abc": np.stack([halves(i["L0_attn_A_log"]), halves(i["L0_attn_B_mat"]), halves(i["L0_attn_C_mat"])], 1),
        "w_in": i["L0_attn_in_proj_w"].T,
        "w_out": i["L0_attn_out_proj_w"].T.reshape(2, P, DIM).transpose(1, 0, 2),
        "w_gu0": np.stack(gu),
        "w_dn0": np.stack([d.reshape(2, P, DIM).transpose(1, 0, 2) for d in dn]),
    }
    table = i["L1_attn_bias_table"]
    rows = np.arange(P)
    near = np.arange(2 * P)
    q_major = np.clip(rows[:, None, None] + P * np.arange(2)[None, :, None] - (near + LEN - 2 * P)[None, None, :] + LEN - 1, 0, BIASED)
    k_major = np.clip(near[None, None, :] - (rows[:, None, None] + P * np.arange(2)[None, :, None] + LEN - 2 * P) + LEN - 1, 0, BIASED)

    def corners(strips):
        return table.T[:, np.concatenate(strips + [np.full((P, 1), BIASED)], 1)]

    arrays.update({
        "small": np.concatenate([i["L1_attn_bq"][:, None], i["L1_attn_bk"][:, None], np.tile(i["L1_attn_temperature"], (P, 1)),
                                 rows[:, None].astype(np.float32), rows[:, None].astype(np.float32) + P,
                                 np.tile(table[BIASED], (P, 1))], 1),
        "w_q": i["L1_attn_Wq"], "w_k": i["L1_attn_Wk"], "w_v": i["L1_attn_Wv"], "w_p": i["L1_attn_Wp"],
        "bv_t": np.tile(i["L1_attn_bv"], (P, 1)), "bp_t": np.tile(i["L1_attn_bp"], (P, 1)),
        "strict": np.triu(np.ones((P, P), np.float32), 1), "ones": np.ones((P, P), np.float32),
        "w_gate1": i["L1_ffn_gate_w"].T, "gbias": np.tile(i["L1_ffn_gate_bias"], (P, 1)),
        "w_sh": np.concatenate([i["L1_ffn_Sg"].T, i["L1_ffn_Su"].T], 1),
        "w_shd": i["L1_ffn_Sd"].T.reshape(2, I1, DIM).transpose(1, 0, 2),
        "w_gu1": np.concatenate([i["L1_ffn_Wg"].transpose(0, 2, 1), i["L1_ffn_Wu"].transpose(0, 2, 1)], 2),
        "w_dn1": i["L1_ffn_Wd"].transpose(0, 2, 1),
        "corners": np.concatenate([corners([q_major[:, 0], q_major[:, 1, P:]]), corners([k_major[:, 1], k_major[:, 0, 0:P]])]),
        "fill_q": np.zeros((16, UNITS * LEN), ml_dtypes.bfloat16),
        "fill_k": np.concatenate([np.ones((3, UNITS * LEN)), np.zeros((13, UNITS * LEN))]).astype(ml_dtypes.bfloat16),
    })
    arrays = {k: t(v) for k, v in arrays.items()}
    nc = bacc.Bacc("TRN2", target_bir_lowering=False, num_devices=1)
    A = {k: nc.dram_tensor("in_" + k, v.shape, mybir.dt.from_np(v.dtype), kind="ExternalInput").ap() for k, v in arrays.items()}
    A["out"] = nc.dram_tensor("out", (TOK, DIM), F32, kind="ExternalOutput").ap()
    build(nc, A)
    r = run_bass_kernel_spmd(nc, [{"in_" + k: v for k, v in arrays.items()}], core_ids=[0])
    return r.results[0]["out"].reshape(BATCH, LEN, DIM)
```
